# Optimizing a Trainium2 kernel written in Bass

```python
import numpy as np
import jax
import jax.numpy as jnp

def _softmax(x, axis=-1):
    return jax.nn.softmax(x, axis=axis)

def _gelu(x):
    return jax.nn.gelu(x, approximate=True)

def _silu(x):
    return jax.nn.silu(x)

def _sigmoid(x):
    return jax.nn.sigmoid(x)

def _layernorm(x, axis=-1, eps=1e-05):
    m = jnp.mean(x, axis=axis, keepdims=True)
    v = jnp.var(x, axis=axis, keepdims=True)
    return (x - m) / jnp.sqrt(v + eps)

def _scatter_add(tgt, idx, src, axis=0):
    return tgt.at[idx].add(src)

def _segment_sum(src, seg, n):
    return jax.ops.segment_sum(src, seg, n)
kernel_name = 'mk_hybrid_d2_jaxref_r8_f91500'

def setup_inputs(seed: int=0):
    np.random.seed(seed)
    _w = jnp.asarray

    def _L0_attn_a_setup():
        import jax, jax.numpy as jnp
        import numpy as np
        import math
        B, S, D = (2, 128, 128)
        H, M, W, RMOD, CR = (16, 16, 8, 8, 8)
        TOPK, ALPHA, MIX, STEP_A, TEMP = (8, 3.0, 0.15, 6.0, 1.0)

        def _topk_sparse(logits, k):
            soft = jax.nn.softmax(logits / max(TEMP, 1e-06), axis=-1)
            _, idx = jax.lax.top_k(soft, k)
            hard = jax.nn.one_hot(idx, logits.shape[-1], dtype=soft.dtype).sum(-2)
            hard = hard / (hard.sum(-1, keepdims=True) + 1e-08)
            return hard + jax.lax.stop_gradient(soft - hard)

        def _step(x):
            hard = (x > 0).astype(x.dtype)
            soft = jax.nn.sigmoid(STEP_A * x)
            return hard + jax.lax.stop_gradient(soft - hard)

        def _ln(x, g, b):
            mu = x.mean(-1, keepdims=True)
            var = x.var(-1, keepdims=True)
            return (x - mu) / jnp.sqrt(var + 1e-05) * g + b
        key = jax.random.key(seed)
        ks = jax.random.split(key, 24)

        def n(i, shape, s=0.02):
            return jax.random.normal(ks[i], shape, jnp.float32) * s
        return {'x': jax.random.normal(ks[0], (B, S, D), jnp.float32), 'v_w': n(1, (D, D)), 'v_b': jnp.zeros((D,), jnp.float32), 'out_w': n(2, (D, D)), 'out_b': jnp.zeros((D,), jnp.float32), 'qmod_w': n(3, (D, H)), 'qmod_b': jnp.zeros((H,), jnp.float32), 'kmod_w': n(4, (D, H)), 'kmod_b': jnp.zeros((H,), jnp.float32), 'gate_w': n(5, (D, H * M)), 'gate_b': jnp.zeros((H * M,), jnp.float32), 'mod_w': n(6, (D, H * RMOD)), 'mod_b': jnp.zeros((H * RMOD,), jnp.float32), 'mod_basis': n(7, (RMOD, H, M), 0.05), 'freqs': n(8, (H, M, W, 2), 1.5), 'amps': n(9, (H, M, W), 0.02) + 0.5, 'phases': n(10, (H, M, W), math.pi), 'cq_w': n(11, (D, H * CR)), 'ck_w': n(12, (D, H * CR)), 'ffn_w1': n(13, (D, 4 * D)), 'ffn_b1': jnp.zeros((4 * D,), jnp.float32), 'ffn_w2': n(14, (4 * D, D)), 'ffn_b2': jnp.zeros((D,), jnp.float32), 'ln1_g': jnp.ones((D,), jnp.float32), 'ln1_b': jnp.zeros((D,), jnp.float32), 'ln2_g': jnp.ones((D,), jnp.float32), 'ln2_b': jnp.zeros((D,), jnp.float32)}
    _L0_attn_a_in = _L0_attn_a_setup()

    def _L0_attn_b_setup():
        import jax, jax.numpy as jnp
        import numpy as np
        DIM = 128
        HEADS = 16
        DIM_HEAD = 64
        key = jax.random.key(seed)
        ks = jax.random.split(key, 6)
        inner = HEADS * DIM_HEAD
        s = lambda fan_in: 1.0 / np.sqrt(fan_in)
        return {'x': jax.random.normal(ks[0], (4, 512, DIM), dtype=jnp.float32), 'W_qkv': jax.random.normal(ks[1], (DIM, inner * 3), dtype=jnp.float32) * s(DIM), 'W_f': jax.random.normal(ks[2], (DIM_HEAD, DIM_HEAD), dtype=jnp.float32) * s(DIM_HEAD), 'b_f': jax.random.normal(ks[3], (DIM_HEAD,), dtype=jnp.float32) * 0.01, 'W_out': jax.random.normal(ks[4], (inner, DIM), dtype=jnp.float32) * s(inner), 'b_out': jax.random.normal(ks[5], (DIM,), dtype=jnp.float32) * 0.01}
    _L0_attn_b_in = _L0_attn_b_setup()

    def _L0_ffn_setup():
        import jax, jax.numpy as jnp
        import numpy as np
        E = 8
        K = 2
        D = 128
        H = 128
        B, T = (2, 128)
        key = jax.random.key(seed)
        ks = jax.random.split(key, 6)
        s = 0.02
        return {'x': jax.random.normal(ks[0], (B, T, D), dtype=jnp.float32), 'gate_w': jax.random.normal(ks[1], (E, D), dtype=jnp.float32) * s, 'lb_bias': jnp.zeros((E,), dtype=jnp.float32), 'w1': jax.random.normal(ks[2], (E, H, D), dtype=jnp.float32) * s, 'w2': jax.random.normal(ks[3], (E, D, H), dtype=jnp.float32) * s, 'cfc': jax.random.normal(ks[4], (H, D), dtype=jnp.float32) * s, 'cproj': jax.random.normal(ks[5], (D, H), dtype=jnp.float32) * s}
    _L0_ffn_in = _L0_ffn_setup()

    def _L1_attn_a_setup():
        import jax, jax.numpy as jnp
        import numpy as np
        D_MODEL, N_HEADS = (128, 16)
        D_H = D_MODEL // N_HEADS
        D_HR = D_H // 2
        D_LATENT = 32
        THETA = 10000.0

        def rope(x, theta=THETA):
            S, d = (x.shape[-2], x.shape[-1])
            inv = theta ** (-jnp.arange(0, d, 2, dtype=jnp.float32) / d)
            ang = jnp.arange(S, dtype=jnp.float32)[:, None] * inv
            cos, sin = (jnp.cos(ang), jnp.sin(ang))
            x1, x2 = (x[..., 0::2], x[..., 1::2])
            r1 = x1 * cos - x2 * sin
            r2 = x1 * sin + x2 * cos
            return jnp.stack([r1, r2], axis=-1).reshape(x.shape)
        key = jax.random.key(seed)
        ks = jax.random.split(key, 9)
        s = lambda fan_in: 1.0 / np.sqrt(fan_in)
        return {'x': jax.random.normal(ks[0], (4, 256, D_MODEL), jnp.float32), 'W_DQ': jax.random.normal(ks[1], (D_MODEL, D_LATENT), jnp.float32) * s(D_MODEL), 'W_UQ': jax.random.normal(ks[2], (D_LATENT, N_HEADS * D_H), jnp.float32) * s(D_LATENT), 'W_QR': jax.random.normal(ks[3], (D_LATENT, N_HEADS * D_HR), jnp.float32) * s(D_LATENT), 'W_DKV': jax.random.normal(ks[4], (D_MODEL, D_LATENT), jnp.float32) * s(D_MODEL), 'W_UK': jax.random.normal(ks[5], (D_LATENT, N_HEADS * D_H), jnp.float32) * s(D_LATENT), 'W_UV': jax.random.normal(ks[6], (D_LATENT, N_HEADS * D_H), jnp.float32) * s(D_LATENT), 'W_KR': jax.random.normal(ks[7], (D_MODEL, D_HR), jnp.float32) * s(D_MODEL), 'W_O': jax.random.normal(ks[8], (N_HEADS * D_H, D_MODEL), jnp.float32) * s(N_HEADS * D_H)}
    _L1_attn_a_in = _L1_attn_a_setup()

    def _L1_attn_b_setup():
        import jax, jax.numpy as jnp
        import numpy as np
        import math
        DIM = 128
        HEADS = 16
        DIM_HEAD = 64
        INNER = HEADS * DIM_HEAD
        NUM_BUCKETS = 32
        MAX_DISTANCE = 128

        def _relative_position_bucket(rel_pos, num_buckets=NUM_BUCKETS, max_distance=MAX_DISTANCE):
            n = jnp.maximum(-rel_pos, 0)
            max_exact = num_buckets // 2
            is_small = n < max_exact
            n_safe = jnp.maximum(n, 1)
            val_if_large = max_exact + (jnp.log(n_safe.astype(jnp.float32) / max_exact) / math.log(max_distance / max_exact) * (num_buckets - max_exact)).astype(jnp.int32)
            val_if_large = jnp.minimum(val_if_large, num_buckets - 1)
            return jnp.where(is_small, n, val_if_large)
        key = jax.random.key(seed)
        ks = jax.random.split(key, 6)
        x = jax.random.normal(ks[0], (2, 256, DIM), dtype=jnp.float32)
        Wq = jax.random.normal(ks[1], (DIM, INNER), dtype=jnp.float32) * DIM ** (-0.5)
        Wkv = jax.random.normal(ks[2], (DIM, 2 * DIM_HEAD), dtype=jnp.float32) * DIM ** (-0.5)
        Wout = jax.random.normal(ks[3], (INNER, DIM), dtype=jnp.float32) * INNER ** (-0.5)
        bout = jnp.zeros((DIM,), dtype=jnp.float32)
        rel_emb = jax.random.normal(ks[4], (NUM_BUCKETS, HEADS), dtype=jnp.float32) * 0.02
        return {'x': x, 'Wq': Wq, 'Wkv': Wkv, 'Wout': Wout, 'bout': bout, 'rel_emb': rel_emb}
    _L1_attn_b_in = _L1_attn_b_setup()

    def _L1_ffn_setup():
        import jax, jax.numpy as jnp
        import numpy as np
        TEMPERATURE = 0.5
        CAPACITY_FACTOR = 1.25
        TOP_K = 1
        key = jax.random.key(seed)
        ks = jax.random.split(key, 5)
        B, S, D, H, E = (4, 256, 128, 256, 8)
        s = 0.02
        return {'x': jax.random.normal(ks[0], (B, S, D), jnp.float32), 'gate_w': jax.random.normal(ks[1], (E, D), jnp.float32) * s, 'gate_b': jnp.zeros((E,), jnp.float32), 'rms_w': jnp.ones((E,), jnp.float32), 'w1': jax.random.normal(ks[2], (E, D, H), jnp.float32) * s, 'b1': jnp.zeros((E, H), jnp.float32), 'w2': jax.random.normal(ks[3], (E, H, D), jnp.float32) * s, 'b2': jnp.zeros((E, D), jnp.float32)}
    _L1_ffn_in = _L1_ffn_setup()
    _d = {'L0_attn_a_x': _L0_attn_a_in['x'], 'L0_attn_a_v_w': _L0_attn_a_in['v_w'], 'L0_attn_a_v_b': _L0_attn_a_in['v_b'], 'L0_attn_a_out_w': _L0_attn_a_in['out_w'], 'L0_attn_a_out_b': _L0_attn_a_in['out_b'], 'L0_attn_a_qmod_w': _L0_attn_a_in['qmod_w'], 'L0_attn_a_qmod_b': _L0_attn_a_in['qmod_b'], 'L0_attn_a_kmod_w': _L0_attn_a_in['kmod_w'], 'L0_attn_a_kmod_b': _L0_attn_a_in['kmod_b'], 'L0_attn_a_gate_w': _L0_attn_a_in['gate_w'], 'L0_attn_a_gate_b': _L0_attn_a_in['gate_b'], 'L0_attn_a_mod_w': _L0_attn_a_in['mod_w'], 'L0_attn_a_mod_b': _L0_attn_a_in['mod_b'], 'L0_attn_a_mod_basis': _L0_attn_a_in['mod_basis'], 'L0_attn_a_freqs': _L0_attn_a_in['freqs'], 'L0_attn_a_amps': _L0_attn_a_in['amps'], 'L0_attn_a_phases': _L0_attn_a_in['phases'], 'L0_attn_a_cq_w': _L0_attn_a_in['cq_w'], 'L0_attn_a_ck_w': _L0_attn_a_in['ck_w'], 'L0_attn_a_ffn_w1': _L0_attn_a_in['ffn_w1'], 'L0_attn_a_ffn_b1': _L0_attn_a_in['ffn_b1'], 'L0_attn_a_ffn_w2': _L0_attn_a_in['ffn_w2'], 'L0_attn_a_ffn_b2': _L0_attn_a_in['ffn_b2'], 'L0_attn_a_ln1_g': _L0_attn_a_in['ln1_g'], 'L0_attn_a_ln1_b': _L0_attn_a_in['ln1_b'], 'L0_attn_a_ln2_g': _L0_attn_a_in['ln2_g'], 'L0_attn_a_ln2_b': _L0_attn_a_in['ln2_b'], 'L0_attn_b_W_qkv': _L0_attn_b_in['W_qkv'], 'L0_attn_b_W_f': _L0_attn_b_in['W_f'], 'L0_attn_b_b_f': _L0_attn_b_in['b_f'], 'L0_attn_b_W_out': _L0_attn_b_in['W_out'], 'L0_attn_b_b_out': _L0_attn_b_in['b_out'], 'L0_ffn_gate_w': _L0_ffn_in['gate_w'], 'L0_ffn_lb_bias': _L0_ffn_in['lb_bias'], 'L0_ffn_w1': _L0_ffn_in['w1'], 'L0_ffn_w2': _L0_ffn_in['w2'], 'L0_ffn_cfc': _L0_ffn_in['cfc'], 'L0_ffn_cproj': _L0_ffn_in['cproj'], 'L1_attn_a_W_DQ': _L1_attn_a_in['W_DQ'], 'L1_attn_a_W_UQ': _L1_attn_a_in['W_UQ'], 'L1_attn_a_W_QR': _L1_attn_a_in['W_QR'], 'L1_attn_a_W_DKV': _L1_attn_a_in['W_DKV'], 'L1_attn_a_W_UK': _L1_attn_a_in['W_UK'], 'L1_attn_a_W_UV': _L1_attn_a_in['W_UV'], 'L1_attn_a_W_KR': _L1_attn_a_in['W_KR'], 'L1_attn_a_W_O': _L1_attn_a_in['W_O'], 'L1_attn_b_Wq': _L1_attn_b_in['Wq'], 'L1_attn_b_Wkv': _L1_attn_b_in['Wkv'], 'L1_attn_b_Wout': _L1_attn_b_in['Wout'], 'L1_attn_b_bout': _L1_attn_b_in['bout'], 'L1_attn_b_rel_emb': _L1_attn_b_in['rel_emb'], 'L1_ffn_gate_w': _L1_ffn_in['gate_w'], 'L1_ffn_gate_b': _L1_ffn_in['gate_b'], 'L1_ffn_rms_w': _L1_ffn_in['rms_w'], 'L1_ffn_w1': _L1_ffn_in['w1'], 'L1_ffn_b1': _L1_ffn_in['b1'], 'L1_ffn_w2': _L1_ffn_in['w2'], 'L1_ffn_b2': _L1_ffn_in['b2']}
    _x0 = _d['L0_attn_a_x']
    _d['L0_attn_a_x'] = jax.random.normal(jax.random.fold_in(jax.random.key(seed), 1), (4, 1024, 128), dtype=_x0.dtype)
    del _x0
    return _d

def reference(L0_attn_a_x, L0_attn_a_v_w, L0_attn_a_v_b, L0_attn_a_out_w, L0_attn_a_out_b, L0_attn_a_qmod_w, L0_attn_a_qmod_b, L0_attn_a_kmod_w, L0_attn_a_kmod_b, L0_attn_a_gate_w, L0_attn_a_gate_b, L0_attn_a_mod_w, L0_attn_a_mod_b, L0_attn_a_mod_basis, L0_attn_a_freqs, L0_attn_a_amps, L0_attn_a_phases, L0_attn_a_cq_w, L0_attn_a_ck_w, L0_attn_a_ffn_w1, L0_attn_a_ffn_b1, L0_attn_a_ffn_w2, L0_attn_a_ffn_b2, L0_attn_a_ln1_g, L0_attn_a_ln1_b, L0_attn_a_ln2_g, L0_attn_a_ln2_b, L0_attn_b_W_qkv, L0_attn_b_W_f, L0_attn_b_b_f, L0_attn_b_W_out, L0_attn_b_b_out, L0_ffn_gate_w, L0_ffn_lb_bias, L0_ffn_w1, L0_ffn_w2, L0_ffn_cfc, L0_ffn_cproj, L1_attn_a_W_DQ, L1_attn_a_W_UQ, L1_attn_a_W_QR, L1_attn_a_W_DKV, L1_attn_a_W_UK, L1_attn_a_W_UV, L1_attn_a_W_KR, L1_attn_a_W_O, L1_attn_b_Wq, L1_attn_b_Wkv, L1_attn_b_Wout, L1_attn_b_bout, L1_attn_b_rel_emb, L1_ffn_gate_w, L1_ffn_gate_b, L1_ffn_rms_w, L1_ffn_w1, L1_ffn_b1, L1_ffn_w2, L1_ffn_b2):

    def _L0_attn_a_ref(x, v_w, v_b, out_w, out_b, qmod_w, qmod_b, kmod_w, kmod_b, gate_w, gate_b, mod_w, mod_b, mod_basis, freqs, amps, phases, cq_w, ck_w, ffn_w1, ffn_b1, ffn_w2, ffn_b2, ln1_g, ln1_b, ln2_g, ln2_b):
        import jax, jax.numpy as jnp
        import numpy as np
        import math
        B, S, D = (2, 128, 128)
        H, M, W, RMOD, CR = (16, 16, 8, 8, 8)
        TOPK, ALPHA, MIX, STEP_A, TEMP = (8, 3.0, 0.15, 6.0, 1.0)

        def _topk_sparse(logits, k):
            soft = jax.nn.softmax(logits / max(TEMP, 1e-06), axis=-1)
            _, idx = jax.lax.top_k(soft, k)
            hard = jax.nn.one_hot(idx, logits.shape[-1], dtype=soft.dtype).sum(-2)
            hard = hard / (hard.sum(-1, keepdims=True) + 1e-08)
            return hard + jax.lax.stop_gradient(soft - hard)

        def _step(x):
            hard = (x > 0).astype(x.dtype)
            soft = jax.nn.sigmoid(STEP_A * x)
            return hard + jax.lax.stop_gradient(soft - hard)

        def _ln(x, g, b):
            mu = x.mean(-1, keepdims=True)
            var = x.var(-1, keepdims=True)
            return (x - mu) / jnp.sqrt(var + 1e-05) * g + b
        Bq, Sq, Dq = x.shape
        Hd = Dq // H
        v = (x @ v_w + v_b).reshape(Bq, Sq, H, Hd).transpose(0, 2, 1, 3)
        pooled = x.mean(axis=1)
        gl = (pooled @ gate_w + gate_b).reshape(Bq, H, M)
        mod = (pooled @ mod_w + mod_b).reshape(Bq, H, RMOD)
        gl = gl + jnp.einsum('bhr,rhm->bhm', mod, mod_basis)
        wts = _topk_sparse(gl.reshape(Bq * H, M), TOPK).reshape(Bq, H, M)
        rel = jnp.arange(-(Sq - 1), Sq, dtype=jnp.float32)
        p1 = rel / Sq
        p2 = jnp.sign(rel) * jnp.sqrt(jnp.abs(rel) + 1e-06) / math.sqrt(Sq)
        pos_kern = jnp.stack([p1, p2], axis=-1)
        arg = jnp.einsum('hmwc,pc->hmwp', freqs, pos_kern) + phases[..., None]
        kern_masks = jnp.einsum('hmw,hmwp->hmp', amps, jnp.sin(arg))
        kern = jnp.einsum('bhm,hmp->bhp', wts, kern_masks)
        density = _step(kern)
        dpos = jnp.arange(Sq, dtype=jnp.float32)
        window = jnp.exp(-dpos ** 2 / (2.0 * (Sq / 4.0) ** 2))
        causal_kern = ALPHA * density[:, :, Sq - 1:] * window
        idx = jnp.arange(Sq)
        doff = idx[:, None] - idx[None, :]
        causal = doff >= 0
        scores = jnp.take(causal_kern, jnp.maximum(doff, 0), axis=-1)
        qm = (x @ qmod_w + qmod_b).transpose(0, 2, 1)
        km = (x @ kmod_w + kmod_b).transpose(0, 2, 1)
        scores = scores + qm[..., :, None] + km[..., None, :]
        qc = (x @ cq_w).reshape(Bq, Sq, H, CR).transpose(0, 2, 1, 3)
        kc = (x @ ck_w).reshape(Bq, Sq, H, CR).transpose(0, 2, 1, 3)
        scores = scores + MIX * jnp.einsum('bhic,bhjc->bhij', qc, kc) / math.sqrt(CR)
        scores = jnp.where(causal, scores, -1000000000.0)
        attn = jax.nn.softmax(scores, axis=-1)
        ctx = jnp.einsum('bhij,bhjd->bhid', attn, v)
        ctx = ctx.transpose(0, 2, 1, 3).reshape(Bq, Sq, Dq)
        attn_out = ctx @ out_w + out_b
        h = _ln(x + attn_out, ln1_g, ln1_b)
        ffn = jax.nn.gelu(h @ ffn_w1 + ffn_b1, approximate=False) @ ffn_w2 + ffn_b2
        return _ln(h + ffn, ln2_g, ln2_b)

    def _L0_attn_b_ref(x, W_qkv, W_f, b_f, W_out, b_out):
        import jax, jax.numpy as jnp
        import numpy as np
        DIM = 128
        HEADS = 16
        DIM_HEAD = 64
        B, N, C = x.shape
        H, D = (HEADS, DIM_HEAD)
        qkv = x @ W_qkv
        q, k, v = jnp.split(qkv, 3, axis=-1)
        reshape = lambda t: t.reshape(B, N, H, D).transpose(0, 2, 1, 3)
        q, k, v = (reshape(q), reshape(k), reshape(v))
        fmap = lambda t: jax.nn.relu(t @ W_f + b_f)
        q = fmap(q)
        k = fmap(k)
        kv = jnp.einsum('bhnd,bhne->bhde', k, v)
        out = jnp.einsum('bhnd,bhde->bhne', q, kv)
        k_sum = k.sum(axis=2)
        normalizer = jnp.einsum('bhnd,bhd->bhn', q, k_sum)
        out = out / (normalizer[..., None] + 1e-06)
        out = out.transpose(0, 2, 1, 3).reshape(B, N, H * D)
        return out @ W_out + b_out

    def _L0_ffn_ref(x, gate_w, lb_bias, w1, w2, cfc, cproj):
        import jax, jax.numpy as jnp
        import numpy as np
        E = 8
        K = 2
        D = 128
        H = 128
        B, T = (2, 128)
        Bx, Tx, Dx = x.shape
        logits = jnp.einsum('btd,ed->bte', x, gate_w)
        _, idx = jax.lax.top_k(logits + lb_bias, K)
        sel_logits = jnp.take_along_axis(logits, idx, axis=-1)
        w = jax.nn.sigmoid(sel_logits)
        w = w / (jnp.sum(w, axis=-1, keepdims=True) + 1e-06)
        xf = x.reshape(-1, Dx)
        idxf = idx.reshape(-1, K)
        wf = w.reshape(-1, K)
        onehot = jax.nn.one_hot(idxf, E, dtype=wf.dtype)
        we = jnp.einsum('nke,nk->ne', onehot, wf)
        hidden = jnp.square(jax.nn.relu(jnp.einsum('nd,ehd->neh', xf, w1)))
        expert_out = jnp.einsum('neh,edh->ned', hidden, w2)
        moe_out = jnp.einsum('ned,ne->nd', expert_out, we).reshape(Bx, Tx, Dx)
        sh = jnp.square(jax.nn.relu(jnp.einsum('btd,hd->bth', x, cfc)))
        shared = jnp.einsum('bth,dh->btd', sh, cproj)
        return moe_out + shared

    def _L1_attn_a_ref(x, W_DQ, W_UQ, W_QR, W_DKV, W_UK, W_UV, W_KR, W_O):
        import jax, jax.numpy as jnp
        import numpy as np
        D_MODEL, N_HEADS = (128, 16)
        D_H = D_MODEL // N_HEADS
        D_HR = D_H // 2
        D_LATENT = 32
        THETA = 10000.0

        def rope(x, theta=THETA):
            S, d = (x.shape[-2], x.shape[-1])
            inv = theta ** (-jnp.arange(0, d, 2, dtype=jnp.float32) / d)
            ang = jnp.arange(S, dtype=jnp.float32)[:, None] * inv
            cos, sin = (jnp.cos(ang), jnp.sin(ang))
            x1, x2 = (x[..., 0::2], x[..., 1::2])
            r1 = x1 * cos - x2 * sin
            r2 = x1 * sin + x2 * cos
            return jnp.stack([r1, r2], axis=-1).reshape(x.shape)
        B, S, _ = x.shape
        d_qk = D_H + D_HR
        c_q = x @ W_DQ
        Qc = (c_q @ W_UQ).reshape(B, S, N_HEADS, D_H).transpose(0, 2, 1, 3)
        Qr = (c_q @ W_QR).reshape(B, S, N_HEADS, D_HR).transpose(0, 2, 1, 3)
        Qr = rope(Qr)
        c_kv = x @ W_DKV
        Kc = (c_kv @ W_UK).reshape(B, S, N_HEADS, D_H).transpose(0, 2, 1, 3)
        Kr = rope((x @ W_KR)[:, None, :, :])
        Kr = jnp.broadcast_to(Kr, (B, N_HEADS, S, D_HR))
        V = (c_kv @ W_UV).reshape(B, S, N_HEADS, D_H).transpose(0, 2, 1, 3)
        Q = jnp.concatenate([Qc, Qr], axis=-1)
        K = jnp.concatenate([Kc, Kr], axis=-1)
        scores = jnp.einsum('bhqd,bhkd->bhqk', Q, K)
        scores = jnp.clip(scores, -80.0, 80.0)
        causal = jnp.tril(jnp.ones((S, S), dtype=bool))
        scores = jnp.where(causal, scores, -jnp.inf)
        weights = jax.nn.softmax(scores / jnp.sqrt(jnp.float32(d_qk)), axis=-1)
        attn = jnp.einsum('bhqk,bhkd->bhqd', weights, V)
        attn = attn.transpose(0, 2, 1, 3).reshape(B, S, N_HEADS * D_H)
        return attn @ W_O

    def _L1_attn_b_ref(x, Wq, Wkv, Wout, bout, rel_emb):
        import jax, jax.numpy as jnp
        import numpy as np
        import math
        DIM = 128
        HEADS = 16
        DIM_HEAD = 64
        INNER = HEADS * DIM_HEAD
        NUM_BUCKETS = 32
        MAX_DISTANCE = 128

        def _relative_position_bucket(rel_pos, num_buckets=NUM_BUCKETS, max_distance=MAX_DISTANCE):
            n = jnp.maximum(-rel_pos, 0)
            max_exact = num_buckets // 2
            is_small = n < max_exact
            n_safe = jnp.maximum(n, 1)
            val_if_large = max_exact + (jnp.log(n_safe.astype(jnp.float32) / max_exact) / math.log(max_distance / max_exact) * (num_buckets - max_exact)).astype(jnp.int32)
            val_if_large = jnp.minimum(val_if_large, num_buckets - 1)
            return jnp.where(is_small, n, val_if_large)
        b, n, _ = x.shape
        scale = DIM_HEAD ** (-0.5)
        bias_scale = DIM_HEAD ** 0.5
        q = (x @ Wq).reshape(b, n, HEADS, DIM_HEAD).transpose(0, 2, 1, 3) * scale
        kv = x @ Wkv
        k, v = (kv[..., :DIM_HEAD], kv[..., DIM_HEAD:])
        sim = jnp.einsum('bhid,bjd->bhij', q, k)
        pos = jnp.arange(n, dtype=jnp.int32)
        rel_pos = pos[None, :] - pos[:, None]
        rp_bucket = _relative_position_bucket(rel_pos)
        bias = rel_emb[rp_bucket]
        sim = sim + jnp.transpose(bias, (2, 0, 1))[None] * bias_scale
        causal_mask = jnp.triu(jnp.ones((n, n), dtype=bool), k=1)
        neg = jnp.finfo(sim.dtype).max
        sim = jnp.where(causal_mask[None, None], -neg, sim)
        attn = jax.nn.softmax(sim, axis=-1)
        out = jnp.einsum('bhij,bjd->bhid', attn, v)
        out = out.transpose(0, 2, 1, 3).reshape(b, n, INNER)
        return out @ Wout + bout

    def _L1_ffn_ref(x, gate_w, gate_b, rms_w, w1, b1, w2, b2):
        import jax, jax.numpy as jnp
        import numpy as np
        TEMPERATURE = 0.5
        CAPACITY_FACTOR = 1.25
        TOP_K = 1
        B, S, D = x.shape
        E = gate_w.shape[0]
        xf = x.reshape(-1, D)
        N = xf.shape[0]
        logits = xf @ gate_w.T + gate_b
        eps = jnp.finfo(logits.dtype).eps
        ms = jnp.mean(logits * logits, axis=-1, keepdims=True)
        logits = logits * jax.lax.rsqrt(ms + eps) * rms_w
        gates = jax.nn.softmax(logits / TEMPERATURE, axis=-1)
        g, idx = jax.lax.top_k(gates, TOP_K)
        g, idx = (g[:, 0], idx[:, 0])
        capacity = min(int(np.ceil(N * TOP_K / E * CAPACITY_FACTOR)), N)
        counts = jnp.zeros((E,), jnp.int32).at[idx].add(1)
        active = (counts > 0) & (capacity >= 1)
        mask = active[idx].astype(gates.dtype)
        masked = g * mask
        norm_g = masked / (masked + 1e-06)
        h = jax.nn.gelu(jnp.einsum('nd,edh->neh', xf, w1) + b1, approximate=False)
        y = jnp.einsum('neh,ehd->ned', h, w2) + b2
        out = (y * norm_g[:, None, None]).sum(axis=1)
        return out.reshape(B, S, D)
    x = L0_attn_a_x
    x = x + _L0_attn_a_ref(_layernorm(x, axis=-1), L0_attn_a_v_w, L0_attn_a_v_b, L0_attn_a_out_w, L0_attn_a_out_b, L0_attn_a_qmod_w, L0_attn_a_qmod_b, L0_attn_a_kmod_w, L0_attn_a_kmod_b, L0_attn_a_gate_w, L0_attn_a_gate_b, L0_attn_a_mod_w, L0_attn_a_mod_b, L0_attn_a_mod_basis, L0_attn_a_freqs, L0_attn_a_amps, L0_attn_a_phases, L0_attn_a_cq_w, L0_attn_a_ck_w, L0_attn_a_ffn_w1, L0_attn_a_ffn_b1, L0_attn_a_ffn_w2, L0_attn_a_ffn_b2, L0_attn_a_ln1_g, L0_attn_a_ln1_b, L0_attn_a_ln2_g, L0_attn_a_ln2_b)
    x = x + _L0_ffn_ref(_layernorm(x, axis=-1), L0_ffn_gate_w, L0_ffn_lb_bias, L0_ffn_w1, L0_ffn_w2, L0_ffn_cfc, L0_ffn_cproj)
    x = x + _L0_attn_b_ref(_layernorm(x, axis=-1), L0_attn_b_W_qkv, L0_attn_b_W_f, L0_attn_b_b_f, L0_attn_b_W_out, L0_attn_b_b_out)
    x = x + _L0_ffn_ref(_layernorm(x, axis=-1), L0_ffn_gate_w, L0_ffn_lb_bias, L0_ffn_w1, L0_ffn_w2, L0_ffn_cfc, L0_ffn_cproj)
    x = x + _L1_attn_a_ref(_layernorm(x, axis=-1), L1_attn_a_W_DQ, L1_attn_a_W_UQ, L1_attn_a_W_QR, L1_attn_a_W_DKV, L1_attn_a_W_UK, L1_attn_a_W_UV, L1_attn_a_W_KR, L1_attn_a_W_O)
    x = x + _L1_ffn_ref(_layernorm(x, axis=-1), L1_ffn_gate_w, L1_ffn_gate_b, L1_ffn_rms_w, L1_ffn_w1, L1_ffn_b1, L1_ffn_w2, L1_ffn_b2)
    x = x + _L1_attn_b_ref(_layernorm(x, axis=-1), L1_attn_b_Wq, L1_attn_b_Wkv, L1_attn_b_Wout, L1_attn_b_bout, L1_attn_b_rel_emb)
    x = x + _L1_ffn_ref(_layernorm(x, axis=-1), L1_ffn_gate_w, L1_ffn_gate_b, L1_ffn_rms_w, L1_ffn_w1, L1_ffn_b1, L1_ffn_w2, L1_ffn_b2)
    return x

_drawn_inputs = setup_inputs


def setup_inputs(seed=0):
    import zlib

    import numpy as np

    out = dict(_drawn_inputs(seed))
    spreads = {'L0_attn_a_v_b': (0.0, 0.474),
     'L0_attn_a_out_b': (0.0, 0.1),
     'L0_attn_a_qmod_b': (0.0, 2.0),
     'L0_attn_a_kmod_b': (0.0, 2.0),
     'L0_attn_a_gate_b': (0.0, 0.8),
     'L0_attn_a_mod_b': (0.0, 0.8),
     'L0_attn_a_ffn_b1': (0.0, 0.523),
     'L0_attn_a_ffn_b2': (0.0, 0.1),
     'L0_attn_a_ln1_g': (1.0, 0.2),
     'L0_attn_a_ln1_b': (0.0, 0.1),
     'L0_attn_a_ln2_g': (1.0, 0.2),
     'L0_attn_a_ln2_b': (0.0, 0.1),
     'L0_ffn_lb_bias': (0.0, 0.8),
     'L1_attn_b_bout': (0.0, 0.447),
     'L1_ffn_gate_b': (0.0, 2.0),
     'L1_ffn_rms_w': (1.0, 0.6),
     'L1_ffn_b1': (0.0, 0.402),
     'L1_ffn_b2': (0.0, 0.1)}
    factors = {'L0_attn_a_v_w': 8.0,
     'L0_attn_a_out_w': 4.117,
     'L0_attn_a_qmod_w': 200.0,
     'L0_attn_a_kmod_w': 8.0,
     'L0_attn_a_gate_w': 8.0,
     'L0_attn_a_mod_w': 8.0,
     'L0_attn_a_mod_basis': 8.0,
     'L0_attn_a_freqs': 8.0,
     'L0_attn_a_amps': 8.0,
     'L0_attn_a_phases': 8.0,
     'L0_attn_a_cq_w': 8.0,
     'L0_attn_a_ck_w': 8.0,
     'L0_attn_b_W_f': 4.202,
     'L0_attn_b_b_f': 155.578,
     'L0_attn_b_b_out': 7.617,
     'L0_ffn_gate_w': 7.214,
     'L0_ffn_w1': 6.625,
     'L0_ffn_w2': 5.995,
     'L0_ffn_cfc': 4.507,
     'L0_ffn_cproj': 4.08,
     'L1_attn_b_rel_emb': 8.0,
     'L1_ffn_gate_w': 200.0,
     'L1_attn_a_W_QR': 5.892,
     'L1_attn_a_W_KR': 5.544,
     'L1_attn_a_W_UQ': 3.556,
     'L1_attn_a_W_UK': 3.533}
    for name, (base, spread) in spreads.items():
        noise = np.random.default_rng([zlib.crc32(name.encode()), seed]).standard_normal(out[name].shape)
        drawn = base * np.exp(spread * noise) if base else spread * noise
        out[name] = jnp.asarray(drawn.astype(out[name].dtype))
    for name, factor in factors.items():
        out[name] = (out[name] * factor).astype(out[name].dtype)
    return out
```

```python
import math
from contextlib import ExitStack

import concourse.bass as bass
from concourse import mybir

STAGES = '1,2,3,4,5,6,7,8'

F32 = mybir.dt.float32
BF16 = mybir.dt.bfloat16
I32 = mybir.dt.int32
ALU = mybir.AluOpType
ACT = mybir.ActivationFunctionType
AX = mybir.AxisListType

BATCH, SEQ, DIM = 4, 1024, 128
TOKENS = BATCH * SEQ
P = 128
GROUP_BLOCKS = 4
GROUP = GROUP_BLOCKS * P
GROUPS = TOKENS // GROUP
BLOCKS = TOKENS // P
LN_EPS = 1e-5


class Steps:

    def __init__(self, eng, sem, per_turn, turn):
        self.eng, self.sem, self.per_turn, self.base, self.k = eng, sem, per_turn, turn * per_turn, 0

    def done(self, ins):
        self.k += 1
        ins.then_inc(self.sem, 1)
        self.eng.wait_ge(self.sem, self.base + self.k)

    def close(self):
        assert self.k == self.per_turn, (self.k, self.per_turn)


def bcast(ap, n):
    return ap.unsqueeze(2).broadcast_to([ap.shape[0], ap.shape[1], n])


def semaphores(nc, ctx, tag):
    taken = []

    def give_back():
        nc.clear_and_free_semaphores(taken)
        nc.all_engine_barrier()

    def sem(name):
        taken.append(nc.alloc_semaphore(f"{tag}_{name}"))
        return taken[-1]

    ctx.callback(give_back)
    return sem


def ln_scratch(sb):
    return dict(st=sb("ln_stats", [P, GROUP_BLOCKS, 6], F32), mv=sb("ln_mean_var", [P, GROUP_BLOCKS, 2], F32),
                ve=sb("ln_var_eps", [P, GROUP_BLOCKS], F32), y=sb("ln_rstd", [P, GROUP_BLOCKS], F32),
                wait=sb("ln_wait", [P, 1], F32), t=sb("ln_newton", [P, GROUP_BLOCKS], F32))


def ln_rstd_vector(nc, dve, S, steps, rough_ready, rough_want, ve_ready):
    st, mv, ve, y, t = S["st"], S["mv"], S["ve"], S["y"], S["t"]
    nc.vector.memset(S["wait"][:], 0.0)
    for k in range(GROUP_BLOCKS):
        ins = nc.vector.bn_aggr(mv[:, k, :], st[:, k, :])
    steps.done(ins)
    nc.vector.tensor_scalar(ve[:], mv[:, :, 1], LN_EPS, None, ALU.add).then_inc(ve_ready, 1)
    dve.wait_ge(rough_ready, rough_want)
    steps.done(nc.vector.tensor_tensor(t[:], y[:], y[:], ALU.mult))
    steps.done(nc.vector.tensor_tensor(t[:], t[:], ve[:], ALU.mult))
    steps.done(nc.vector.tensor_scalar(t[:], t[:], -0.5, 1.5, ALU.mult, ALU.add))
    steps.done(nc.vector.tensor_tensor(y[:], y[:], t[:], ALU.mult))


def ln_group_vector(nc, dve, src, out, S, steps, rough_ready, rough_want, ve_ready):
    for k in range(GROUP_BLOCKS):
        ins = nc.vector.bn_stats(S["st"][:, k, :], src(k))
    steps.done(ins)
    ln_rstd_vector(nc, dve, S, steps, rough_ready, rough_want, ve_ready)
    for k in range(GROUP_BLOCKS):
        ins = nc.vector.tensor_scalar(out[:, k, :], src(k), S["mv"][:, k, 0:1], S["y"][:, k:k + 1],
                                      ALU.subtract, ALU.mult)
    return ins


LN_STEPS = 6


def store_x(sp, out, x, x_done, stored):
    with sp.Fori(0, GROUPS) as g:
        sp.wait_ge(x_done, g + 3)
        sp.dma_start(out[bass.ds(g * GROUP, GROUP), :].rearrange("(k p) d -> p k d", p=P),
                     x[:, bass.ds((g + 1) * GROUP_BLOCKS, GROUP_BLOCKS), :]).then_inc(stored, 16)
    sp.wait_ge(stored, 16 * GROUPS)


def l1_ffn(nc, D, x, C, tag, out=None):
    E, H = 8, 256
    HT = E * H // P
    RMS_EPS = 1.1920928955078125e-07
    with ExitStack() as ctx:
        def sb(name, shape, dt=F32):
            return ctx.enter_context(nc.sbuf_tensor(f"{tag}_{name}", shape, dt))

        def pb(name, shape, dt=F32):
            return ctx.enter_context(nc.psum_tensor(f"{tag}_{name}", shape, dt))

        sem = semaphores(nc, ctx, tag)

        S = ln_scratch(sb)
        w1 = sb("w1", [P, HT, P])
        w2 = sb("w2", [P, HT, DIM])
        b1 = sb("b1", [P, HT])
        b2 = sb("b2", [P, E])
        b2s = sb("b2s", [P, 1])
        gw = sb("gw", [P, E])
        gb = sb("gb", [P, E])
        rw = sb("rw", [P, E])
        xn = sb("xn", [P, 2, GROUP_BLOCKS, DIM])
        xt = sb("xt", [P, 2, GROUP])
        hT = sb("hT", [P, 4, GROUP])
        yT = sb("yT", [P, 2, GROUP])
        lgT = sb("lgT", [E, GROUP])
        lg = sb("lg", [P, GROUP_BLOCKS, E])
        lq = sb("lq", [P, GROUP_BLOCKS, E])
        ms = sb("ms", [P, GROUP_BLOCKS])
        rr = sb("rr", [P, GROUP_BLOCKS])
        tt = sb("tt", [P, GROUP_BLOCKS])
        ng = sb("ng", [P, 3, GROUP_BLOCKS])
        upd = sb("upd", [P, GROUP_BLOCKS, DIM])
        pH = [pb(f"pH{i}", [P, GROUP]) for i in range(4)]
        pY, pB, pT, pG = (pb(n, [P, GROUP]) for n in ("pY", "pB", "pT", "pG"))

        w_in, setup = sem("weights_in"), sem("setup")
        ln_step, ln_ve, ln_rough = sem("ln_step"), sem("ln_ve"), sem("ln_rough")
        xn_ready, xT_done, xt_ready = sem("xn_ready"), sem("xT_done"), sem("xt_ready")
        lg_done, lgT_ready, lgB_done = sem("lg_done"), sem("lgT_ready"), sem("lgB_done")
        g_step, g_ms, g_rough, g_exp = sem("g_step"), sem("g_ms"), sem("g_rough"), sem("g_exp")
        g_scores = sem("g_scores")
        h_done, hT_ready, hT_used = sem("h_done"), sem("hT_ready"), sem("hT_used")
        yT_ready, yB_done, x_step, x_done = (sem(n) for n in ("yT_ready", "yB_done", "x_step", "x_done"))
        stored = sem("stored")

        block = ctx.enter_context(nc.Block())
        NW = 7

        @block.sync
        def _(sp):
            sp.dma_start(gw[:], D["L1_ffn_gate_wT"]).then_inc(w_in, 16)
            sp.dma_start(gb[:], D["L1_ffn_gate_b"].broadcast_to([P, E])).then_inc(w_in, 16)
            sp.dma_start(rw[:], D["L1_ffn_rms_w"].broadcast_to([P, E])).then_inc(w_in, 16)
            sp.dma_start(b1[:], D["L1_ffn_b1"].rearrange("t p -> p t"), allow_slow_non_contiguous=True).then_inc(w_in, 16)
            sp.dma_start(b2[:], D["L1_ffn_b2"].rearrange("e d -> d e"), allow_slow_non_contiguous=True).then_inc(w_in, 16)
            sp.dma_start(w1[:], D["L1_ffn_w1"].rearrange("e d h -> d e h")).then_inc(w_in, 16)
            sp.dma_start(w2[:], D["L1_ffn_w2"].rearrange("t p d -> p t d")).then_inc(w_in, 16)
            if out is not None:
                store_x(sp, out, x, x_done, stored)

        @block.gpsimd
        def _(pool):
            nc.gpsimd.memset(yT[:, 1, :], 0.0)
            nc.gpsimd.memset(ng[:], 0.0).then_inc(setup, 1)

            def powers(turn):
                pool.wait_ge(ln_ve, turn + 1)
                nc.gpsimd.tensor_tensor(S["y"][:], S["ve"][:], C["mhalf"][:, 0:GROUP_BLOCKS], ALU.pow).then_inc(ln_rough, 1)
                pool.wait_ge(g_ms, turn + 1)
                nc.gpsimd.tensor_tensor(rr[:], ms[:], C["mhalf"][:, 0:GROUP_BLOCKS], ALU.pow).then_inc(g_rough, 1)

            powers(0)
            with pool.Fori(0, GROUPS) as g:
                powers(g + 1)

        def layernorm(dve, gn, par):
            steps = Steps(dve, ln_step, LN_STEPS, gn)
            dve.wait_ge(xT_done, gn)
            ln_group_vector(nc, dve, lambda k: x[:, bass.ds((gn + 1) * GROUP_BLOCKS + k, 1), :], xn[:, par], S, steps,
                            ln_rough, gn + 1, ln_ve).then_inc(xn_ready, 1)
            steps.close()

        def gate(dve, gn, par):
            steps = Steps(dve, g_step, 16, gn)
            dve.wait_ge(lgB_done, gn + 1)
            steps.done(nc.vector.tensor_tensor(lg[:], pT[:, 0:GROUP_BLOCKS * E].rearrange("p (k e) -> p k e", e=E),
                                               gb[:].unsqueeze(1).broadcast_to([P, GROUP_BLOCKS, E]), ALU.add))
            steps.done(nc.vector.tensor_tensor(lq[:], lg[:], lg[:], ALU.mult))
            steps.done(nc.vector.tensor_reduce(tt[:], lq[:], AX.X, ALU.add))
            nc.vector.tensor_scalar(ms[:], tt[:], 1.0 / E, RMS_EPS, ALU.mult, ALU.add).then_inc(g_ms, 1)
            dve.wait_ge(g_rough, gn + 1)
            steps.done(nc.vector.tensor_tensor(tt[:], rr[:], rr[:], ALU.mult))
            steps.done(nc.vector.tensor_tensor(tt[:], tt[:], ms[:], ALU.mult))
            steps.done(nc.vector.tensor_scalar(tt[:], tt[:], -0.5, 1.5, ALU.mult, ALU.add))
            steps.done(nc.vector.tensor_tensor(rr[:], rr[:], tt[:], ALU.mult))
            steps.done(nc.vector.tensor_tensor(lg[:], lg[:], bcast(rr[:], E), ALU.mult))
            steps.done(nc.vector.tensor_tensor(lg[:], lg[:], rw[:].unsqueeze(1).broadcast_to([P, GROUP_BLOCKS, E]), ALU.mult))
            steps.done(nc.vector.tensor_reduce(tt[:], lg[:], AX.X, ALU.max))
            nc.vector.tensor_tensor(lg[:], lg[:], bcast(tt[:], E), ALU.subtract).then_inc(g_scores, 1)
            dve.wait_ge(g_exp, gn + 1)
            steps.done(nc.vector.tensor_reduce(tt[:], lq[:], AX.X, ALU.add))
            steps.done(nc.vector.reciprocal(ms[:], tt[:]))
            steps.done(nc.vector.tensor_scalar(tt[:], ms[:], 1e-6, None, ALU.add))
            steps.done(nc.vector.reciprocal(rr[:], tt[:]))
            steps.done(nc.vector.tensor_tensor(ng[:, par, :], ms[:], rr[:], ALU.mult))
            steps.done(nc.vector.tensor_copy(tt[:], ms[:]))
            steps.close()

        def finish(dve, gp, par, turn):
            dve.wait_ge(yB_done, turn + 1)
            xs = x[:, bass.ds((gp + 1) * GROUP_BLOCKS, GROUP_BLOCKS), :]
            nc.vector.tensor_tensor(upd[:], pB[:].rearrange("p (k d) -> p k d", d=DIM), bcast(ng[:, par, :], DIM),
                                    ALU.mult).then_inc(x_step, 1)
            dve.wait_ge(x_step, turn + 2)
            nc.vector.tensor_tensor(xs, xs, upd[:], ALU.add).then_inc(x_done, 1)

        @block.vector
        def _(dve):
            dve.wait_ge(w_in, 16 * NW)
            nc.vector.tensor_reduce(b2s[:], b2[:], AX.X, ALU.add).then_inc(setup, 1)
            layernorm(dve, 0, 0)
            dve.wait_ge(setup, 2)
            gate(dve, 0, 0)
            with dve.Fori(0, GROUPS // 2) as it:
                for par in (0, 1):
                    g = it * 2 + par
                    layernorm(dve, g + 1, 1 - par)
                    finish(dve, g - 1, 1 - par, g)
                    gate(dve, g + 1, 1 - par)
            finish(dve, GROUPS - 1, 1, GROUPS)

        @block.scalar
        def _(act):
            def to_xt(gn, par):
                act.wait_ge(xT_done, gn + 1)
                nc.scalar.activation(xt[:, par, :], pT[:], ACT.Copy).then_inc(xt_ready, 1)

            def to_lgT(gn):
                act.wait_ge(lg_done, gn + 1)
                nc.scalar.activation(lgT[:], pG[0:E, :], ACT.Copy).then_inc(lgT_ready, 1)

            def gate_exp(gn):
                act.wait_ge(g_scores, gn + 1)
                nc.scalar.activation(lq[:], lg[:], ACT.Exp, scale=2.0).then_inc(g_exp, 1)

            act.wait_ge(w_in, 16 * NW)
            act.wait_ge(setup, 2)
            to_xt(0, 0)
            to_lgT(0)
            gate_exp(0)
            with act.Fori(0, GROUPS // 2) as it:
                for par in (0, 1):
                    g = it * 2 + par
                    for f in range(HT):
                        act.wait_ge(h_done, g * HT + f + 1)
                        act.wait_ge(hT_used, g * HT + f + 1)
                        nc.scalar.activation(hT[:, f % 4, :], pH[f % 4][:], ACT.Gelu, bias=b1[:, f:f + 1]).then_inc(hT_ready, 1)
                        if f == 9:
                            to_xt(g + 1, 1 - par)
                        if f == 11:
                            to_lgT(g + 1)
                        if f == 15:
                            gate_exp(g + 1)
                    act.wait_ge(hT_used, (g + 1) * HT + 4)
                    nc.scalar.activation(yT[:, par, :], pY[:], ACT.Identity, bias=b2s[:, 0:1]).then_inc(yT_ready, 1)

        @block.tensor
        def _(pe):
            def transposes(gn, par):
                pe.wait_ge(xn_ready, gn + 1)
                for k in range(GROUP_BLOCKS):
                    ins = nc.tensor.transpose(pT[:, k * P:(k + 1) * P], xn[:, par, k, :], C["ident"][:])
                ins.then_inc(xT_done, 1)

            def logits(gn, par):
                pe.wait_ge(xt_ready, gn + 1)
                nc.tensor.matmul(pG[0:E, :], gw[:], xt[:, par, :], start=True, stop=True).then_inc(lg_done, 1)

            def logits_back(gn):
                pe.wait_ge(lgT_ready, gn + 1)
                for k in range(GROUP_BLOCKS):
                    ins = nc.tensor.matmul(pT[:, k * E:(k + 1) * E], lgT[:, k * P:(k + 1) * P], C["ident"][0:E, 0:E],
                                           start=True, stop=True)
                ins.then_inc(lgB_done, 1)

            def y_back(turn, par):
                pe.wait_ge(yT_ready, turn + 1)
                pe.wait_ge(x_step, turn + 1)
                for k in range(GROUP_BLOCKS):
                    ins = nc.tensor.transpose(pB[:, k * P:(k + 1) * P], yT[:, par, k * P:(k + 1) * P], C["ident"][:])
                ins.then_inc(yB_done, 1)

            pe.wait_ge(w_in, 16 * NW)
            pe.wait_ge(setup, 2)
            pe.sem_inc(hT_used, 4)
            pe.sem_inc(yT_ready, 1)
            pe.sem_inc(x_step, 1)
            pe.sem_inc(x_done, 1)
            transposes(0, 0)
            logits(0, 0)
            logits_back(0)
            with pe.Fori(0, GROUPS // 2) as it:
                for par in (0, 1):
                    g = it * 2 + par

                    def down(f):
                        pe.wait_ge(hT_ready, g * HT + f + 1)
                        nc.tensor.matmul(pY[:], w2[:, f, :], hT[:, f % 4, :], start=(f == 0),
                                         stop=(f == HT - 1)).then_inc(hT_used, 1)

                    for f in range(HT):
                        if f >= 4:
                            pe.wait_ge(hT_ready, g * HT + f - 3)
                        else:
                            pe.wait_ge(yT_ready, g + 1)
                        nc.tensor.matmul(pH[f % 4][:], w1[:, f, :], xt[:, par, :], start=True, stop=True).then_inc(h_done, 1)
                        if f >= 2:
                            down(f - 2)
                        if f == 4:
                            y_back(g, 1 - par)
                        if f == 7:
                            pe.wait_ge(g_step, (g + 1) * 16)
                            transposes(g + 1, 1 - par)
                        if f == 9:
                            logits(g + 1, 1 - par)
                        if f == 11:
                            logits_back(g + 1)
                    down(HT - 2)
                    down(HT - 1)
            y_back(GROUPS, 1)


def l0_ffn(nc, D, x, C, tag, out=None):
    E = 8
    HT = E + 1
    NSLOT = 3
    with ExitStack() as ctx:
        def sb(name, shape, dt=F32):
            return ctx.enter_context(nc.sbuf_tensor(f"{tag}_{name}", shape, dt))

        def pb(name, shape, dt=F32):
            return ctx.enter_context(nc.psum_tensor(f"{tag}_{name}", shape, dt))

        sem = semaphores(nc, ctx, tag)

        S = ln_scratch(sb)
        w1 = sb("w1", [P, HT, P])
        w2 = sb("w2", [P, HT, DIM])
        gw = sb("gw", [P, E])
        lb = sb("lb", [P, E])
        rank = sb("rank", [P, E])
        sel24 = sb("sel24", [3 * E, E, P], BF16)
        xn = sb("xn", [P, 2, GROUP_BLOCKS, DIM])
        xt = sb("xt", [P, 2, GROUP])
        rT = sb("rT", [P, NSLOT, GROUP])
        hT = sb("hT", [P, NSLOT, GROUP])
        yT = sb("yT", [P, 2, GROUP])
        lgT = sb("lgT", [E, GROUP])
        G8 = [P, GROUP_BLOCKS, E]
        lg, sc, eq, sel1, sel2, sg, we, rest = (sb(n, G8) for n in ("lg", "sc", "eq", "sel1", "sel2", "sg", "we", "rest"))
        mx, den = sb("mx", [P, GROUP_BLOCKS]), sb("den", [P, GROUP_BLOCKS])
        we3 = sb("we3", [P, GROUP_BLOCKS, 3 * E], BF16)
        weT = sb("weT", [3 * E, 2, GROUP], BF16)
        pH = [pb(f"pH{i}", [P, GROUP]) for i in range(2)]
        pW = [pb(f"pW{i}", [P, GROUP]) for i in range(2)]
        pY, pB, pT, pG = (pb(n, [P, GROUP]) for n in ("pY", "pB", "pT", "pG"))
        pGb = pG[:].bitcast(BF16)

        w_in, setup = sem("weights_in"), sem("setup")
        ln_step, ln_ve, ln_rough = sem("ln_step"), sem("ln_ve"), sem("ln_rough")
        xn_ready, xT_done, xt_ready = sem("xn_ready"), sem("xT_done"), sem("xt_ready")
        lg_done, lgT_ready, lgB_done = sem("lg_done"), sem("lgT_ready"), sem("lgB_done")
        g_step, lg_ready, sg_ready = sem("g_step"), sem("lg_ready"), sem("sg_ready")
        we_done, weT_ready, wb_done, wb_used = sem("we_done"), sem("weT_ready"), sem("wb_done"), sem("wb_used")
        h_done, r_ready, s_ready, hT_ready, hT_used = (sem(n) for n in
                                                      ("h_done", "r_ready", "s_ready", "hT_ready", "hT_used"))
        yT_ready, yB_done, x_step, x_done = (sem(n) for n in ("yT_ready", "yB_done", "x_step", "x_done"))
        stored = sem("stored")
        NW = 8
        G_STEPS = 23

        block = ctx.enter_context(nc.Block())

        @block.sync
        def _(sp):
            sp.dma_start(gw[:], D["L0_ffn_gate_wT"]).then_inc(w_in, 16)
            sp.dma_start(lb[:], D["L0_ffn_lb_bias"].broadcast_to([P, E])).then_inc(w_in, 16)
            sp.dma_start(rank[:], D["rank"].broadcast_to([P, E])).then_inc(w_in, 16)
            sp.dma_start(sel24[:], D["sel24"]).then_inc(w_in, 16)
            sp.dma_start(w1[:, 0:E, :], D["L0_ffn_w1T"].rearrange("e d h -> d e h")).then_inc(w_in, 16)
            sp.dma_start(w1[:, E, :], D["L0_ffn_cfcT"]).then_inc(w_in, 16)
            sp.dma_start(w2[:, 0:E, :], D["L0_ffn_w2T"].rearrange("e h d -> h e d")).then_inc(w_in, 16)
            sp.dma_start(w2[:, E, :], D["L0_ffn_cprojT"]).then_inc(w_in, 16)
            if out is not None:
                store_x(sp, out, x, x_done, stored)

        @block.gpsimd
        def _(pool):
            nc.gpsimd.memset(yT[:, 1, :], 0.0).then_inc(setup, 1)

            def powers(turn):
                pool.wait_ge(ln_ve, turn + 1)
                nc.gpsimd.tensor_tensor(S["y"][:], S["ve"][:], C["mhalf"][:, 0:GROUP_BLOCKS], ALU.pow).then_inc(ln_rough, 1)

            powers(0)
            with pool.Fori(0, GROUPS) as g:
                powers(g + 1)

        def layernorm(dve, gn, par):
            steps = Steps(dve, ln_step, LN_STEPS, gn)
            dve.wait_ge(xT_done, gn)
            ln_group_vector(nc, dve, lambda k: x[:, bass.ds((gn + 1) * GROUP_BLOCKS + k, 1), :], xn[:, par], S, steps,
                            ln_rough, gn + 1, ln_ve).then_inc(xn_ready, 1)
            steps.close()

        def gate(dve, gn):
            steps = Steps(dve, g_step, G_STEPS, gn)

            def spread(t):
                return t[:].unsqueeze(1).broadcast_to(G8)

            dve.wait_ge(lgB_done, gn + 1)
            nc.vector.tensor_copy(lg[:], pT[:, 0:GROUP_BLOCKS * E].rearrange("p (k e) -> p k e", e=E)).then_inc(lg_ready, 1)
            dve.wait_ge(lg_ready, gn + 1)
            steps.done(nc.vector.tensor_tensor(sc[:], lg[:], spread(lb), ALU.add))
            for sel in (sel1, sel2):
                steps.done(nc.vector.tensor_reduce(mx[:], sc[:], AX.X, ALU.max))
                steps.done(nc.vector.tensor_tensor(eq[:], sc[:], bcast(mx[:], E), ALU.is_ge))
                steps.done(nc.vector.tensor_tensor(eq[:], eq[:], spread(rank), ALU.mult))
                steps.done(nc.vector.tensor_reduce(mx[:], eq[:], AX.X, ALU.max))
                steps.done(nc.vector.tensor_tensor(sel[:], eq[:], bcast(mx[:], E), ALU.is_equal))
                if sel is sel1:
                    steps.done(nc.vector.scalar_tensor_tensor(sc[:], sel1[:], -3e38, sc[:], ALU.mult, ALU.add))
            steps.done(nc.vector.tensor_tensor(sel1[:], sel1[:], sel2[:], ALU.add))
            dve.wait_ge(sg_ready, gn + 1)
            steps.done(nc.vector.tensor_tensor(sg[:], sg[:], sel1[:], ALU.mult))
            steps.done(nc.vector.tensor_reduce(den[:], sg[:], AX.X, ALU.add))
            steps.done(nc.vector.tensor_scalar(den[:], den[:], 1e-6, None, ALU.add))
            steps.done(nc.vector.reciprocal(mx[:], den[:]))
            steps.done(nc.vector.tensor_tensor(we[:], sg[:], bcast(mx[:], E), ALU.mult))
            steps.done(nc.vector.tensor_copy(we3[:, :, 0:E], we[:]))
            steps.done(nc.vector.tensor_tensor(rest[:], we[:], we3[:, :, 0:E], ALU.subtract))
            steps.done(nc.vector.tensor_copy(we3[:, :, E:2 * E], rest[:]))
            steps.done(nc.vector.tensor_tensor(rest[:], rest[:], we3[:, :, E:2 * E], ALU.subtract))
            steps.done(nc.vector.tensor_copy(we3[:, :, 2 * E:3 * E], rest[:]))
            steps.close()

        def finish(dve, gp, turn):
            dve.wait_ge(yB_done, turn + 1)
            xs = x[:, bass.ds((gp + 1) * GROUP_BLOCKS, GROUP_BLOCKS), :]
            nc.vector.tensor_tensor(xs, xs, pB[:].rearrange("p (k d) -> p k d", d=DIM), ALU.add).then_inc(x_done, 1)

        @block.vector
        def _(dve):
            dve.wait_ge(w_in, 16 * NW)
            layernorm(dve, 0, 0)
            gate(dve, 0)
            with dve.Fori(0, GROUPS // 2) as it:
                for par in (0, 1):
                    g = it * 2 + par

                    def weigh(e):
                        n = g * E + e + 1
                        dve.wait_ge(wb_done, n)
                        dve.wait_ge(s_ready, g * HT + e + 1)
                        dve.wait_ge(hT_used, g * HT + e + 1)
                        nc.vector.tensor_tensor(hT[:, e % NSLOT, :], rT[:, e % NSLOT, :], pW[e % 2][:], ALU.mult).then_inc(wb_used, 1)

                    weigh(0)
                    layernorm(dve, g + 1, 1 - par)
                    weigh(1)
                    finish(dve, g - 1, g)
                    weigh(2)
                    weigh(3)
                    gate(dve, g + 1)
                    for e in range(4, E):
                        weigh(e)
            finish(dve, GROUPS - 1, GROUPS)

        @block.scalar
        def _(act):
            def to_xt(gn, par):
                act.wait_ge(xT_done, gn + 1)
                nc.scalar.activation(xt[:, par, :], pT[:], ACT.Copy).then_inc(xt_ready, 1)

            def to_lgT(gn):
                act.wait_ge(lg_done, gn + 1)
                nc.scalar.activation(lgT[:], pG[0:E, :], ACT.Copy).then_inc(lgT_ready, 1)

            def gate_sigmoid(gn):
                act.wait_ge(lg_ready, gn + 1)
                nc.scalar.activation(sg[:], lg[:], ACT.Sigmoid).then_inc(sg_ready, 1)

            def to_weT(gn, par):
                act.wait_ge(we_done, gn + 1)
                nc.scalar.activation(weT[:, par, :], pGb[0:3 * E, 0:GROUP], ACT.Copy).then_inc(weT_ready, 1)

            act.wait_ge(w_in, 16 * NW)
            to_xt(0, 0)
            to_lgT(0)
            gate_sigmoid(0)
            to_weT(0, 0)
            with act.Fori(0, GROUPS // 2) as it:
                for par in (0, 1):
                    g = it * 2 + par

                    def relu(f):
                        act.wait_ge(h_done, g * HT + f + 1)
                        if f >= NSLOT:
                            act.wait_ge(wb_used, g * E + f - NSLOT + 1)
                        nc.scalar.activation(rT[:, f % NSLOT, :], pH[f % 2][:], ACT.Relu).then_inc(r_ready, 1)

                    def square(f):
                        act.wait_ge(r_ready, g * HT + f + 1)
                        to = rT
                        if f == E:
                            act.wait_ge(hT_used, g * HT + f + 1)
                            to = hT
                        nc.scalar.activation(to[:, f % NSLOT, :], rT[:, f % NSLOT, :], ACT.Square).then_inc(s_ready, 1)

                    relu(0)
                    for f in range(1, HT):
                        relu(f)
                        square(f - 1)
                        if f == 3:
                            to_xt(g + 1, 1 - par)
                        if f == 4:
                            to_lgT(g + 1)
                        if f == 5:
                            gate_sigmoid(g + 1)
                    square(E)
                    act.wait_ge(hT_used, (g + 1) * HT + NSLOT)
                    nc.scalar.activation(yT[:, par, :], pY[:], ACT.Copy).then_inc(yT_ready, 1)
                    to_weT(g + 1, 1 - par)

        @block.tensor
        def _(pe):
            def transposes(gn, par):
                pe.wait_ge(xn_ready, gn + 1)
                for k in range(GROUP_BLOCKS):
                    ins = nc.tensor.transpose(pT[:, k * P:(k + 1) * P], xn[:, par, k, :], C["ident"][:])
                ins.then_inc(xT_done, 1)

            def logits(gn, par):
                pe.wait_ge(xt_ready, gn + 1)
                nc.tensor.matmul(pG[0:E, :], gw[:], xt[:, par, :], start=True, stop=True).then_inc(lg_done, 1)

            def logits_back(gn):
                pe.wait_ge(lgT_ready, gn + 1)
                for k in range(GROUP_BLOCKS):
                    ins = nc.tensor.matmul(pT[:, k * E:(k + 1) * E], lgT[:, k * P:(k + 1) * P], C["ident"][0:E, 0:E],
                                           start=True, stop=True)
                ins.then_inc(lgB_done, 1)

            def weights_T(gn):
                pe.wait_ge(g_step, (gn + 1) * G_STEPS)
                for k in range(GROUP_BLOCKS):
                    ins = nc.tensor.transpose(pGb[0:3 * E, k * P:(k + 1) * P], we3[:, k, :], C["ident16"][:])
                ins.then_inc(we_done, 1)

            def y_back(turn, par):
                pe.wait_ge(yT_ready, turn + 1)
                pe.wait_ge(x_done, turn + 1)
                for k in range(GROUP_BLOCKS):
                    ins = nc.tensor.transpose(pB[:, k * P:(k + 1) * P], yT[:, par, k * P:(k + 1) * P], C["ident"][:])
                ins.then_inc(yB_done, 1)

            pe.wait_ge(w_in, 16 * NW)
            pe.wait_ge(setup, 1)
            pe.sem_inc(hT_used, NSLOT)
            pe.sem_inc(yT_ready, 1)
            pe.sem_inc(x_done, 1)
            transposes(0, 0)
            logits(0, 0)
            logits_back(0)
            weights_T(0)
            with pe.Fori(0, GROUPS // 2) as it:
                for par in (0, 1):
                    g = it * 2 + par

                    def down(f):
                        if f < E:
                            pe.wait_ge(wb_used, g * E + f + 1)
                        else:
                            pe.wait_ge(s_ready, (g + 1) * HT)
                        nc.tensor.matmul(pY[:], w2[:, f, :], hT[:, f % NSLOT, :], start=(f == 0),
                                         stop=(f == HT - 1)).then_inc(hT_used, 1)

                    pe.wait_ge(weT_ready, g + 1)
                    for f in range(HT):
                        if f >= 2:
                            pe.wait_ge(r_ready, g * HT + f - 1)
                        nc.tensor.matmul(pH[f % 2][:], w1[:, f, :], xt[:, par, :], start=True, stop=True).then_inc(h_done, 1)
                        if f < E:
                            if f >= 2:
                                pe.wait_ge(wb_used, g * E + f - 1)
                            nc.tensor.matmul(pW[f % 2][:], sel24[:, f, :], weT[:, par, :], start=True, stop=True).then_inc(wb_done, 1)
                        if f == 1:
                            y_back(g, 1 - par)
                        if f == 2:
                            pe.wait_ge(lg_ready, g + 1)
                            transposes(g + 1, 1 - par)
                        if f == 3:
                            logits(g + 1, 1 - par)
                        if f == 4:
                            logits_back(g + 1)
                        if f >= 2:
                            down(f - 2)
                    down(HT - 2)
                    down(HT - 1)
                    weights_T(g + 1)
            y_back(GROUPS, 1)


def l0_attn_b(nc, D, x, C, tag, out=None):
    HEADS, HD = 16, 64
    INNER = HEADS * HD
    PAIRS = HEADS // 2
    BANK_PAIRS = 3
    VC = 2 * HD + 1
    HALVES = SEQ // GROUP
    with ExitStack() as ctx:
        def sb(name, shape, dt=F32):
            return ctx.enter_context(nc.sbuf_tensor(f"{tag}_{name}", shape, dt))

        def pb(name, shape, dt=F32):
            return ctx.enter_context(nc.psum_tensor(f"{tag}_{name}", shape, dt))

        sem = semaphores(nc, ctx, tag)

        S = ln_scratch(sb)
        wqkT = sb("wqkT", [HD, 2 * HEADS, DIM])
        wf = sb("wf", [HD, HD])
        wq = sb("wq", [P, INNER])
        wk = sb("wk", [P, INNER])
        wv = sb("wv", [P, INNER])
        wo = sb("wo", [P, PAIRS, DIM])
        bo = sb("bo", [P, 1])
        bf = sb("bf", [P, 1])
        bfr = sb("bfr", [P, GROUP // HD, HD])
        eps = sb("eps", [P, 1])
        xn = sb("xn", [P, 2, GROUP_BLOCKS, DIM])
        xt = sb("xt", [P, 2, GROUP])
        qT = sb("qT", [P, PAIRS, SEQ])
        kr = sb("kr", [P, 2, INNER])
        vb = sb("vb", [P, 2, PAIRS, VC])
        kvd = sb("kvd", [P, PAIRS, P])
        ksd = sb("ksd", [P, PAIRS, P])
        dn = sb("dn", [P, 2, GROUP])
        cT = sb("cT", [P, 2, GROUP])
        yT = sb("yT", [P, 2, GROUP])
        pA = [pb(f"pA{i}", [P, GROUP]) for i in range(3)]
        pK = [pb(f"pK{i}", [P, GROUP]) for i in range(3)]
        pY, pT = pb("pY", [P, GROUP]), pb("pT", [P, GROUP])

        w_in, setup, folded, fold_used = sem("weights_in"), sem("setup"), sem("folded"), sem("fold_used")
        ln_step, ln_ve, ln_rough = sem("ln_step"), sem("ln_ve"), sem("ln_rough")
        xn_ready, xT_done, xt_ready = sem("xn_ready"), sem("xT_done"), sem("xt_ready")
        q_done, q_used, k_done, k_raw, k_ready = sem("q_done"), sem("q_used"), sem("k_done"), sem("k_raw"), sem("k_ready")
        v_done, v_ready, kv_done, kvd_ready = sem("v_done"), sem("v_ready"), sem("kv_done"), sem("kvd_ready")
        nd_done, dn_ready, dn_step, c_ready, c_used = (sem(n) for n in
                                                      ("nd_done", "dn_ready", "dn_step", "c_ready", "c_used"))
        yT_ready, yB_done, x_done = (sem(n) for n in ("yT_ready", "yB_done", "x_done"))
        stored = sem("stored")
        NW = 7

        jobs = []
        for half in range(HALVES):
            jobs += [("q", half, i) for i in range(PAIRS)]
            for tb in range(GROUP_BLOCKS):
                jobs += [("k", half * GROUP_BLOCKS + tb, i) for i in (0, 1)]
                jobs += [("v", half * GROUP_BLOCKS + tb, i) for i in (0, 1)]
        PER = {"q": HALVES * PAIRS, "k": 2 * HALVES * GROUP_BLOCKS, "v": 2 * HALVES * GROUP_BLOCKS}
        used = {"q": q_used, "k": k_raw, "v": v_ready}

        def number(job):
            kind, a, i = job
            return a * PAIRS + i if kind == "q" else 2 * a + i

        block = ctx.enter_context(nc.Block())

        @block.sync
        def _(sp):
            sp.dma_start(wf[:], D["L0_attn_b_W_f"]).then_inc(w_in, 16)
            sp.dma_start(wqkT[:], D["L0_attn_b_WqkT"].rearrange("(h d) n -> d h n", d=HD)).then_inc(w_in, 16)
            sp.dma_start(wv[:], D["L0_attn_b_Wv"]).then_inc(w_in, 16)
            sp.dma_start(wo[:], D["L0_attn_b_W_out"].rearrange("(t p) n -> p t n", p=P)).then_inc(w_in, 16)
            sp.dma_start(bo[:], D["L0_attn_b_b_out"]).then_inc(w_in, 16)
            sp.dma_start(bf[:], D["L0_attn_b_b_f2"]).then_inc(w_in, 16)
            sp.dma_start(bfr[:], D["L0_attn_b_b_f"].unsqueeze(1).broadcast_to([P, GROUP // HD, HD])).then_inc(w_in, 16)
            if out is not None:
                store_x(sp, out, x, x_done, stored)

        @block.gpsimd
        def _(pool):
            nc.gpsimd.memset(yT[:, 1, :], 0.0).then_inc(setup, 1)
            nc.gpsimd.memset(eps[:], 1e-6).then_inc(setup, 1)
            nc.gpsimd.memset(kvd[:], 0.0).then_inc(setup, 1)
            nc.gpsimd.memset(ksd[:], 0.0).then_inc(setup, 1)
            nc.gpsimd.memset(vb[:, :, :, VC - 1:VC], 1.0).then_inc(setup, 1)

            def powers(turn):
                pool.wait_ge(ln_ve, turn + 1)
                nc.gpsimd.tensor_tensor(S["y"][:], S["ve"][:], C["mhalf"][:, 0:GROUP_BLOCKS], ALU.pow).then_inc(ln_rough, 1)

            powers(0)
            with pool.Fori(0, GROUPS) as g:
                powers(g + 1)

        def layernorm(dve, gn, par):
            steps = Steps(dve, ln_step, LN_STEPS, gn)
            dve.wait_ge(xT_done, gn)
            ln_group_vector(nc, dve, lambda k: x[:, bass.ds((gn + 1) * GROUP_BLOCKS + k, 1), :], xn[:, par], S, steps,
                            ln_rough, gn + 1, ln_ve).then_inc(xn_ready, 1)
            steps.close()

        def finish(dve, gp, turn):
            dve.wait_ge(yB_done, turn + 1)
            xs = x[:, bass.ds((gp + 1) * GROUP_BLOCKS, GROUP_BLOCKS), :]
            nc.vector.tensor_tensor(xs, xs, pT[:].rearrange("p (k d) -> p k d", d=DIM), ALU.add).then_inc(x_done, 1)

        @block.vector
        def _(dve):
            dve.wait_ge(w_in, 16 * NW)
            for i, w in enumerate((wq, wk)):
                dve.wait_ge(folded, i + 1)
                for j in (0, 1):
                    nc.vector.tensor_copy(w[:, j * GROUP:(j + 1) * GROUP], pA[j][:]).then_inc(fold_used, 1)
            dve.wait_ge(setup, 5)
            layernorm(dve, 0, 0)
            with dve.Fori(0, BATCH) as b:
                layernorm(dve, b * 2 + 1, 1)
                finish(dve, b * 2 - 1, b * 2)
                for job in jobs:
                    if job[0] != "k":
                        continue
                    n, tb = number(job), job[1]
                    i = job[2]
                    dve.wait_ge(k_done, b * PER["k"] + n + 1)
                    dve.wait_ge(kv_done, b * 8 + tb + 1)
                    bank = jobs.index(job) % 3
                    nc.vector.tensor_tensor(kr[:, tb % 2, i * GROUP:(i + 1) * GROUP], pA[bank][:],
                                            bfr[:].rearrange("p a d -> p (a d)"), ALU.add).then_inc(k_raw, 1)
                dve.wait_ge(kv_done, b * 8 + 10)
                for t in range(PAIRS):
                    src = pK[t // BANK_PAIRS][:, (t % BANK_PAIRS) * VC:(t % BANK_PAIRS + 1) * VC]
                    for lo in (0, HD):
                        nc.vector.tensor_copy(kvd[lo:lo + HD, t, lo:lo + HD], src[lo:lo + HD, lo:lo + HD])
                        ins = nc.vector.tensor_copy(ksd[lo:lo + HD, t, lo:lo + HD],
                                                    src[lo:lo + HD, VC - 1:VC].broadcast_to([HD, HD]))
                ins.then_inc(kvd_ready, 1)
                layernorm(dve, b * 2 + 2, 0)
                for half in range(HALVES):
                    for t in range(PAIRS):
                        n = b * HALVES * PAIRS + half * PAIRS + t
                        dve.wait_ge(dn_ready, n + 1)
                        nc.vector.reciprocal(dn[:, t % 2, :], dn[:, t % 2, :]).then_inc(dn_step, 1)
                        dve.wait_ge(dn_step, n + 1)
                        dve.wait_ge(c_used, n + 1)
                        nc.vector.tensor_tensor(cT[:, t % 2, :], pA[t % 2][:], dn[:, t % 2, :], ALU.mult).then_inc(c_ready, 1)
                        if half == 1 and t == 2:
                            finish(dve, b * 2, b * 2 + 1)
            finish(dve, GROUPS - 1, GROUPS)

        @block.scalar
        def _(act):
            def to_xt(gn, par):
                act.wait_ge(xT_done, gn + 1)
                nc.scalar.activation(xt[:, par, :], pT[:], ACT.Copy).then_inc(xt_ready, 1)

            act.wait_ge(w_in, 16 * NW)
            act.wait_ge(setup, 5)
            to_xt(0, 0)
            with act.Fori(0, BATCH) as b:
                for j, job in enumerate(jobs):
                    kind, a, i = job
                    n = b * PER[kind] + number(job)
                    if kind == "q":
                        act.wait_ge(q_done, n + 1)
                        nc.scalar.activation(qT[:, i, a * GROUP:(a + 1) * GROUP], pA[j % 3][:], ACT.Relu,
                                             bias=bf[:, 0:1]).then_inc(q_used, 1)
                        if a == 0 and i == 6:
                            to_xt(b * 2 + 1, 1)
                    elif kind == "k":
                        act.wait_ge(k_raw, n + 1)
                        ks = kr[:, a % 2, i * GROUP:(i + 1) * GROUP]
                        nc.scalar.activation(ks, ks, ACT.Relu).then_inc(k_ready, 1)
                    else:
                        act.wait_ge(v_done, n + 1)
                        act.wait_ge(kv_done, b * 8 + a + 1)
                        nc.scalar.activation(vb[:, a % 2, i * 4:i * 4 + 4, 0:2 * HD],
                                             pA[j % 3][:].rearrange("p (t c) -> p t c", c=2 * HD), ACT.Copy).then_inc(v_ready, 1)
                for half in range(HALVES):
                    for t in range(PAIRS):
                        n = b * HALVES * PAIRS + half * PAIRS + t
                        act.wait_ge(nd_done, n + 1)
                        act.wait_ge(c_used, n + 1)
                        nc.scalar.activation(dn[:, t % 2, :], pK[t % 2][:], ACT.Identity, bias=eps[:, 0:1]).then_inc(dn_ready, 1)
                        if half == 0 and t == 2:
                            to_xt(b * 2 + 2, 0)
                    act.wait_ge(c_used, (b * 2 + half + 1) * PAIRS + 2)
                    nc.scalar.activation(yT[:, half, :], pY[:], ACT.Identity, bias=bo[:, 0:1]).then_inc(yT_ready, 1)

        @block.tensor
        def _(pe):
            def transposes(gn, par):
                pe.wait_ge(xn_ready, gn + 1)
                for k in range(GROUP_BLOCKS):
                    ins = nc.tensor.transpose(pT[:, k * P:(k + 1) * P], xn[:, par, k, :], C["ident"][:])
                ins.then_inc(xT_done, 1)

            def y_back(turn, par):
                pe.wait_ge(yT_ready, turn + 1)
                for k in range(GROUP_BLOCKS):
                    ins = nc.tensor.transpose(pT[:, k * P:(k + 1) * P], yT[:, par, k * P:(k + 1) * P], C["ident"][:])
                ins.then_inc(yB_done, 1)

            pe.wait_ge(w_in, 16 * NW)
            for i in (0, 1):
                if i:
                    pe.wait_ge(fold_used, 2)
                for h in range(HEADS):
                    ins = nc.tensor.matmul(pA[h // 8][:, (h % 8) * HD:(h % 8 + 1) * HD], wqkT[:, i * HEADS + h, :], wf[:],
                                           start=True, stop=True)
                ins.then_inc(folded, 1)
            pe.wait_ge(fold_used, 4)
            pe.wait_ge(setup, 5)
            pe.sem_inc(kv_done, 2)
            pe.sem_inc(c_used, 2)
            pe.sem_inc(yT_ready, 1)
            pe.sem_inc(x_done, 1)
            transposes(0, 0)
            with pe.Fori(0, BATCH) as b:
                def kv(tb):
                    pe.wait_ge(k_ready, b * PER["k"] + 2 * tb + 2)
                    pe.wait_ge(v_ready, b * PER["v"] + 2 * tb + 2)
                    for t in range(PAIRS):
                        ins = nc.tensor.matmul(pK[t // BANK_PAIRS][:, (t % BANK_PAIRS) * VC:(t % BANK_PAIRS + 1) * VC],
                                               kr[:, tb % 2, t * P:(t + 1) * P], vb[:, tb % 2, t, :],
                                               start=(tb == 0 and t % BANK_PAIRS == 0), stop=(tb == 7),
                                               skip_group_check=True)
                    ins.then_inc(kv_done, 1)

                pe.wait_ge(yT_ready, b * 2 + 1)
                for j, job in enumerate(jobs):
                    kind, a, i = job
                    if j % (len(jobs) // 2) == 0:
                        pe.wait_ge(xt_ready, b * 2 + j // (len(jobs) // 2) + 1)
                    if j >= 3:
                        before = jobs[j - 3]
                        pe.wait_ge(used[before[0]], b * PER[before[0]] + number(before) + 1)
                    half = a if kind == "q" else a // GROUP_BLOCKS
                    if kind == "q":
                        nc.tensor.matmul(pA[j % 3][:], wq[:, i * P:(i + 1) * P], xt[:, half, :], start=True, stop=True).then_inc(q_done, 1)
                        if a == 0 and i == 2:
                            y_back(b * 2, 1)
                        if a == 0 and i == 6:
                            pe.wait_ge(x_done, b * 2 + 2)
                            transposes(b * 2 + 1, 1)
                    else:
                        w, done = (wk, k_done) if kind == "k" else (wv, v_done)
                        tb = a % GROUP_BLOCKS
                        nc.tensor.matmul(pA[j % 3][:], xt[:, half, tb * P:(tb + 1) * P], w[:, i * GROUP:(i + 1) * GROUP],
                                         start=True, stop=True).then_inc(done, 1)
                        if kind == "v" and i == 1 and a >= 1:
                            kv(a - 1)
                kv(7)
                pe.wait_ge(kvd_ready, b + 1)
                for half in range(HALVES):
                    def down(t):
                        pe.wait_ge(c_ready, b * HALVES * PAIRS + half * PAIRS + t + 1)
                        nc.tensor.matmul(pY[:], wo[:, t, :], cT[:, t % 2, :], start=(t == 0), stop=(t == PAIRS - 1)).then_inc(c_used, 1)

                    if half:
                        pe.wait_ge(yT_ready, b * 2 + 2)
                    for t in range(PAIRS):
                        n = b * HALVES * PAIRS + half * PAIRS + t
                        if half or t >= 2:
                            pe.wait_ge(c_ready, n - 1)
                        q = qT[:, t, half * GROUP:(half + 1) * GROUP]
                        nc.tensor.matmul(pA[t % 2][:], kvd[:, t, :], q, start=True, stop=True)
                        nc.tensor.matmul(pK[t % 2][:], ksd[:, t, :], q, start=True, stop=True).then_inc(nd_done, 1)
                        if t >= 1:
                            down(t - 1)
                        if half == 0 and t == 2:
                            transposes(b * 2 + 2, 0)
                        if half == 1 and t == 2:
                            pe.wait_ge(xt_ready, b * 2 + 3)
                            y_back(b * 2 + 1, 0)
                    down(PAIRS - 1)
            y_back(GROUPS, 1)


def attention_rows(nc, C, tag, hd, q_stacks, k_stacks, products, table, v_at, ctx_at=None, out_dram=None):
    HEADS = 64
    U = SEQ // P
    with ExitStack() as ctx:
        def sb(name, shape, dt=F32):
            return ctx.enter_context(nc.sbuf_tensor(f"{tag}_{name}", shape, dt))

        def pb(name, shape, dt=F32):
            return ctx.enter_context(nc.psum_tensor(f"{tag}_{name}", shape, dt))

        sem = semaphores(nc, ctx, tag)

        qs = [sb(f"qs{i}", [s["rows"], 2, SEQ], BF16) for i, s in enumerate(q_stacks)]
        ks = [s["resident"] if "resident" in s else sb(f"ks{i}", [s["rows"], 2, SEQ], BF16) for i, s in enumerate(k_stacks)]
        tab = sb("tab", [P, 2, SEQ])
        vh = sb("vh", [P, 2, U, hd])
        sg = sb("sg", [P, 4, SEQ])
        mn = sb("mn", [P, 4])
        den = sb("den", [P, 2, U])
        rd = sb("rd", [P, U])
        pT = sb("pT", [P, 2, SEQ])
        co = sb("co", [P, U, 2, hd]) if out_dram is not None else None
        pS = [pb(f"pS{i}", [P, SEQ]) for i in range(2)]
        pX = [pb(f"pX{i}", [P, GROUP]) for i in range(2)]
        pO = [pb(f"pO{i}", [P, GROUP]) for i in range(2)]

        waited = sem("waited")
        const_in, loaded, v_ready = sem("const_in"), [sem("loaded0"), sem("loaded1")], sem("v_ready")
        s_done, m_done, e_done, t_done = sem("s_done"), sem("m_done"), sem("e_done"), sem("t_done")
        x_act, x_dve, pv_done, rd_ready, norm_done, sent = (sem(n) for n in
                                                    ("x_act", "x_dve", "pv_done", "rd_ready", "norm_done", "sent"))

        width = [SEQ - u * P for u in range(U)]
        chunks, first_chunk = [], []
        for u in range(U):
            first_chunk.append(len(chunks))
            for lo in range(0, width[u], GROUP):
                chunks.append((u, lo, min(GROUP, width[u] - lo)))
        by_act = {(0, 0), (1, 0), (2, 0), (3, 0), (5, 0)}
        NC = len(chunks)
        owner = ["act" if (u, lo) in by_act else "dve" for u, lo, _ in chunks]
        per = {e: owner.count(e) for e in ("act", "dve")}

        def copied(eng, head, c):
            if c < 0:
                head, c = head - 1, c + NC
            e = owner[c]
            eng.wait_ge(x_act if e == "act" else x_dve, head * per[e] + owner[:c + 1].count(e))

        def place(s):
            return s // U, s % U

        block = ctx.enter_context(nc.Block())
        NL = sum(len(s["loads"](0)) for s in q_stacks + k_stacks if "loads" in s) + 1
        consts = []
        for t, s in list(zip(qs, q_stacks)) + list(zip(ks, k_stacks)):
            for lo, n, src in s.get("consts", []):
                consts += [(t[lo:lo + n, i, :], src) for i in (0, 1)]

        @block.sync
        def _(sp):
            for dst, src in consts:
                sp.dma_start(dst, src).then_inc(const_in, 16)

            def load(bh, par):
                for t, s in list(zip(qs, q_stacks)) + list(zip(ks, k_stacks)):
                    for lo, n, src in s["loads"](bh) if "loads" in s else []:
                        sp.dma_start(t[lo:lo + n, par, :], src).then_inc(loaded[par], 16)
                sp.dma_start(tab[:, par, :], table(bh)).then_inc(loaded[par], 16)

            def store(pair):
                sp.wait_ge(norm_done, pair * 2 + 4)
                sp.dma_start(out_dram(pair), co[:].rearrange("p u i d -> p (u i d)")).then_inc(sent, 16)

            load(0, 0)
            load(1, 1)
            with sp.Fori(1, HEADS // 2) as it:
                for par in (0, 1):
                    bh = it * 2 + par
                    sp.wait_ge(m_done, (bh - 1) * U)
                    load(bh, par)
                if out_dram is not None:
                    store(it - 1)
            sp.wait_ge(m_done, (HEADS - 1) * U)
            load(HEADS, 0)
            if out_dram is not None:
                store(HEADS // 2 - 1)
                sp.wait_ge(sent, (HEADS // 2 + 1) * 16)

        @block.gpsimd
        def _(pool):
            def v_copy(bh, par):
                nc.gpsimd.tensor_copy(vh[:, par, :, :], v_at(bh)).then_inc(v_ready, 1)

            v_copy(0, 0)
            v_copy(1, 1)
            with pool.Fori(1, HEADS // 2) as it:
                for par in (0, 1):
                    bh = it * 2 + par
                    pool.wait_ge(pv_done, bh * U - U)
                    v_copy(bh, par)

        @block.tensor
        def _(pe):
            if consts:
                pe.wait_ge(const_in, 16 * len(consts))
            pe.sem_inc(norm_done, 2)

            def scores(bh, par, u, slot, free=None):
                if u == 0:
                    pe.wait_ge(loaded[par], ((bh - par) // 2 + 1) * 16 * NL if isinstance(bh, int)
                               else (bh + (2 - par)) * (8 * NL))
                if free is not None:
                    pe.wait_ge(m_done, free)
                lo = (U - 1 - u) * P
                for c in range(0, width[u], GROUP):
                    w = min(GROUP, width[u] - c)
                    for i, (q, k) in enumerate(products):
                        rhs = (ks[k][:, bass.ds(bh // 16 * SEQ + c, w)] if "resident" in k_stacks[k]
                               else ks[k][:, par, c:c + w])
                        ins = nc.tensor.matmul(pS[slot][:, c:c + w], qs[q][:, par, lo:lo + P], rhs,
                                               start=(i == 0), stop=(i == len(products) - 1))
                ins.then_inc(s_done, 1)

            def turn(bh, u, n, first=False):
                pe.wait_ge(e_done, n + 1)
                for c, (cu, lo, w) in enumerate(chunks):
                    if cu != u:
                        continue
                    if not (first and c < 2):
                        copied(pe, bh, c - 2)
                    for a in range(lo, lo + w, P):
                        ins = nc.tensor.transpose(pX[c % 2][:, a - lo:a - lo + P], sg[:, u % 4, a:a + P], C["ident"][:])
                    ins.then_inc(t_done, 1)

            def weigh(bh, par, u):
                if u == 0:
                    pe.wait_ge(v_ready, bh + 1)
                    pe.wait_ge(norm_done, bh + 1)
                for c, (cu, lo, w) in enumerate(chunks):
                    if cu != u:
                        continue
                    copied(pe, bh, c)
                    for a in range(lo, lo + w, P):
                        ins = nc.tensor.matmul(pO[par][:, (U - 1 - u) * hd:(U - u) * hd], pT[:, u % 2, a:a + P],
                                               vh[:, par, a // P, :], start=(u == 0 and a == 0),
                                               stop=(a + P == width[u]), skip_group_check=True)
                ins.then_inc(pv_done, 1)

            scores(0, 0, 0, 0)
            scores(0, 0, 1, 1)
            scores(0, 0, 2, 0, free=1)
            turn(0, 0, 0, first=True)
            with pe.Fori(0, HEADS // 2) as it:
                for s in range(2 * U):
                    n = it * (2 * U) + s
                    h3, u3 = place(s + 3)
                    scores(it * 2 + h3, h3 % 2, u3, (s + 3) % 2, free=n + 2)
                    h1, u1 = place(s + 1)
                    turn(it * 2 + h1, u1, n + 1)
                    h0, u0 = place(s)
                    weigh(it * 2 + h0, h0, u0)

        def copies(eng, name, bh, u, out_sem, copy):
            for c, (cu, lo, w) in enumerate(chunks):
                if cu == u and owner[c] == name:
                    eng.wait_ge(t_done, bh * NC + c + 1)
                    copy(pT[:, u % 2, lo:lo + w], pX[c % 2][:, 0:w]).then_inc(out_sem, 1)

        @block.vector
        def _(dve):
            def add_min(par, u, n):
                dve.wait_ge(s_done, n + 1)
                dve.sem_inc(waited, 1)
                w = width[u]
                nc.vector.tensor_tensor_reduce(sg[:, u % 4, 0:w], pS[u % 2][:, 0:w], tab[:, par, SEQ - w:SEQ], 1.0, 3e38,
                                               ALU.add, ALU.min, mn[:, u % 4:u % 4 + 1]).then_inc(m_done, 1)

            def norm(bh, par):
                dve.wait_ge(pv_done, (bh + 1) * U)
                nc.vector.reciprocal(rd[:], den[:, par, :]).then_inc(rd_ready, 1)
                dve.wait_ge(rd_ready, bh + 1)
                if out_dram is not None and par == 0:
                    dve.wait_ge(sent, (bh // 2 + 1) * 16)
                nc.vector.tensor_tensor(ctx_at(bh) if co is None else co[:, :, par, :],
                                        pO[par][:, 0:U * hd].rearrange("p (u d) -> p u d", d=hd),
                                        bcast(rd[:], hd), ALU.mult).then_inc(norm_done, 1)

            if out_dram is not None:
                dve.sem_inc(sent, 16)
            dve.wait_ge(loaded[0], 16 * NL)
            add_min(0, 0, 0)
            add_min(0, 1, 1)
            copies(dve, "dve", 0, 0, x_dve, nc.vector.tensor_copy)
            with dve.Fori(0, HEADS // 2) as it:
                for s in range(2 * U):
                    n = it * (2 * U) + s
                    h2, u2 = place(s + 2)
                    if u2 == 0:
                        dve.wait_ge(loaded[h2 % 2], (it * 2 + h2 + (2 - h2 % 2)) * (8 * NL))
                    add_min(h2 % 2, u2, n + 2)
                    h1, u1 = place(s + 1)
                    copies(dve, "dve", it * 2 + h1, u1, x_dve, nc.vector.tensor_copy)
                    if s % U == U - 1:
                        norm(it * 2 + s // U, s // U)

        @block.scalar
        def _(act):
            def exps(bh, par, u, n):
                act.wait_ge(m_done, n + 1)
                if u == 0 and not isinstance(bh, int):
                    act.wait_ge(norm_done, bh + 1)
                w = width[u]
                nc.scalar.activation(sg[:, u % 4, 0:w], sg[:, u % 4, 0:w], ACT.Exp, bias=mn[:, u % 4:u % 4 + 1],
                                     scale=-1.0, accum_out=den[:, par, U - 1 - u:U - u]).then_inc(e_done, 1)

            def copy(dst, src):
                return nc.scalar.activation(dst, src, ACT.Copy)

            exps(0, 0, 0, 0)
            exps(0, 0, 1, 1)
            copies(act, "act", 0, 0, x_act, copy)
            with act.Fori(0, HEADS // 2) as it:
                for s in range(2 * U):
                    h1, u1 = place(s + 1)
                    copies(act, "act", it * 2 + h1, u1, x_act, copy)
                    h2, u2 = place(s + 2)
                    exps(it * 2 + h2, h2 % 2, u2, it * (2 * U) + s + 2)


def l0_attn_a(nc, D, x, C, tag, out=None):
    with ExitStack() as ctx:
        h0 = ctx.enter_context(nc.sbuf_tensor(f"{tag}_h0", [P, BLOCKS, DIM], F32))
        attn = ctx.enter_context(nc.sbuf_tensor(f"{tag}_ctx", [P, SEQ // P, BATCH * DIM], F32))
        with ExitStack() as inner:
            v_all = inner.enter_context(nc.sbuf_tensor(f"{tag}_v", [P, SEQ // P, BATCH * DIM], F32))
            pooled = inner.enter_context(nc.sbuf_tensor(f"{tag}_pooled", [P, BATCH], F32))
            NPOS = 6
            qd, kd = (nc.dram_tensor(f"{tag}_{n}", (BATCH + 1, NPOS, P, SEQ), BF16, kind="Internal").ap() for n in ("qd", "kd"))
            qm, km = (nc.dram_tensor(f"{tag}_{n}", (BATCH + 1, 3, 16, SEQ), BF16, kind="Internal").ap() for n in ("qm", "km"))
            table = nc.dram_tensor(f"{tag}_table", (65, SEQ + P), F32, kind="Internal").ap()
            mods = [nc.dram_tensor(f"{tag}_mods{n}", (BATCH, n), F32, kind="Internal").ap() for n in (256, 128)]
            l0a_project(nc, D, x, C, f"{tag}p", h0, v_all, pooled, qd, kd, qm, km)
            l0a_table(nc, D, C, f"{tag}t", pooled, mods, table)

            def dots(dram):
                return lambda bh: [(0, NPOS * 8, dram[bass.ds(bh // 16, 1), :, bass.ds(bh % 16 * 8, 8), :]
                                    .rearrange("o s c t -> (o s) c t"))]

            def singles(dram, lo):
                return lambda bh: [(lo, 3, dram[bass.ds(bh // 16, 1), :, bass.ds(bh % 16, 1), :]
                                    .rearrange("o s c t -> (o s c) t"))]

            qd_at, kd_at = dots(qd), dots(kd)
            qm_at, km_at = singles(qm, 48), singles(km, 51)
            attention_rows(
                nc, C, f"{tag}a", 8,
                q_stacks=[dict(rows=54, loads=lambda bh: qd_at(bh) + qm_at(bh), consts=[(51, 3, D["minus_ones"])])],
                k_stacks=[dict(rows=54, loads=lambda bh: kd_at(bh) + km_at(bh), consts=[(48, 3, D["ones"])])],
                products=[(0, 0)],
                table=lambda bh: bass.AP(table.tensor, bh * (SEQ + P), [[1, P], [1, SEQ]]),
                v_at=lambda bh: v_all[:, :, bass.ds(bh * 8, 8)],
                ctx_at=lambda bh: attn[:, :, bass.ds(bh * 8, 8)])
        l0a_output(nc, D, x, C, f"{tag}o", h0, attn, out)


def l0a_project(nc, D, x, C, tag, h0, v_all, pooled, qd, kd, qm, km):
    SCALE = -0.15 / 8 ** 0.5
    Q_PART, K_PART = (0, 1, 0, 1, 0, 2), (0, 0, 1, 1, 2, 0)
    with ExitStack() as ctx:
        def sb(name, shape, dt=F32):
            return ctx.enter_context(nc.sbuf_tensor(f"{tag}_{name}", shape, dt))

        def pb(name, shape, dt=F32):
            return ctx.enter_context(nc.psum_tensor(f"{tag}_{name}", shape, dt))

        sem = semaphores(nc, ctx, tag)

        S = ln_scratch(sb)
        cq, ck, vw = sb("cq", [P, P]), sb("ck", [P, P]), sb("vw", [P, DIM])
        qmw, kmw = sb("qmw", [P, 32]), sb("kmw", [P, 32])
        mb, msign = sb("mb", [32, 1]), sb("msign", [32, 1])
        vb = sb("vb", [P, DIM])
        xn = sb("xn", [P, 2, GROUP_BLOCKS, DIM])
        xt, xr = sb("xt", [P, 2, GROUP]), sb("xr", [P, 2, GROUP])
        total = sb("total", [P, 2])
        f = {n: sb(f"f{n}", [rows, GROUP]) for n, rows in (("q", P), ("k", P), ("m", 32))}
        part = {n: sb(f"part{n}", [rows, 2, 3, GROUP], BF16) for n, rows in (("q", P), ("k", P), ("m", 32))}
        pT, pR, pQ, pK, pM, pV = (pb(n, [P, GROUP]) for n in ("pT", "pR", "pQ", "pK", "pM", "pV"))
        src = {"q": pQ, "k": pK, "m": f["m"]}

        w_in, zeroed = sem("weights_in"), sem("zeroed")
        ln_step, ln_ve, ln_rough = sem("ln_step"), sem("ln_ve"), sem("ln_rough")
        xn_ready, xT_done, xt_ready, h0_ready = sem("xn_ready"), sem("xT_done"), sem("xt_ready"), sem("h0_ready")
        done = {n: sem(f"{n}_done") for n in "qkmv"}
        hi, rest, mid, low = ({n: sem(f"{n}_{w}") for n in "qkm"} for w in ("hi", "rest", "mid", "low"))
        m_ready, v_ready, total_ready, sent = sem("m_ready"), sem("v_ready"), sem("total_ready"), [sem("sent0"), sem("sent1")]
        NW = 8

        block = ctx.enter_context(nc.Block())
        SENDS = 2 * len(Q_PART) + 6

        @block.sync
        def _(sp):
            for dst, name in ((cq, "cq_w"), (ck, "ck_w"), (vw, "v_w"), (qmw, "qmw32"), (kmw, "kmw32"), (mb, "mb32")):
                sp.dma_start(dst[:], D[f"L0_attn_a_{name}"]).then_inc(w_in, 16)
            sp.dma_start(msign[:], D["msign"]).then_inc(w_in, 16)
            sp.dma_start(vb[:], D["L0_attn_a_v_b"].broadcast_to([P, DIM])).then_inc(w_in, 16)
            for d in (qd, kd):
                sp.dma_start(d[BATCH, :, 0:8, :], D["zeros"][0:48, :].rearrange("(s c) t -> s c t", c=8)).then_inc(zeroed, 16)
            for d in (qm, km):
                sp.dma_start(d[BATCH, :, 0, :], D["zeros"][0:3, :]).then_inc(zeroed, 16)
            with sp.Fori(0, BATCH) as b:
                for par in (0, 1):
                    g = b * 2 + par
                    t = slice(par * GROUP, (par + 1) * GROUP)
                    sp.wait_ge(low["q"], g + 1)
                    for pos, p in enumerate(Q_PART):
                        sp.dma_start(qd[bass.ds(b, 1), pos, :, t].rearrange("o p t -> (o p) t"),
                                     part["q"][:, par, p, :]).then_inc(sent[par], 16)
                    sp.wait_ge(low["k"], g + 1)
                    for pos, p in enumerate(K_PART):
                        sp.dma_start(kd[bass.ds(b, 1), pos, :, t].rearrange("o p t -> (o p) t"),
                                     part["k"][:, par, p, :]).then_inc(sent[par], 16)
                    sp.wait_ge(low["m"], g + 2)
                    for p in range(3):
                        sp.dma_start(qm[bass.ds(b, 1), p, :, t].rearrange("o p t -> (o p) t"),
                                     part["m"][0:16, par, p, :]).then_inc(sent[par], 16)
                        sp.dma_start(km[bass.ds(b, 1), p, :, t].rearrange("o p t -> (o p) t"),
                                     part["m"][16:32, par, p, :]).then_inc(sent[par], 16)
            for par in (0, 1):
                sp.wait_ge(sent[par], 16 * SENDS * (BATCH + 1))
            sp.wait_ge(zeroed, 64)

        @block.gpsimd
        def _(pool):
            def powers(turn):
                pool.wait_ge(ln_ve, turn + 1)
                nc.gpsimd.tensor_tensor(S["y"][:], S["ve"][:], C["mhalf"][:, 0:GROUP_BLOCKS], ALU.pow).then_inc(ln_rough, 1)

            with pool.Fori(0, BATCH) as b:
                for par in (0, 1):
                    powers(b * 2 + par)
                    pool.wait_ge(xn_ready, b * 2 + par + 1)
                    nc.gpsimd.tensor_copy(h0[:, bass.ds((b * 2 + par) * GROUP_BLOCKS, GROUP_BLOCKS), :],
                                          xn[:, par, :, :]).then_inc(h0_ready, 1)

        @block.vector
        def _(dve):
            def split(n, g, par):
                dve.wait_ge(hi[n], g + 1)
                if n == "q":
                    nc.vector.scalar_tensor_tensor(f[n][:], src[n][:], SCALE, part[n][:, par, 0, :], ALU.mult,
                                                   ALU.subtract).then_inc(rest[n], 1)
                else:
                    nc.vector.tensor_tensor(f[n][:], src[n][:], part[n][:, par, 0, :], ALU.subtract).then_inc(rest[n], 1)

            def split_low(n, g, par):
                dve.wait_ge(mid[n], g + 1)
                nc.vector.tensor_tensor(part[n][:, par, 2, :], f[n][:], part[n][:, par, 1, :], ALU.subtract).then_inc(low[n], 1)

            for par in (0, 1):
                dve.sem_inc(sent[par], 16 * SENDS)
            dve.wait_ge(w_in, 16 * NW)
            with dve.Fori(0, BATCH) as b:
                for par in (0, 1):
                    g = b * 2 + par
                    steps = Steps(dve, ln_step, LN_STEPS, g)
                    dve.wait_ge(h0_ready, g + 1)
                    dve.wait_ge(xT_done, g + 1)
                    ln_group_vector(nc, dve, lambda k: x[:, bass.ds((g + 1) * GROUP_BLOCKS + k, 1), :], xn[:, par], S, steps,
                                    ln_rough, g + 1, ln_ve).then_inc(xn_ready, 1)
                    steps.close()
                    dve.wait_ge(done["m"], g + 1)
                    dve.wait_ge(low["m"], g + 1)
                    nc.vector.tensor_scalar(f["m"][:], pM[0:32, :], mb[:, 0:1], msign[:, 0:1], ALU.add, ALU.mult).then_inc(m_ready, 1)
                    split("q", g, par)
                    split("k", g, par)
                    dve.wait_ge(done["v"], g + 1)
                    nc.vector.tensor_tensor(v_all[:, par * GROUP_BLOCKS:(par + 1) * GROUP_BLOCKS, bass.ds(b * DIM, DIM)],
                                            pV[:].rearrange("p (k d) -> p k d", d=DIM),
                                            vb[:].unsqueeze(1).broadcast_to([P, GROUP_BLOCKS, DIM]), ALU.add).then_inc(v_ready, 1)
                    split("m", g, par)
                    for n in "qkm":
                        split_low(n, g, par)
                dve.wait_ge(total_ready, b * 2 + 2)
                nc.vector.tensor_tensor(pooled[:, bass.ds(b, 1)], total[:, 0:1], total[:, 1:2], ALU.add).then_inc(v_ready, 1)

        @block.scalar
        def _(act):
            act.wait_ge(w_in, 16 * NW)
            with act.Fori(0, BATCH) as b:
                for par in (0, 1):
                    g = b * 2 + par
                    act.wait_ge(xT_done, g + 3)
                    if par == 0:
                        act.wait_ge(v_ready, b * 3 + 1)
                    nc.scalar.activation(xt[:, par, :], pT[:], ACT.Copy, accum_out=total[:, par:par + 1]).then_inc(total_ready, 1)
                    nc.scalar.activation(xr[:, par, :], pR[:], ACT.Copy).then_inc(xt_ready, 1)
                    act.wait_ge(sent[par], (b + 1) * (16 * SENDS))
                    for n, scale in (("q", SCALE), ("k", 1.0)):
                        act.wait_ge(done[n], g + 1)
                        nc.scalar.activation(part[n][:, par, 0, :], src[n][:], ACT.Copy, scale=scale).then_inc(hi[n], 1)
                    act.wait_ge(m_ready, g + 1)
                    nc.scalar.activation(part["m"][:, par, 0, :], f["m"][:], ACT.Copy).then_inc(hi["m"], 1)
                    for n in "qkm":
                        act.wait_ge(rest[n], g + 1)
                        nc.scalar.activation(part[n][:, par, 1, :], f[n][:], ACT.Copy).then_inc(mid[n], 1)

        @block.tensor
        def _(pe):
            pe.wait_ge(w_in, 16 * NW)
            pe.sem_inc(h0_ready, 2)
            pe.sem_inc(xT_done, 2)
            pe.sem_inc(low["m"], 1)
            pe.sem_inc(v_ready, 1)
            with pe.Fori(0, BATCH) as b:
                for par in (0, 1):
                    g = b * 2 + par
                    pe.wait_ge(xn_ready, g + 1)
                    for k in range(GROUP_BLOCKS):
                        nc.tensor.transpose(pT[:, k * P:(k + 1) * P], xn[:, par, k, :], C["ident"][:])
                    for k in range(GROUP_BLOCKS):
                        ins = nc.tensor.matmul(pR[:, k * P:(k + 1) * P], xn[:, par, k, :], C["flip"][:], start=True, stop=True)
                    ins.then_inc(xT_done, 1)
                    pe.wait_ge(xt_ready, g + 1)
                    pe.wait_ge(low["m"], g + 1)
                    nc.tensor.matmul(pM[0:32, :], qmw[:], xr[:, par, :], start=True, stop=False)
                    nc.tensor.matmul(pM[0:32, :], kmw[:], xt[:, par, :], start=False, stop=True).then_inc(done["m"], 1)
                    nc.tensor.matmul(pQ[:], cq[:], xr[:, par, :], start=True, stop=True).then_inc(done["q"], 1)
                    nc.tensor.matmul(pK[:], ck[:], xt[:, par, :], start=True, stop=True).then_inc(done["k"], 1)
                    for k in range(GROUP_BLOCKS):
                        ins = nc.tensor.matmul(pV[:, k * P:(k + 1) * P], xt[:, par, k * P:(k + 1) * P], vw[:], start=True, stop=True)
                    ins.then_inc(done["v"], 1)


def l0a_table(nc, D, C, tag, pooled, mods, table):
    H, M, W, R = 16, 16, 8, 8
    BH = BATCH * H
    ROUND = 1.5 * 2 ** 23
    TWO_PI = 6.283185
    with ExitStack() as ctx:
        def sb(name, shape, dt=F32):
            return ctx.enter_context(nc.sbuf_tensor(f"{tag}_{name}", shape, dt))

        def pb(name, shape, dt=F32):
            return ctx.enter_context(nc.psum_tensor(f"{tag}_{name}", shape, dt))

        sem = semaphores(nc, ctx, tag)

        fp = sb("fp", [3, H * P])
        pos = sb("pos", [3, SEQ])
        win = sb("win", [BH, SEQ])
        amps = sb("amps", [P, H])
        gmw = sb("gmw", [P, 384])
        gmb = sb("gmb", [BH, M + R])
        basis = sb("basis", [BH, R, M])
        spread = sb("spread", [M, P])
        pl = sb("pl", [P, BATCH])
        g4 = sb("g4", [BATCH, 384])
        gl = sb("gl", [BH, M + R])
        soft, hard, t16 = sb("soft", [BH, M]), sb("hard", [BH, M]), sb("t16", [BH, M])
        top, one, two = sb("top", [BH, 8]), sb("one", [BH, 1]), sb("two", [BH, 1])
        wT = sb("wT", [M, BH])
        L = sb("L", [P, H, BH])
        rn, fr = sb("rn", [P, 2, SEQ]), sb("fr", [P, 3, SEQ])
        sf, hd = sb("sf", [BH, SEQ]), sb("hd", [BH, SEQ])
        tb = sb("tb", [BH, SEQ + P])
        pU = [pb(f"pU{i}", [P, SEQ]) for i in range(2)]
        pN = pb("pN", [P, SEQ])
        pG, pW = pb("pG", [P, GROUP]), pb("pW", [P, GROUP])

        w_in, zero, pooled_in, g_done, g_out, g_back, g_in = (sem(n) for n in
            ("weights_in", "zero", "pooled_in", "g_done", "g_out", "g_back", "g_in"))
        st, e_in, e_out, wt_done, wt_in, wx_done, L_ready = (sem(n) for n in
            ("step", "e_in", "e_out", "wt_done", "wt_in", "wx_done", "L_ready"))
        u_done, f_step, f_ready, s_ready, n_done, sg_ready, t_ready, stored = (sem(n) for n in
            ("u_done", "f_step", "f_ready", "s_ready", "n_done", "sg_ready", "t_ready", "stored"))
        NW = 8

        block = ctx.enter_context(nc.Block())

        @block.sync
        def _(sp):
            for dst, name in ((fp, "L0_attn_a_fp"), (pos, "positions"), (win, "window"), (amps, "L0_attn_a_ampsT"),
                              (gmw, "L0_attn_a_gmw"), (gmb, "L0_attn_a_gmb"), (basis, "L0_attn_a_basis"), (spread, "spread")):
                sp.dma_start(dst[:], D[name]).then_inc(w_in, 16)
            sp.wait_ge(g_out, 1)
            sp.dma_start(mods[0], g4[:, 0:256]).then_inc(g_back, 16)
            sp.dma_start(mods[1], g4[:, 256:384]).then_inc(g_back, 16)
            sp.wait_ge(g_back, 32)
            sp.dma_start(gl[:, 0:M], mods[0].rearrange("b (h m) -> (b h) m", m=M)).then_inc(g_in, 16)
            sp.dma_start(gl[:, M:M + R], mods[1].rearrange("b (h r) -> (b h) r", r=R)).then_inc(g_in, 16)
            sp.wait_ge(t_ready, 2)
            sp.dma_start(table[0:BH, :], tb[:]).then_inc(stored, 16)
            sp.dma_start(table[BH:BH + 1, :], tb[0:1, :]).then_inc(stored, 16)
            sp.wait_ge(stored, 32)

        @block.gpsimd
        def _(pool):
            nc.gpsimd.memset(L[:], 0.0).then_inc(zero, 1)
            nc.gpsimd.memset(tb[:, SEQ:], 1e30).then_inc(t_ready, 1)

        @block.scalar
        def _(act):
            act.wait_ge(w_in, 16 * NW)
            nc.scalar.activation(pl[:], pooled[:], ACT.Copy, scale=1.0 / SEQ).then_inc(pooled_in, 1)
            act.wait_ge(g_done, 1)
            nc.scalar.activation(g4[:], pG[0:BATCH, 0:384], ACT.Copy).then_inc(g_out, 1)
            act.wait_ge(e_in, 1)
            nc.scalar.activation(soft[:], t16[:], ACT.Exp).then_inc(e_out, 1)
            act.wait_ge(wt_done, 1)
            nc.scalar.activation(wT[:], pG[0:M, 0:BH], ACT.Copy).then_inc(wt_in, 1)
            for h in range(H):
                act.wait_ge(f_ready, h + 1)
                nc.scalar.activation(fr[:, h % 3, :], fr[:, h % 3, :], ACT.Sin, scale=TWO_PI).then_inc(s_ready, 1)
            act.wait_ge(n_done, H)
            nc.scalar.activation(sf[:], pN[0:BH, :], ACT.Sigmoid, scale=6.0).then_inc(sg_ready, 1)

        @block.vector
        def _(dve):
            def reduce_range(h):
                dve.wait_ge(u_done, h + 1)
                nc.vector.tensor_scalar(rn[:, h % 2, :], pU[h % 2][:], ROUND, -ROUND, ALU.add, ALU.add).then_inc(f_step, 1)
                dve.wait_ge(f_step, h + 1)
                if h >= 3:
                    dve.wait_ge(n_done, h - 2)
                nc.vector.tensor_tensor(fr[:, h % 3, :], pU[h % 2][:], rn[:, h % 2, :], ALU.subtract).then_inc(f_ready, 1)

            steps = Steps(dve, st, 0, 0)
            dve.wait_ge(w_in, 16 * NW)
            reduce_range(0)
            reduce_range(1)
            dve.wait_ge(g_in, 32)
            steps.done(nc.vector.tensor_tensor(gl[:], gl[:], gmb[:], ALU.add))
            for r in range(R):
                steps.done(nc.vector.scalar_tensor_tensor(gl[:, 0:M], basis[:, r, :], gl[:, M + r:M + r + 1], gl[:, 0:M],
                                                          ALU.mult, ALU.add))
            steps.done(nc.vector.tensor_reduce(one[:], gl[:, 0:M], AX.X, ALU.max))
            nc.vector.tensor_scalar(t16[:], gl[:, 0:M], one[:, 0:1], None, ALU.subtract).then_inc(e_in, 1)
            dve.wait_ge(e_out, 1)
            steps.done(nc.vector.tensor_reduce(one[:], soft[:], AX.X, ALU.add))
            steps.done(nc.vector.reciprocal(two[:], one[:]))
            steps.done(nc.vector.tensor_scalar(soft[:], soft[:], two[:, 0:1], None, ALU.mult))
            steps.done(nc.vector.max(top[:], soft[:]))
            steps.done(nc.vector.tensor_scalar(hard[:], soft[:], top[:, 7:8], None, ALU.is_ge))
            steps.done(nc.vector.tensor_reduce(one[:], hard[:], AX.X, ALU.add))
            steps.done(nc.vector.tensor_scalar(one[:], one[:], 1e-8, None, ALU.add))
            steps.done(nc.vector.reciprocal(two[:], one[:]))
            steps.done(nc.vector.tensor_scalar(hard[:], hard[:], two[:, 0:1], None, ALU.mult))
            steps.done(nc.vector.tensor_tensor(soft[:], soft[:], hard[:], ALU.subtract))
            steps.done(nc.vector.tensor_tensor(soft[:], hard[:], soft[:], ALU.add))
            assert steps.k == 21
            dve.wait_ge(wx_done, 1)
            dve.wait_ge(zero, 1)
            diag = bass.AP(L[:].tensor, L[:].offset, [list(L[:].ap[0]), [BH + 1, H], [H, BATCH]])
            nc.vector.tensor_tensor(diag, pW[:, 0:BH].rearrange("p (b h) -> p h b", h=H), bcast(amps[:], BATCH),
                                    ALU.mult).then_inc(L_ready, 1)
            for h in range(2, H):
                reduce_range(h)
            dve.wait_ge(n_done, H)
            dve.wait_ge(sg_ready, 1)
            nc.vector.tensor_scalar(hd[:], pN[0:BH, :], 0.0, None, ALU.is_gt).then_inc(f_step, 1)
            dve.wait_ge(f_step, H + 1)
            nc.vector.tensor_tensor(sf[:], sf[:], hd[:], ALU.subtract).then_inc(f_step, 1)
            dve.wait_ge(f_step, H + 2)
            nc.vector.tensor_tensor(sf[:], hd[:], sf[:], ALU.add).then_inc(f_step, 1)
            dve.wait_ge(f_step, H + 3)
            nc.vector.tensor_tensor(tb[:, 0:SEQ], sf[:], win[:], ALU.mult).then_inc(t_ready, 1)

        @block.tensor
        def _(pe):
            def phases(h):
                if h >= 2:
                    pe.wait_ge(f_ready, h - 1)
                for c in (0, GROUP):
                    ins = nc.tensor.matmul(pU[h % 2][:, c:c + GROUP], fp[:, h * P:(h + 1) * P], pos[:, c:c + GROUP],
                                           start=True, stop=True)
                ins.then_inc(u_done, 1)

            pe.wait_ge(w_in, 16 * NW)
            phases(0)
            phases(1)
            pe.wait_ge(pooled_in, 1)
            nc.tensor.matmul(pG[0:BATCH, 0:384], pl[:], gmw[:], start=True, stop=True).then_inc(g_done, 1)
            pe.wait_ge(st, 21)
            nc.tensor.transpose(pG[0:M, 0:BH], soft[:], C["ident"][0:BH, 0:BH]).then_inc(wt_done, 1)
            pe.wait_ge(wt_in, 1)
            nc.tensor.matmul(pW[:, 0:BH], spread[:], wT[:], start=True, stop=True).then_inc(wx_done, 1)
            pe.wait_ge(L_ready, 1)
            for h in range(H):
                if h + 2 < H:
                    phases(h + 2)
                pe.wait_ge(s_ready, h + 1)
                for c in (0, GROUP):
                    ins = nc.tensor.matmul(pN[0:BH, c:c + GROUP], L[:, h, :], fr[:, h % 3, c:c + GROUP],
                                           start=(h == 0), stop=(h == H - 1))
                ins.then_inc(n_done, 1)


def l0a_output(nc, D, x, C, tag, h0, attn, out=None):
    FT = 4
    with ExitStack() as ctx:
        def sb(name, shape, dt=F32):
            return ctx.enter_context(nc.sbuf_tensor(f"{tag}_{name}", shape, dt))

        def pb(name, shape, dt=F32):
            return ctx.enter_context(nc.psum_tensor(f"{tag}_{name}", shape, dt))

        sem = semaphores(nc, ctx, tag)

        S = ln_scratch(sb)
        ow, w1, w2 = sb("ow", [P, DIM]), sb("w1", [P, FT * P]), sb("w2", [P, FT, DIM])
        ob, b1, b2 = sb("ob", [P, 1]), sb("b1", [P, FT]), sb("b2", [P, 1])
        g1, c1, g2, c2 = (sb(n, [P, DIM]) for n in ("g1", "c1", "g2", "c2"))
        B4 = [P, GROUP_BLOCKS, DIM]
        cg, r, h, u = sb("cg", [P, 2] + B4[1:]), sb("r", B4), sb("h", B4), sb("u", B4)
        cT, aT, hT, fT = (sb(n, [P, GROUP]) for n in ("cT", "aT", "hT", "fT"))
        hid = sb("hid", [P, FT, GROUP])
        pC, pA, pB, pH0, pH1, pF = (pb(n, [P, GROUP]) for n in ("pC", "pA", "pB", "pH0", "pH1", "pF"))
        pH = [pH0, pH1]
        w_in, ln_step, ln_ve, ln_rough, stored = (sem(n) for n in ("weights_in", "ln_step", "ln_ve", "ln_rough", "stored"))
        cg_ready, c_done, c_in, a_done, a_in, aB_done = (sem(n) for n in ("cg_ready", "c_done", "c_in", "a_done", "a_in", "aB_done"))
        h_ready, hT_done, hT_in, u_done, u_in, f_done, f_in, fB_done = (sem(n) for n in
            ("h_ready", "hT_done", "hT_in", "u_done", "u_in", "f_done", "f_in", "fB_done"))
        st, x_done = sem("step"), sem("x_done")
        NW = 10
        block = ctx.enter_context(nc.Block())

        @block.sync
        def _(sp):
            for dst, name in ((ow, "out_w"), (w1, "ffn_w1"), (ob, "out_b"), (b1, "ffn_b1"), (b2, "ffn_b2")):
                sp.dma_start(dst[:], D[f"L0_attn_a_{name}"]).then_inc(w_in, 16)
            sp.dma_start(w2[:], D["L0_attn_a_ffn_w2"].rearrange("(t p) n -> p t n", p=P)).then_inc(w_in, 16)
            for dst, name in ((g1, "ln1_g"), (c1, "ln1_b"), (g2, "ln2_g"), (c2, "ln2_b")):
                sp.dma_start(dst[:], D[f"L0_attn_a_{name}"].broadcast_to([P, DIM])).then_inc(w_in, 16)
            if out is not None:
                store_x(sp, out, x, x_done, stored)

        @block.gpsimd
        def _(pool):
            with pool.Fori(0, BATCH) as b:
                for par in (0, 1):
                    g = b * 2 + par
                    pool.wait_ge(c_done, g + 1)
                    nc.gpsimd.tensor_copy(cg[:, par, :, :], attn[:, par * GROUP_BLOCKS:(par + 1) * GROUP_BLOCKS,
                                                              bass.ds(b * DIM, DIM)]).then_inc(cg_ready, 1)
                    for i in (0, 1):
                        pool.wait_ge(ln_ve, g * 2 + i + 1)
                        nc.gpsimd.tensor_tensor(S["y"][:], S["ve"][:], C["mhalf"][:, 0:GROUP_BLOCKS],
                                                ALU.pow).then_inc(ln_rough, 1)

        @block.vector
        def _(dve):
            def spread(t):
                return t[:].unsqueeze(1).broadcast_to(B4)

            dve.wait_ge(w_in, 16 * NW)
            with dve.Fori(0, BATCH) as b:
                for par in (0, 1):
                    g = b * 2 + par
                    steps = Steps(dve, st, 7 + 2 * LN_STEPS, g)
                    xs = x[:, bass.ds((g + 1) * GROUP_BLOCKS, GROUP_BLOCKS), :]
                    dve.wait_ge(aB_done, g + 1)
                    steps.done(nc.vector.tensor_tensor(r[:], pB[:].rearrange("p (k d) -> p k d", d=DIM),
                                                       h0[:, bass.ds(g * GROUP_BLOCKS, GROUP_BLOCKS), :], ALU.add))
                    steps.done(ln_group_vector(nc, dve, lambda k: r[:, k, :], u, S, steps, ln_rough, g * 2 + 1, ln_ve))
                    steps.done(nc.vector.tensor_tensor(u[:], u[:], spread(g1), ALU.mult))
                    nc.vector.tensor_tensor(h[:], u[:], spread(c1), ALU.add).then_inc(h_ready, 1)
                    dve.wait_ge(fB_done, g + 1)
                    dve.wait_ge(h_ready, g + 1)
                    steps.done(nc.vector.tensor_tensor(r[:], pB[:].rearrange("p (k d) -> p k d", d=DIM), h[:], ALU.add))
                    steps.done(ln_group_vector(nc, dve, lambda k: r[:, k, :], u, S, steps, ln_rough, g * 2 + 2, ln_ve))
                    steps.done(nc.vector.tensor_tensor(u[:], u[:], spread(g2), ALU.mult))
                    steps.done(nc.vector.tensor_tensor(u[:], u[:], spread(c2), ALU.add))
                    nc.vector.tensor_tensor(xs, xs, u[:], ALU.add).then_inc(x_done, 1)
                    steps.close()

        @block.scalar
        def _(act):
            act.wait_ge(w_in, 16 * NW)
            with act.Fori(0, GROUPS) as g:
                act.wait_ge(c_done, g + 3)
                nc.scalar.activation(cT[:], pC[:], ACT.Copy).then_inc(c_in, 1)
                act.wait_ge(a_done, g + 1)
                nc.scalar.activation(aT[:], pA[:], ACT.Identity, bias=ob[:, 0:1]).then_inc(a_in, 1)
                act.wait_ge(hT_done, g + 1)
                nc.scalar.activation(hT[:], pC[:], ACT.Copy).then_inc(hT_in, 1)
                for t in range(FT):
                    act.wait_ge(u_done, g * FT + t + 1)
                    nc.scalar.activation(hid[:, t, :], pH[t % 2][:], ACT.Gelu, bias=b1[:, t:t + 1]).then_inc(u_in, 1)
                act.wait_ge(f_done, g + 1)
                nc.scalar.activation(fT[:], pF[:], ACT.Identity, bias=b2[:, 0:1]).then_inc(f_in, 1)

        @block.tensor
        def _(pe):
            pe.wait_ge(w_in, 16 * NW)
            pe.sem_inc(c_done, 2)
            pe.sem_inc(x_done, 2)
            with pe.Fori(0, BATCH) as b:
                for par in (0, 1):
                    g = b * 2 + par
                    pe.wait_ge(cg_ready, g + 1)
                    for k in range(GROUP_BLOCKS):
                        ins = nc.tensor.matmul(pC[:, k * P:(k + 1) * P], cg[:, par, k, :], C["flip"][:], start=True, stop=True)
                    ins.then_inc(c_done, 1)
                    pe.wait_ge(c_in, g + 1)
                    nc.tensor.matmul(pA[:], ow[:], cT[:], start=True, stop=True).then_inc(a_done, 1)
                    pe.wait_ge(a_in, g + 1)
                    for k in range(GROUP_BLOCKS):
                        ins = nc.tensor.transpose(pB[:, k * P:(k + 1) * P], aT[:, k * P:(k + 1) * P], C["ident"][:])
                    ins.then_inc(aB_done, 1)
                    pe.wait_ge(h_ready, g + 1)
                    for k in range(GROUP_BLOCKS):
                        ins = nc.tensor.transpose(pC[:, k * P:(k + 1) * P], h[:, k, :], C["ident"][:])
                    ins.then_inc(hT_done, 1)
                    pe.wait_ge(hT_in, g + 1)
                    for t in range(FT):
                        if t >= 2:
                            pe.wait_ge(u_in, g * FT + t - 1)
                        nc.tensor.matmul(pH[t % 2][:], w1[:, t * P:(t + 1) * P], hT[:], start=True, stop=True).then_inc(u_done, 1)
                    for t in range(FT):
                        pe.wait_ge(u_in, g * FT + t + 1)
                        ins = nc.tensor.matmul(pF[:], w2[:, t, :], hid[:, t, :], start=(t == 0), stop=(t == FT - 1))
                    ins.then_inc(f_done, 1)
                    pe.wait_ge(f_in, g + 1)
                    for k in range(GROUP_BLOCKS):
                        ins = nc.tensor.transpose(pB[:, k * P:(k + 1) * P], fT[:, k * P:(k + 1) * P], C["ident"][:])
                    ins.then_inc(fB_done, 1)


def l1_attn_b(nc, D, x, C, tag, out=None):
    HD = 64
    with ExitStack() as ctx:
        ks = [ctx.enter_context(nc.sbuf_tensor(f"{tag}_k{i}", [P, (BATCH + 1) * SEQ], BF16)) for i in range(3)]
        qd = nc.dram_tensor(f"{tag}_qd", (BATCH + 1, 3, 16 * HD, SEQ), BF16, kind="Internal").ap()
        cx = nc.dram_tensor(f"{tag}_ctx", (BATCH * 8, P, SEQ // P * 2 * HD), F32, kind="Internal").ap()
        table = nc.dram_tensor(f"{tag}_table", (16, SEQ + P), F32, kind="Internal").ap()
        with ExitStack() as inner:
            v_all = inner.enter_context(nc.sbuf_tensor(f"{tag}_v", [P, SEQ // P, BATCH * HD], F32))
            l1b_project(nc, D, x, C, f"{tag}p", v_all, ks, qd, table)

            def q_part(p):
                return lambda bh: (qd[bass.ds(bh // 16, 1), p, bass.ds(bh % 16 * HD, HD), :].rearrange("o c t -> (o c) t"))

            hi, mid, low = q_part(0), q_part(1), q_part(2)
            attention_rows(
                nc, C, f"{tag}a", HD,
                q_stacks=[dict(rows=P, loads=lambda bh: [(0, HD, hi(bh)), (HD, HD, mid(bh))]),
                          dict(rows=P, loads=lambda bh: [(0, HD, hi(bh)), (HD, HD, low(bh))])],
                k_stacks=[dict(rows=P, resident=k) for k in ks],
                products=[(0, 0), (0, 1), (1, 2)],
                table=lambda bh: bass.AP(table.tensor, bh % 16 * (SEQ + P), [[1, P], [1, SEQ]]),
                v_at=lambda bh: v_all[:, :, bass.ds(bh // 16 * HD, HD)],
                out_dram=lambda pair: cx[bass.ds(pair, 1), :, :].rearrange("o p e -> (o p) e"))
        l1b_output(nc, D, x, C, f"{tag}o", cx, out)


def l1b_project(nc, D, x, C, tag, v_all, ks, qd, table):
    HD, QT = 64, 8
    SCALE = -0.125
    with ExitStack() as ctx:
        def sb(name, shape, dt=F32):
            return ctx.enter_context(nc.sbuf_tensor(f"{tag}_{name}", shape, dt))

        def pb(name, shape, dt=F32):
            return ctx.enter_context(nc.psum_tensor(f"{tag}_{name}", shape, dt))

        sem = semaphores(nc, ctx, tag)

        S = ln_scratch(sb)
        wq, wk, wv = sb("wq", [P, QT * P]), sb("wk", [P, P]), sb("wv", [P, HD])
        rel, tb = sb("rel", [16, SEQ]), sb("tb", [16, SEQ + P])
        xn = sb("xn", [P, 2, GROUP_BLOCKS, DIM])
        xt, xr = sb("xt", [P, GROUP]), sb("xr", [P, GROUP])
        fk, fq = sb("fk", [P, GROUP]), sb("fq", [P, 2, GROUP])
        part = sb("part", [P, 2, 3, GROUP], BF16)
        pT, pR, pK, pV = (pb(n, [P, GROUP]) for n in ("pT", "pR", "pK", "pV"))
        pQ = [pb(f"pQ{i}", [P, GROUP]) for i in range(2)]

        w_in, zeroed, t_ready = sem("weights_in"), sem("zeroed"), sem("t_ready")
        ln_step, ln_ve, ln_rough = sem("ln_step"), sem("ln_ve"), sem("ln_rough")
        xn_ready, xT_done, xt_ready = sem("xn_ready"), sem("xT_done"), sem("xt_ready")
        k_copied = sem("k_copied")
        k_done, k_hi, k_rest, k_mid, k_low, v_done, v_ready = (sem(n) for n in
            ("k_done", "k_hi", "k_rest", "k_mid", "k_low", "v_done", "v_ready"))
        q_done, q_hi, q_rest, q_mid, q_low, sent = (sem(n) for n in
            ("q_done", "q_hi", "q_rest", "q_mid", "q_low", "sent0"))
        sent = [sent, sem("sent1")]
        NW = 4

        block = ctx.enter_context(nc.Block())

        @block.sync
        def _(sp):
            for dst, name in ((wk, "Wkk"), (wv, "Wv"), (rel, "rel_by_distance"), (wq, "Wq")):
                sp.dma_start(dst[:], D[f"L1_attn_b_{name}"]).then_inc(w_in, 16)
            for p in range(3):
                sp.dma_start(qd[BATCH, p, 0:HD, :], D["zeros"]).then_inc(zeroed, 16)
            sp.wait_ge(t_ready, 2)
            sp.dma_start(table, tb[:]).then_inc(zeroed, 16)
            with sp.Fori(0, BATCH) as b:
                for par in (0, 1):
                    for t in range(QT):
                        sp.wait_ge(q_low, (b * 2 + par) * QT + t + 1)
                        sp.dma_start(qd[bass.ds(b, 1), :, t * P:(t + 1) * P, par * GROUP:(par + 1) * GROUP]
                                     .rearrange("o s p t -> p (o s) t"), part[:, t % 2, :, :]).then_inc(sent[t % 2], 16)
            for i in (0, 1):
                sp.wait_ge(sent[i], 16 * (1 + GROUPS * QT // 2))
            sp.wait_ge(zeroed, 64)

        @block.gpsimd
        def _(pool):
            def powers(turn):
                pool.wait_ge(ln_ve, turn + 1)
                nc.gpsimd.tensor_tensor(S["y"][:], S["ve"][:], C["mhalf"][:, 0:GROUP_BLOCKS], ALU.pow).then_inc(ln_rough, 1)

            nc.gpsimd.memset(tb[:, SEQ:], 1e30).then_inc(t_ready, 1)
            for k in ks:
                nc.gpsimd.memset(k[:, BATCH * SEQ:], 0.0)
            powers(0)
            with pool.Fori(0, GROUPS) as g:
                pool.wait_ge(k_hi, g + 1)
                at = g * GROUP
                nc.gpsimd.tensor_copy(ks[2][HD:P, bass.ds(at, GROUP)], ks[0][HD:P, bass.ds(at, GROUP)]).then_inc(k_copied, 1)
                pool.wait_ge(k_copied, g + 1)
                powers(g + 1)

        @block.vector
        def _(dve):
            def layernorm(gn, par):
                steps = Steps(dve, ln_step, LN_STEPS, gn)
                dve.wait_ge(xT_done, gn + 1)
                ln_group_vector(nc, dve, lambda k: x[:, bass.ds((gn + 1) * GROUP_BLOCKS + k, 1), :], xn[:, par], S, steps,
                                ln_rough, gn + 1, ln_ve).then_inc(xn_ready, 1)
                steps.close()

            dve.wait_ge(w_in, 16 * NW)
            layernorm(0, 0)
            nc.vector.tensor_scalar(tb[:, 0:SEQ], rel[:], -8.0, None, ALU.mult).then_inc(t_ready, 1)
            with dve.Fori(0, BATCH) as b:
                for par in (0, 1):
                    g = b * 2 + par
                    at = g * GROUP
                    dve.wait_ge(k_hi, g + 1)
                    nc.vector.tensor_tensor(fk[:], pK[:], ks[0][:, bass.ds(at, GROUP)], ALU.subtract).then_inc(k_rest, 1)
                    dve.wait_ge(v_done, g + 1)
                    nc.vector.tensor_copy(v_all[:, par * GROUP_BLOCKS:(par + 1) * GROUP_BLOCKS, bass.ds(b * HD, HD)],
                                          pV[:, 0:GROUP_BLOCKS * HD].rearrange("p (k d) -> p k d", d=HD)).then_inc(v_ready, 1)
                    dve.wait_ge(k_mid, g + 1)
                    nc.vector.tensor_tensor(ks[2][0:HD, bass.ds(at, GROUP)], fk[0:HD, :], ks[1][0:HD, bass.ds(at, GROUP)],
                                            ALU.subtract).then_inc(k_low, 1)
                    for t in range(QT + 1):
                        n = g * QT + t
                        if t < QT:
                            dve.wait_ge(q_hi, n + 1)
                            nc.vector.scalar_tensor_tensor(fq[:, t % 2, :], pQ[t % 2][:], SCALE, part[:, t % 2, 0, :],
                                                           ALU.mult, ALU.subtract).then_inc(q_rest, 1)
                        if t == 4:
                            layernorm(g + 1, 1 - par)
                        if t >= 1:
                            dve.wait_ge(q_mid, n)
                            u = (t - 1) % 2
                            nc.vector.tensor_tensor(part[:, u, 2, :], fq[:, u, :], part[:, u, 1, :],
                                                    ALU.subtract).then_inc(q_low, 1)

        @block.scalar
        def _(act):
            def to_xt(gn):
                act.wait_ge(xT_done, gn + 3)
                nc.scalar.activation(xt[:], pT[:], ACT.Copy)
                nc.scalar.activation(xr[:], pR[:], ACT.Copy).then_inc(xt_ready, 1)

            act.wait_ge(w_in, 16 * NW)
            to_xt(0)
            with act.Fori(0, BATCH) as b:
                for par in (0, 1):
                    g = b * 2 + par
                    at = g * GROUP
                    act.wait_ge(k_done, g + 1)
                    nc.scalar.activation(ks[0][:, bass.ds(at, GROUP)], pK[:], ACT.Copy).then_inc(k_hi, 1)
                    act.wait_ge(k_rest, g + 1)
                    nc.scalar.activation(ks[1][:, bass.ds(at, GROUP)], fk[:], ACT.Copy).then_inc(k_mid, 1)
                    for t in range(QT + 1):
                        n = g * QT + t
                        if t < QT:
                            act.wait_ge(q_done, n + 1)
                            act.wait_ge(sent[t % 2], (g * (QT // 2) + t // 2 + 1) * 16)
                            nc.scalar.activation(part[:, t % 2, 0, :], pQ[t % 2][:], ACT.Copy, scale=SCALE).then_inc(q_hi, 1)
                        if t >= 1:
                            act.wait_ge(q_rest, n + 2)
                            u = (t - 1) % 2
                            nc.scalar.activation(part[:, u, 1, :], fq[:, u, :], ACT.Copy).then_inc(q_mid, 1)
                    to_xt(g + 1)

        @block.tensor
        def _(pe):
            def transposes(gn, par):
                pe.wait_ge(xn_ready, gn + 1)
                for k in range(GROUP_BLOCKS):
                    nc.tensor.transpose(pT[:, k * P:(k + 1) * P], xn[:, par, k, :], C["ident"][:])
                for k in range(GROUP_BLOCKS):
                    ins = nc.tensor.matmul(pR[:, k * P:(k + 1) * P], xn[:, par, k, :], C["flip"][:], start=True, stop=True)
                ins.then_inc(xT_done, 1)

            pe.wait_ge(w_in, 16 * NW)
            pe.sem_inc(xT_done, 2)
            pe.sem_inc(q_rest, 2)
            for i in (0, 1):
                pe.sem_inc(sent[i], 16)
            transposes(0, 0)
            with pe.Fori(0, BATCH) as b:
                for par in (0, 1):
                    g = b * 2 + par
                    pe.wait_ge(xt_ready, g + 1)
                    nc.tensor.matmul(pK[:], wk[:], xt[:], start=True, stop=True).then_inc(k_done, 1)
                    for k in range(GROUP_BLOCKS):
                        ins = nc.tensor.matmul(pV[:, k * HD:(k + 1) * HD], xt[:, k * P:(k + 1) * P], wv[:], start=True, stop=True)
                    ins.then_inc(v_done, 1)
                    for t in range(QT):
                        pe.wait_ge(q_rest, g * QT + t + 1)
                        nc.tensor.matmul(pQ[t % 2][:], wq[:, t * P:(t + 1) * P], xr[:], start=True, stop=True).then_inc(q_done, 1)
                    transposes(g + 1, 1 - par)


def l1b_output(nc, D, x, C, tag, cx, out=None):
    T = 8
    with ExitStack() as ctx:
        def sb(name, shape, dt=F32):
            return ctx.enter_context(nc.sbuf_tensor(f"{tag}_{name}", shape, dt))

        def pb(name, shape, dt=F32):
            return ctx.enter_context(nc.psum_tensor(f"{tag}_{name}", shape, dt))

        sem = semaphores(nc, ctx, tag)

        wo, bo = sb("wo", [P, T, DIM]), sb("bo", [P, DIM])
        cg = sb("cg", [P, 2, T, GROUP_BLOCKS, P])
        cT = sb("cT", [P, T, GROUP])
        yr = sb("yr", [P, GROUP])
        pC = [pb(f"pC{i}", [P, GROUP]) for i in range(4)]
        pY, pB = pb("pY", [P, GROUP]), pb("pB", [P, GROUP])
        w_in, stored, x_done = sem("weights_in"), sem("stored"), sem("x_done")
        cg_in, c_act, c_dve, c_done = [sem("cg_in0"), sem("cg_in1")], sem("c_act"), sem("c_dve"), sem("c_done")
        y_done, y_in, b_done = sem("y_done"), sem("y_in"), sem("b_done")
        block = ctx.enter_context(nc.Block())

        @block.sync
        def _(sp):
            sp.dma_start(wo[:], D["L1_attn_b_Wout"].rearrange("(t p) d -> p t d", p=P)).then_inc(w_in, 16)
            sp.dma_start(bo[:], D["L1_attn_b_bout"].broadcast_to([P, DIM])).then_inc(w_in, 16)
            with sp.Fori(0, BATCH) as b:
                for par in (0, 1):
                    sp.wait_ge(c_done, (b * 2 + par + 1) * T)
                    sp.dma_start(cg[:, par].rearrange("p t k e -> p t (k e)"),
                                 cx[bass.ds(b * T, T), :, par * GROUP_BLOCKS * P:(par + 1) * GROUP_BLOCKS * P]
                                 .rearrange("t p e -> p t e")).then_inc(cg_in[par], 16)
            if out is not None:
                store_x(sp, out, x, x_done, stored)

        @block.vector
        def _(dve):
            dve.wait_ge(w_in, 32)
            with dve.Fori(0, GROUPS) as g:
                for t in range(1, T, 2):
                    dve.wait_ge(c_done, (g + 2) * T + t + 1)
                    nc.vector.tensor_copy(cT[:, t, :], pC[t % 4][:]).then_inc(c_dve, 1)
                dve.wait_ge(y_done, g + 1)
                nc.vector.tensor_tensor(yr[:].rearrange("p (k d) -> p k d", d=DIM), pY[:].rearrange("p (k d) -> p k d", d=DIM),
                                        bo[:].unsqueeze(1).broadcast_to([P, GROUP_BLOCKS, DIM]), ALU.add).then_inc(y_in, 1)
                dve.wait_ge(b_done, g + 1)
                xs = x[:, bass.ds((g + 1) * GROUP_BLOCKS, GROUP_BLOCKS), :]
                nc.vector.tensor_tensor(xs, xs, pB[:].rearrange("p (k d) -> p k d", d=DIM), ALU.add).then_inc(x_done, 1)

        @block.scalar
        def _(act):
            with act.Fori(0, GROUPS) as g:
                for t in range(0, T, 2):
                    act.wait_ge(c_done, (g + 2) * T + t + 1)
                    nc.scalar.activation(cT[:, t, :], pC[t % 4][:], ACT.Copy).then_inc(c_act, 1)

        @block.tensor
        def _(pe):
            pe.wait_ge(w_in, 32)
            pe.sem_inc(c_done, 2 * T)
            pe.sem_inc(x_done, 2)
            pe.sem_inc(c_act, 2)
            pe.sem_inc(c_dve, 2)
            with pe.Fori(0, BATCH) as b:
                for par in (0, 1):
                    g = b * 2 + par
                    pe.wait_ge(cg_in[par], 16 * (b + 1))
                    for t in range(T):
                        pe.wait_ge((c_act, c_dve)[t % 2], g * (T // 2) + t // 2 + 1)
                        for k in range(GROUP_BLOCKS):
                            ins = nc.tensor.transpose(pC[t % 4][:, k * P:(k + 1) * P],
                                                      cg[:, par, t, k, :], C["ident"][:])
                        ins.then_inc(c_done, 1)
                    pe.wait_ge(c_act, (g + 1) * (T // 2) + 2)
                    pe.wait_ge(c_dve, (g + 1) * (T // 2) + 2)
                    for k in range(GROUP_BLOCKS):
                        for t in range(T):
                            ins = nc.tensor.matmul(pY[:, k * P:(k + 1) * P], cT[:, t, k * P:(k + 1) * P], wo[:, t, :],
                                                   start=(t == 0), stop=(t == T - 1))
                    ins.then_inc(y_done, 1)
                    pe.wait_ge(y_in, g + 1)
                    pe.wait_ge(x_done, g + 2)
                    nc.tensor.matmul(pB[:], C["flip"][:], yr[:], start=True, stop=True).then_inc(b_done, 1)


def l1_attn_a(nc, D, x, C, tag, out=None):
    with ExitStack() as ctx:
        attn = ctx.enter_context(nc.sbuf_tensor(f"{tag}_ctx", [P, SEQ // P, BATCH * DIM], F32))
        with ExitStack() as inner:
            v_all = inner.enter_context(nc.sbuf_tensor(f"{tag}_v", [P, SEQ // P, BATCH * DIM], F32))
            NPOS = 6
            dram = {n: nc.dram_tensor(f"{tag}_{n}", (BATCH + 1, NPOS, rows, SEQ), BF16, kind="Internal").ap()
                    for n, rows in (("qc", P), ("kc", P), ("qr", 64), ("kr", 4))}
            l1a_project(nc, D, x, C, f"{tag}p", v_all, dram)
            attention_columns(nc, D, C, f"{tag}a", dram, v_all, attn)
        l1a_output(nc, D, x, C, f"{tag}o", attn, out)


def l1a_project(nc, D, x, C, tag, v_all, dram):
    Q_PART, K_PART = (0, 1, 0, 1, 0, 2), (0, 0, 1, 1, 2, 0)
    R = 68
    with ExitStack() as ctx:
        def sb(name, shape, dt=F32):
            return ctx.enter_context(nc.sbuf_tensor(f"{tag}_{name}", shape, dt))

        def pb(name, shape, dt=F32):
            return ctx.enter_context(nc.psum_tensor(f"{tag}_{name}", shape, dt))

        sem = semaphores(nc, ctx, tag)

        S = ln_scratch(sb)
        wdq, wdkv = sb("wdq", [P, 32]), sb("wdkv", [P, 32])
        wuq, wuk, wuv = (sb(n, [32, P]) for n in ("wuq", "wuk", "wuv"))
        wqr, wkr = sb("wqr", [32, 2, R]), sb("wkr", [P, 2, R])
        cos, sin = sb("cos", [R, SEQ]), sb("sin", [R, SEQ])
        xn = sb("xn", [P, 2, GROUP_BLOCKS, DIM])
        xt = sb("xt", [P, GROUP])
        cq, ckv = sb("cq", [32, GROUP]), sb("ckv", [32, GROUP])
        t1, t2 = sb("t1", [R, GROUP]), sb("t2", [R, GROUP])
        f = {n: sb(f"f{n}", [rows, GROUP]) for n, rows in (("q", P), ("k", P), ("r", R))}
        part = {n: sb(f"part{n}", [rows, 2, 3, GROUP], BF16) for n, rows in (("q", P), ("k", P), ("r", R))}
        pT, pA, pB, pQ, pK, pR, pS, pV = (pb(n, [P, GROUP]) for n in ("pT", "pA", "pB", "pQ", "pK", "pR", "pS", "pV"))
        src = {"q": pQ, "k": pK, "r": f["r"]}

        w_in, zeroed = sem("weights_in"), sem("zeroed")
        ln_step, ln_ve, ln_rough = sem("ln_step"), sem("ln_ve"), sem("ln_rough")
        xn_ready, xT_done, xt_ready = sem("xn_ready"), sem("xT_done"), sem("xt_ready")
        lat_done, lat_in, rope = sem("lat_done"), sem("lat_in"), sem("rope")
        done = {n: sem(f"{n}_done") for n in "qkrv"}
        hi, rest, mid, low = ({n: sem(f"{n}_{w}") for n in "qkr"} for w in ("hi", "rest", "mid", "low"))
        r_ready, v_ready, sent = sem("r_ready"), sem("v_ready"), [sem("sent0"), sem("sent1")]
        NW = 9

        block = ctx.enter_context(nc.Block())
        SENDS = 4 * len(Q_PART)

        @block.sync
        def _(sp):
            for dst, name in ((wdq, "L1_attn_a_W_DQ"), (wdkv, "L1_attn_a_W_DKV"), (wuq, "L1_attn_a_W_UQ"),
                              (wuk, "L1_attn_a_W_UK"), (wuv, "L1_attn_a_W_UV"), (wqr, "L1_attn_a_W_QR2"),
                              (wkr, "L1_attn_a_W_KR2"), (cos, "rope_cos"), (sin, "rope_sin")):
                sp.dma_start(dst[:], D[name]).then_inc(w_in, 16)
            for n, rows in (("qc", 8), ("kc", 8), ("qr", 4), ("kr", 4)):
                sp.dma_start(dram[n][BATCH, :, 0:rows, :], D["zeros"][0:6 * rows, :].rearrange("(s c) t -> s c t", c=rows)).then_inc(zeroed, 16)
            with sp.Fori(0, BATCH) as b:
                for par in (0, 1):
                    g = b * 2 + par
                    t = slice(par * GROUP, (par + 1) * GROUP)

                    def send(name, pos, rows, p, lo, hi_):
                        sp.dma_start(dram[name][bass.ds(b, 1), pos, :, t].rearrange("o p t -> (o p) t"),
                                     part[rows][lo:hi_, par, p, :]).then_inc(sent[par], 16)

                    sp.wait_ge(low["q"], g + 1)
                    for pos, p in enumerate(Q_PART):
                        send("qc", pos, "q", p, 0, P)
                    sp.wait_ge(low["k"], g + 1)
                    for pos, p in enumerate(K_PART):
                        send("kc", pos, "k", p, 0, P)
                    sp.wait_ge(low["r"], g + 2)
                    for pos, p in enumerate(Q_PART):
                        send("qr", pos, "r", p, 0, 64)
                    for pos, p in enumerate(K_PART):
                        send("kr", pos, "r", p, 64, R)
            for par in (0, 1):
                sp.wait_ge(sent[par], 16 * SENDS * (BATCH + 1))
            sp.wait_ge(zeroed, 64)

        @block.gpsimd
        def _(pool):
            with pool.Fori(0, GROUPS) as g:
                pool.wait_ge(ln_ve, g + 1)
                nc.gpsimd.tensor_tensor(S["y"][:], S["ve"][:], C["mhalf"][:, 0:GROUP_BLOCKS], ALU.pow).then_inc(ln_rough, 1)

        @block.vector
        def _(dve):
            for par in (0, 1):
                dve.sem_inc(sent[par], 16 * SENDS)
            dve.wait_ge(w_in, 16 * NW)
            with dve.Fori(0, BATCH) as b:
                for par in (0, 1):
                    g = b * 2 + par
                    t = slice(par * GROUP, (par + 1) * GROUP)
                    steps = Steps(dve, ln_step, LN_STEPS, g)
                    dve.wait_ge(xT_done, g + 1)
                    ln_group_vector(nc, dve, lambda k: x[:, bass.ds((g + 1) * GROUP_BLOCKS + k, 1), :], xn[:, par], S, steps,
                                    ln_rough, g + 1, ln_ve).then_inc(xn_ready, 1)
                    steps.close()
                    dve.wait_ge(done["r"], g + 1)
                    dve.wait_ge(low["r"], g + 1)
                    nc.vector.tensor_tensor(t1[:], pR[0:R, :], cos[:, t], ALU.mult)
                    nc.vector.tensor_tensor(t2[:], pS[0:R, :], sin[:, t], ALU.mult).then_inc(rope, 1)
                    dve.wait_ge(rope, g + 1)
                    nc.vector.tensor_tensor(f["r"][:], t1[:], t2[:], ALU.add).then_inc(r_ready, 1)
                    for n in "qk":
                        dve.wait_ge(hi[n], g + 1)
                        nc.vector.tensor_tensor(f[n][:], src[n][:], part[n][:, par, 0, :], ALU.subtract).then_inc(rest[n], 1)
                    dve.wait_ge(done["v"], g + 1)
                    nc.vector.tensor_copy(v_all[:, par * GROUP_BLOCKS:(par + 1) * GROUP_BLOCKS, bass.ds(b * DIM, DIM)],
                                          pV[:].rearrange("p (k d) -> p k d", d=DIM)).then_inc(v_ready, 1)
                    dve.wait_ge(hi["r"], g + 1)
                    nc.vector.tensor_tensor(f["r"][:], f["r"][:], part["r"][:, par, 0, :], ALU.subtract).then_inc(rest["r"], 1)
                    for n in "qkr":
                        dve.wait_ge(mid[n], g + 1)
                        nc.vector.tensor_tensor(part[n][:, par, 2, :], f[n][:], part[n][:, par, 1, :], ALU.subtract).then_inc(low[n], 1)

        @block.scalar
        def _(act):
            act.wait_ge(w_in, 16 * NW)
            with act.Fori(0, BATCH) as b:
                for par in (0, 1):
                    g = b * 2 + par
                    act.wait_ge(xT_done, g + 3)
                    nc.scalar.activation(xt[:], pT[:], ACT.Copy).then_inc(xt_ready, 1)
                    act.wait_ge(lat_done, g + 1)
                    nc.scalar.activation(cq[:], pA[0:32, :], ACT.Copy)
                    nc.scalar.activation(ckv[:], pB[0:32, :], ACT.Copy).then_inc(lat_in, 1)
                    act.wait_ge(sent[par], (b + 1) * (16 * SENDS))
                    for n in "qk":
                        act.wait_ge(done[n], g + 1)
                        nc.scalar.activation(part[n][:, par, 0, :], src[n][:], ACT.Copy).then_inc(hi[n], 1)
                    act.wait_ge(r_ready, g + 1)
                    nc.scalar.activation(part["r"][:, par, 0, :], f["r"][:], ACT.Copy).then_inc(hi["r"], 1)
                    for n in "qkr":
                        act.wait_ge(rest[n], g + 1)
                        nc.scalar.activation(part[n][:, par, 1, :], f[n][:], ACT.Copy).then_inc(mid[n], 1)

        @block.tensor
        def _(pe):
            pe.wait_ge(w_in, 16 * NW)
            pe.sem_inc(xT_done, 2)
            pe.sem_inc(low["r"], 1)
            with pe.Fori(0, BATCH) as b:
                for par in (0, 1):
                    g = b * 2 + par
                    pe.wait_ge(xn_ready, g + 1)
                    for k in range(GROUP_BLOCKS):
                        ins = nc.tensor.transpose(pT[:, k * P:(k + 1) * P], xn[:, par, k, :], C["ident"][:])
                    ins.then_inc(xT_done, 1)
                    pe.wait_ge(xt_ready, g + 1)
                    nc.tensor.matmul(pA[0:32, :], wdq[:], xt[:], start=True, stop=True)
                    nc.tensor.matmul(pB[0:32, :], wdkv[:], xt[:], start=True, stop=True).then_inc(lat_done, 1)
                    pe.wait_ge(low["r"], g + 1)
                    pe.wait_ge(lat_in, g + 1)
                    for i, p in enumerate((pR, pS)):
                        nc.tensor.matmul(p[0:R, :], wqr[:, i, :], cq[:], start=True, stop=False)
                        ins = nc.tensor.matmul(p[0:R, :], wkr[:, i, :], xt[:], start=False, stop=True)
                    ins.then_inc(done["r"], 1)
                    nc.tensor.matmul(pQ[:], wuq[:], cq[:], start=True, stop=True).then_inc(done["q"], 1)
                    nc.tensor.matmul(pK[:], wuk[:], ckv[:], start=True, stop=True).then_inc(done["k"], 1)
                    for k in range(GROUP_BLOCKS):
                        ins = nc.tensor.matmul(pV[:, k * P:(k + 1) * P], ckv[:, k * P:(k + 1) * P], wuv[:], start=True, stop=True)
                    ins.then_inc(done["v"], 1)


def attention_columns(nc, D, C, tag, dram, v_all, attn):
    HEADS, HD, U, ROWS = 64, 8, SEQ // P, 72
    ROOT = 12 ** 0.5
    CLIP = 80.0
    with ExitStack() as ctx:
        def sb(name, shape, dt=F32):
            return ctx.enter_context(nc.sbuf_tensor(f"{tag}_{name}", shape, dt))

        def pb(name, shape, dt=F32):
            return ctx.enter_context(nc.psum_tensor(f"{tag}_{name}", shape, dt))

        sem = semaphores(nc, ctx, tag)

        qs, ks = sb("qs", [ROWS, 2, SEQ], BF16), sb("ks", [ROWS, 2, SEQ], BF16)
        ceiling = sb("ceiling", [P, P])
        vh = sb("vh", [P, 2, U, HD + 1])
        e = sb("e", [P, 4, SEQ])
        rd = sb("rd", [P, U])
        pS = [pb(f"pS{i}", [P, SEQ]) for i in range(2)]
        pO = [pb(f"pO{i}", [P, GROUP]) for i in range(2)]
        const_in, loaded, v_ready, ones_set = sem("const_in"), [sem("loaded0"), sem("loaded1")], sem("v_ready"), sem("ones_set")
        s_done, e_done, clipped, pv_done, rd_ready, norm_done = (sem(n) for n in
            ("s_done", "e_done", "clipped", "pv_done", "rd_ready", "norm_done"))
        width = [SEQ - u * P for u in range(U)]
        NL = 4
        block = ctx.enter_context(nc.Block())

        def place(s):
            return s // U, s % U

        @block.sync
        def _(sp):
            sp.dma_start(ceiling[:], D["causal_ceiling"]).then_inc(const_in, 16)

            def load(bh, par):
                for dst, lo, name, rows, h in ((qs, 0, "qc", 8, bh % 16 * 8), (ks, 0, "kc", 8, bh % 16 * 8),
                                               (qs, 48, "qr", 4, bh % 16 * 4), (ks, 48, "kr", 4, 0)):
                    src = dram[name][bass.ds(bh // 16, 1), :, bass.ds(h, rows), :]
                    sp.dma_start(dst[lo:lo + 6 * rows, par, :], src.rearrange("o s c t -> (o s) c t")).then_inc(loaded[par], 16)

            load(0, 0)
            load(1, 1)
            with sp.Fori(1, HEADS // 2) as it:
                for par in (0, 1):
                    bh = it * 2 + par
                    sp.wait_ge(s_done, (bh - 1) * U)
                    load(bh, par)
            sp.wait_ge(s_done, (HEADS - 1) * U)
            load(HEADS, 0)

        @block.gpsimd
        def _(pool):
            def v_copy(bh, par):
                nc.gpsimd.tensor_copy(vh[:, par, :, 0:HD], v_all[:, :, bass.ds(bh * HD, HD)]).then_inc(v_ready, 1)

            nc.gpsimd.memset(vh[:], 1.0).then_inc(ones_set, 1)
            pool.wait_ge(ones_set, 1)
            v_copy(0, 0)
            v_copy(1, 1)
            with pool.Fori(1, HEADS // 2) as it:
                for par in (0, 1):
                    bh = it * 2 + par
                    pool.wait_ge(pv_done, (bh - 1) * U + 4)
                    v_copy(bh, par)

        @block.tensor
        def _(pe):
            pe.sem_inc(norm_done, 2)
            pe.sem_inc(pv_done, 4)

            def scores(bh, par, u, slot, free=None):
                if u == 0:
                    pe.wait_ge(loaded[par], ((bh - par) // 2 + 1) * 16 * NL if isinstance(bh, int)
                               else (bh + (2 - par)) * (8 * NL))
                if free is not None:
                    pe.wait_ge(clipped, free)
                k = ks[:, par, u * P:(u + 1) * P]
                for a in range(0, width[u], GROUP):
                    z = min(a + GROUP, width[u])
                    ins = nc.tensor.matmul(pS[slot][:, a:z], k, qs[:, par, u * P + a:u * P + z], start=True, stop=True)
                ins.then_inc(s_done, 1)

            def weigh(bh, par, u, n):
                if u == 0:
                    pe.wait_ge(v_ready, bh + 1)
                    pe.wait_ge(norm_done, bh + 1)
                pe.wait_ge(e_done, n + 1)
                for i in range(u, U):
                    ins = nc.tensor.matmul(pO[par][:, i * (HD + 1):(i + 1) * (HD + 1)], e[:, u % 4, (i - u) * P:(i - u + 1) * P],
                                           vh[:, par, u, :], start=(u == 0 and i == 0), stop=(u == i), skip_group_check=True)
                ins.then_inc(pv_done, 1)

            scores(0, 0, 0, 0)
            scores(0, 0, 1, 1)
            scores(0, 0, 2, 0, free=1)
            with pe.Fori(0, HEADS // 2) as it:
                for s in range(2 * U):
                    n = it * (2 * U) + s
                    h3, u3 = place(s + 3)
                    scores(it * 2 + h3, h3 % 2, u3, (s + 3) % 2, free=n + 2)
                    h0, u0 = place(s)
                    weigh(it * 2 + h0, h0, u0, n)

        @block.scalar
        def _(act):
            def exps(u, n):
                act.wait_ge(clipped, n + 1)
                w = width[u]
                nc.scalar.activation(e[:, u % 4, 0:w], e[:, u % 4, 0:w], ACT.Exp, scale=1 / ROOT).then_inc(e_done, 1)

            with act.Fori(0, HEADS // 2) as it:
                for s in range(2 * U):
                    exps(s % U, it * (2 * U) + s)

        @block.vector
        def _(dve):
            def clip(u, n):
                dve.wait_ge(s_done, n + 1)
                dve.wait_ge(pv_done, n + 1)
                s, w = pS[u % 2], width[u]
                ins = nc.vector.scalar_tensor_tensor(e[:, u % 4, 0:P], s[:, 0:P], -CLIP, ceiling[:], ALU.max, ALU.min)
                if w > P:
                    ins = nc.vector.tensor_scalar(e[:, u % 4, P:w], s[:, P:w], -CLIP, CLIP, ALU.max, ALU.min)
                ins.then_inc(clipped, 1)

            def norm(bh, par):
                dve.wait_ge(pv_done, (bh + 1) * U + 4)
                o = pO[par][:, 0:U * (HD + 1)].rearrange("p (u d) -> p u d", d=HD + 1)
                nc.vector.reciprocal(rd[:], o[:, :, HD]).then_inc(rd_ready, 1)
                dve.wait_ge(rd_ready, bh + 1)
                nc.vector.tensor_tensor(attn[:, :, bass.ds(bh * HD, HD)], o[:, :, 0:HD], bcast(rd[:], HD),
                                        ALU.mult).then_inc(norm_done, 1)

            dve.wait_ge(const_in, 16)
            clip(0, 0)
            with dve.Fori(0, HEADS // 2) as it:
                for s in range(2 * U):
                    clip((s + 1) % U, it * (2 * U) + s + 1)
                    if s == U + 1:
                        norm(it * 2, 0)
                norm(it * 2 + 1, 1)


def l1a_output(nc, D, x, C, tag, attn, out=None):
    with ExitStack() as ctx:
        def sb(name, shape, dt=F32):
            return ctx.enter_context(nc.sbuf_tensor(f"{tag}_{name}", shape, dt))

        def pb(name, shape, dt=F32):
            return ctx.enter_context(nc.psum_tensor(f"{tag}_{name}", shape, dt))

        sem = semaphores(nc, ctx, tag)

        wo = sb("wo", [P, DIM])
        cg, cT = sb("cg", [P, 2, GROUP_BLOCKS, DIM]), sb("cT", [P, 2, GROUP])
        pC, pY = ([pb(f"{n}{i}", [P, GROUP]) for i in range(2)] for n in ("pC", "pY"))
        w_in, stored, x_done = sem("weights_in"), sem("stored"), sem("x_done")
        cg_ready, c_done, c_in, y_done = (sem(n) for n in ("cg_ready", "c_done", "c_in", "y_done"))
        block = ctx.enter_context(nc.Block())

        @block.sync
        def _(sp):
            sp.dma_start(wo[:], D["L1_attn_a_W_O"]).then_inc(w_in, 16)
            if out is not None:
                store_x(sp, out, x, x_done, stored)

        @block.gpsimd
        def _(pool):
            with pool.Fori(0, BATCH) as b:
                for par in (0, 1):
                    pool.wait_ge(c_done, b * 2 + par + 1)
                    nc.gpsimd.tensor_copy(cg[:, par, :, :], attn[:, par * GROUP_BLOCKS:(par + 1) * GROUP_BLOCKS,
                                                              bass.ds(b * DIM, DIM)]).then_inc(cg_ready, 1)

        @block.vector
        def _(dve):
            with dve.Fori(0, BATCH) as b:
                for par in (0, 1):
                    g = b * 2 + par
                    xs = x[:, bass.ds((g + 1) * GROUP_BLOCKS, GROUP_BLOCKS), :]
                    dve.wait_ge(y_done, g + 1)
                    nc.vector.tensor_tensor(xs, xs, pY[par][:].rearrange("p (k d) -> p k d", d=DIM), ALU.add).then_inc(x_done, 1)

        @block.scalar
        def _(act):
            with act.Fori(0, BATCH) as b:
                for par in (0, 1):
                    act.wait_ge(c_done, b * 2 + par + 3)
                    nc.scalar.activation(cT[:, par, :], pC[par][:], ACT.Copy).then_inc(c_in, 1)

        @block.tensor
        def _(pe):
            pe.wait_ge(w_in, 16)
            pe.sem_inc(c_done, 2)
            pe.sem_inc(x_done, 2)
            with pe.Fori(0, BATCH) as b:
                for par in (0, 1):
                    g = b * 2 + par
                    pe.wait_ge(cg_ready, g + 1)
                    for k in range(GROUP_BLOCKS):
                        ins = nc.tensor.transpose(pC[par][:, k * P:(k + 1) * P], cg[:, par, k, :], C["ident"][:])
                    ins.then_inc(c_done, 1)
                    pe.wait_ge(c_in, g + 1)
                    pe.wait_ge(x_done, g + 1)
                    for k in range(GROUP_BLOCKS):
                        ins = nc.tensor.matmul(pY[par][:, k * P:(k + 1) * P], cT[:, par, k * P:(k + 1) * P], wo[:], start=True, stop=True)
                    ins.then_inc(y_done, 1)


def build(nc, D, out):
    with ExitStack() as ctx:
        x = ctx.enter_context(nc.sbuf_tensor("x", [P, (GROUPS + 2) * GROUP_BLOCKS, DIM], F32))
        ident = ctx.enter_context(nc.sbuf_tensor("ident", [P, P], F32))
        mhalf = ctx.enter_context(nc.sbuf_tensor("minus_half", [P, 32], F32))
        loaded = ctx.enter_context(nc.semaphore("x_loaded"))
        ident16 = ctx.enter_context(nc.sbuf_tensor("ident16", [P, P], BF16))
        flip = ctx.enter_context(nc.sbuf_tensor("flip", [P, P], F32))
        C = dict(ident=ident, mhalf=mhalf, ident16=ident16, flip=flip)
        with nc.Block() as block:
            @block.sync
            def _(sp):
                sp.dma_start(ident[:], D["identity"]).then_inc(loaded, 16)
                sp.dma_start(ident16[:], D["identity16"]).then_inc(loaded, 16)
                sp.dma_start(flip[:], D["flip"]).then_inc(loaded, 16)
                sp.dma_start(x[:, GROUP_BLOCKS:GROUP_BLOCKS + BLOCKS, :],
                             D["x"].rearrange("(b p) d -> p b d", p=P)).then_inc(loaded, 16)
                sp.wait_ge(loaded, 66)

            @block.vector
            def _(dve):
                nc.vector.memset(x[:, 0:GROUP_BLOCKS, :], 0.0)
                nc.vector.memset(x[:, GROUP_BLOCKS + BLOCKS:, :], 0.0).then_inc(loaded, 1)
                nc.vector.memset(mhalf[:], -0.5).then_inc(loaded, 1)
        stages = STAGES.split(",")
        for n in stages:
            last = out if n == stages[-1] else None
            if n == "1":
                l0_attn_a(nc, D, x, C, "s1", last)
            if n == "3":
                l0_attn_b(nc, D, x, C, "s3", last)
            if n == "5":
                l1_attn_a(nc, D, x, C, "s5", last)
            if n == "7":
                l1_attn_b(nc, D, x, C, "s7", last)
            if n in "24":
                l0_ffn(nc, D, x, C, f"s{n}", last)
            if n in "68":
                l1_ffn(nc, D, x, C, f"s{n}", last)


def kernel(**inputs):
    import ml_dtypes
    import numpy as np
    import concourse.bacc as bacc
    from concourse.bass_utils import run_bass_kernel_spmd

    a = {k: np.asarray(v) for k, v in inputs.items()}
    bf16 = ml_dtypes.bfloat16
    distance = np.arange(SEQ - 1, -1, -1, dtype=np.float64)
    root = np.sign(distance) * np.sqrt(distance + 1e-6) / np.sqrt(SEQ)
    positions = (np.stack([distance / SEQ, root, np.ones(SEQ)]) / (2 * np.pi)).astype(np.float32)
    window = (-3.0 * np.exp(-distance ** 2 / (2.0 * (SEQ / 4.0) ** 2))).astype(np.float32)
    n = np.arange(SEQ - 1, -1, -1)
    bucket = np.where(n < 16, n, np.minimum(16 + (np.log(np.maximum(n, 1) / 16.0) / np.log(8.0) * 16).astype(np.int32), 31))
    pairs = np.arange(64) ^ 1
    wqr, wkr = a["L1_attn_a_W_QR"], a["L1_attn_a_W_KR"]
    angle = np.arange(SEQ, dtype=np.float32)[None, :] * (np.float32(10000) ** (-np.arange(0, 4, 2, dtype=np.float32) / 4))[:, None]
    cos = np.tile(np.repeat(np.cos(angle.astype(np.float64)), 2, 0), (17, 1)).astype(np.float32)
    sin = np.tile(np.repeat(np.sin(angle.astype(np.float64)), 2, 0) * np.array([[-1], [1], [-1], [1]]), (17, 1)).astype(np.float32)
    later = np.arange(P)[None, :] >= np.arange(P)[:, None]
    zero16 = np.zeros((DIM, 16), np.float32)
    arrays = {
        "x": a["L0_attn_a_x"].reshape(TOKENS, DIM),
        "identity": np.eye(P, dtype=np.float32),
        "flip": np.eye(P, dtype=np.float32)[::-1],
        "zeros": np.zeros((64, SEQ), bf16), "ones": np.ones((3, SEQ), bf16), "minus_ones": -np.ones((3, SEQ), bf16),
        "positions": positions, "window": np.broadcast_to(window, (64, SEQ)),
        "msign": np.repeat(np.float32([-1, 1]), 16).reshape(32, 1),
        "spread": np.kron(np.eye(16), np.ones((1, 8))).astype(np.float32),
        "L0_attn_a_cq_w": a["L0_attn_a_cq_w"], "L0_attn_a_ck_w": a["L0_attn_a_ck_w"], "L0_attn_a_v_w": a["L0_attn_a_v_w"],
        "L0_attn_a_qmw32": np.concatenate([a["L0_attn_a_qmod_w"], zero16], 1),
        "L0_attn_a_kmw32": np.concatenate([zero16, a["L0_attn_a_kmod_w"]], 1),
        "L0_attn_a_mb32": np.concatenate([a["L0_attn_a_qmod_b"], a["L0_attn_a_kmod_b"]]).reshape(32, 1),
        "L0_attn_a_v_b": a["L0_attn_a_v_b"].reshape(1, DIM),
        "L0_attn_a_fp": np.concatenate([a["L0_attn_a_freqs"].reshape(2048, 2).T, a["L0_attn_a_phases"].reshape(1, 2048)]),
        "L0_attn_a_ampsT": a["L0_attn_a_amps"].reshape(16, P).T,
        "L0_attn_a_gmw": np.concatenate([a["L0_attn_a_gate_w"], a["L0_attn_a_mod_w"]], 1),
        "L0_attn_a_gmb": np.tile(np.concatenate([a["L0_attn_a_gate_b"].reshape(16, 16),
                                                 a["L0_attn_a_mod_b"].reshape(16, 8)], 1), (BATCH, 1)),
        "L0_attn_a_basis": np.tile(a["L0_attn_a_mod_basis"].transpose(1, 0, 2), (BATCH, 1, 1)),
        "L0_attn_a_out_w": a["L0_attn_a_out_w"], "L0_attn_a_out_b": a["L0_attn_a_out_b"].reshape(DIM, 1),
        "L0_attn_a_ffn_w1": a["L0_attn_a_ffn_w1"], "L0_attn_a_ffn_b1": a["L0_attn_a_ffn_b1"].reshape(4, P).T,
        "L0_attn_a_ffn_w2": a["L0_attn_a_ffn_w2"], "L0_attn_a_ffn_b2": a["L0_attn_a_ffn_b2"].reshape(DIM, 1),
        **{f"L0_attn_a_{n}": a[f"L0_attn_a_{n}"].reshape(1, DIM) for n in ("ln1_g", "ln1_b", "ln2_g", "ln2_b")},
        "identity16": np.eye(P, dtype=bf16),
        "rank": np.arange(8, 0, -1, dtype=np.float32).reshape(1, 8),
        "sel24": np.ascontiguousarray(np.broadcast_to(np.tile(np.eye(8), (3, 1))[:, :, None], (24, 8, P))).astype(bf16),
        "L0_attn_b_W_f": a["L0_attn_b_W_f"],
        "L0_attn_b_WqkT": a["L0_attn_b_W_qkv"][:, :2048].T,
        "L0_attn_b_Wv": a["L0_attn_b_W_qkv"][:, 2048:],
        "L0_attn_b_W_out": a["L0_attn_b_W_out"],
        "L0_attn_b_b_out": a["L0_attn_b_b_out"].reshape(DIM, 1),
        "L0_attn_b_b_f2": np.concatenate([a["L0_attn_b_b_f"]] * 2).reshape(P, 1),
        "L0_attn_b_b_f": a["L0_attn_b_b_f"].reshape(1, 64),
        "L0_ffn_gate_wT": a["L0_ffn_gate_w"].T,
        "L0_ffn_lb_bias": a["L0_ffn_lb_bias"].reshape(1, 8),
        "L0_ffn_w1T": a["L0_ffn_w1"].transpose(0, 2, 1),
        "L0_ffn_w2T": a["L0_ffn_w2"].transpose(0, 2, 1),
        "L0_ffn_cfcT": a["L0_ffn_cfc"].T,
        "L0_ffn_cprojT": a["L0_ffn_cproj"].T,
        **{f"L1_attn_a_{n}": a[f"L1_attn_a_{n}"] for n in ("W_DQ", "W_DKV", "W_UQ", "W_UK", "W_UV", "W_O")},
        "L1_attn_a_W_QR2": np.stack([np.concatenate([w, np.zeros((32, 4), np.float32)], 1) for w in (wqr, wqr[:, pairs])], 1),
        "L1_attn_a_W_KR2": np.stack([np.concatenate([np.zeros((P, 64), np.float32), w], 1) for w in (wkr, wkr[:, pairs[:4]])], 1),
        "rope_cos": cos, "rope_sin": sin,
        "causal_ceiling": np.where(later, 80.0, -1e30).astype(np.float32),
        "L1_attn_b_Wq": a["L1_attn_b_Wq"], "L1_attn_b_Wout": a["L1_attn_b_Wout"],
        "L1_attn_b_Wkk": np.concatenate([a["L1_attn_b_Wkv"][:, :64]] * 2, 1), "L1_attn_b_Wv": a["L1_attn_b_Wkv"][:, 64:],
        "L1_attn_b_bout": a["L1_attn_b_bout"].reshape(1, DIM),
        "L1_attn_b_rel_by_distance": a["L1_attn_b_rel_emb"][bucket].T,
        "L1_ffn_gate_wT": a["L1_ffn_gate_w"].T,
        "L1_ffn_gate_b": a["L1_ffn_gate_b"].reshape(1, 8),
        "L1_ffn_rms_w": a["L1_ffn_rms_w"].reshape(1, 8),
        "L1_ffn_w1": a["L1_ffn_w1"],
        "L1_ffn_b1": a["L1_ffn_b1"].reshape(16, P),
        "L1_ffn_w2": a["L1_ffn_w2"].reshape(16, P, DIM),
        "L1_ffn_b2": a["L1_ffn_b2"],
    }
    nc = bacc.Bacc("TRN2", target_bir_lowering=False, num_devices=1)
    D, feeds = {}, {}
    for name, v in arrays.items():
        v = np.ascontiguousarray(v)
        feeds[f"in_{name}"] = v
        D[name] = nc.dram_tensor(f"in_{name}", v.shape, mybir.dt.from_np(v.dtype), kind="ExternalInput").ap()
    out = nc.dram_tensor("out", (TOKENS, DIM), F32, kind="ExternalOutput").ap()
    build(nc, D, out)
    r = run_bass_kernel_spmd(nc, [feeds], core_ids=[0])
    return r.results[0]["out"].reshape(BATCH, SEQ, DIM)
```

```python
import math
from contextlib import ExitStack

import concourse.bass as bass
from concourse import mybir

F32 = mybir.dt.float32
BF16 = mybir.dt.bfloat16
I32 = mybir.dt.int32
ALU = mybir.AluOpType
ACT = mybir.ActivationFunctionType
AX = mybir.AxisListType

BATCH, SEQ, DIM = 4, 1024, 128
TOKENS = BATCH * SEQ
P = 128
GROUP_BLOCKS = 4
GROUP = GROUP_BLOCKS * P
GROUPS = TOKENS // GROUP
BLOCKS = TOKENS // P
LN_EPS = 1e-5


class Steps:

    def __init__(self, eng, sem, per_turn, turn):
        self.eng, self.sem, self.per_turn, self.base, self.k = eng, sem, per_turn, turn * per_turn, 0

    def done(self, ins):
        self.k += 1
        ins.then_inc(self.sem, 1)
        self.eng.wait_ge(self.sem, self.base + self.k)

    def close(self):
        assert self.k == self.per_turn, (self.k, self.per_turn)


def bcast(ap, n):
    return ap.unsqueeze(2).broadcast_to([ap.shape[0], ap.shape[1], n])


def semaphores(nc, ctx, tag):
    taken = []

    def give_back():
        nc.clear_and_free_semaphores(taken)
        nc.all_engine_barrier()

    def sem(name):
        taken.append(nc.alloc_semaphore(f"{tag}_{name}"))
        return taken[-1]

    ctx.callback(give_back)
    return sem


def ln_scratch(sb):
    return dict(st=sb("ln_stats", [P, GROUP_BLOCKS, 6], F32), mv=sb("ln_mean_var", [P, GROUP_BLOCKS, 2], F32),
                ve=sb("ln_var_eps", [P, GROUP_BLOCKS], F32), y=sb("ln_rstd", [P, GROUP_BLOCKS], F32),
                wait=sb("ln_wait", [P, 1], F32), t=sb("ln_newton", [P, GROUP_BLOCKS], F32))


def ln_variance(nc, S, steps, ve_ready):
    nc.vector.memset(S["wait"][:], 0.0)
    for k in range(GROUP_BLOCKS):
        ins = nc.vector.bn_aggr(S["mv"][:, k, :], S["st"][:, k, :])
    steps.done(ins)
    nc.vector.tensor_scalar(S["ve"][:], S["mv"][:, :, 1], LN_EPS, None, ALU.add).then_inc(ve_ready, 1)


def ln_newton(nc, dve, S, steps, rough_ready, rough_want):
    ve, y, t = S["ve"], S["y"], S["t"]
    dve.wait_ge(rough_ready, rough_want)
    steps.done(nc.vector.tensor_tensor(t[:], y[:], y[:], ALU.mult))
    steps.done(nc.vector.tensor_tensor(t[:], t[:], ve[:], ALU.mult))
    steps.done(nc.vector.tensor_scalar(t[:], t[:], -0.5, 1.5, ALU.mult, ALU.add))
    steps.done(nc.vector.tensor_tensor(y[:], y[:], t[:], ALU.mult))


def ln_apply(nc, src, out, S):
    for k in range(GROUP_BLOCKS):
        ins = nc.vector.tensor_scalar(out[:, k, :], src(k), S["mv"][:, k, 0:1], S["y"][:, k:k + 1],
                                      ALU.subtract, ALU.mult)
    return ins


def ln_group_vector(nc, dve, src, out, S, steps, rough_ready, rough_want, ve_ready):
    for k in range(GROUP_BLOCKS):
        ins = nc.vector.bn_stats(S["st"][:, k, :], src(k))
    steps.done(ins)
    ln_variance(nc, S, steps, ve_ready)
    ln_newton(nc, dve, S, steps, rough_ready, rough_want)
    return ln_apply(nc, src, out, S)


LN_STEPS = 6


def store_x(sp, out, x, x_done, stored):
    with sp.Fori(0, GROUPS) as g:
        sp.wait_ge(x_done, g + 3)
        sp.dma_start(out[bass.ds(g * GROUP, GROUP), :].rearrange("(k p) d -> p k d", p=P),
                     x[:, bass.ds((g + 1) * GROUP_BLOCKS, GROUP_BLOCKS), :]).then_inc(stored, 16)
    sp.wait_ge(stored, 16 * GROUPS)


FFN_LOADS = 6


def load_ffn_weights(sp, D, C):
    E = 8
    for dst, src in ((C["l0_w1"][:, 0:E, :], D["L0_ffn_w1T"].rearrange("e d h -> d e h")), (C["l0_w1"][:, E, :], D["L0_ffn_cfcT"]),
                     (C["l0_w2"][:, 0:E, :], D["L0_ffn_w2T"].rearrange("e h d -> h e d")), (C["l0_w2"][:, E, :], D["L0_ffn_cprojT"]),
                     (C["l1_w1"][:], D["L1_ffn_w1"].rearrange("e d h -> d e h")),
                     (C["l1_w2"][:], D["L1_ffn_w2"].rearrange("t p d -> p t d"))):
        sp.dma_start(dst, src).then_inc(C["ffn_in"], 16)


def l1_ffn(nc, D, x, C, tag, out=None):
    E, H = 8, 256
    HT = E * H // P
    RMS_EPS = 1.1920928955078125e-07
    with ExitStack() as ctx:
        def sb(name, shape, dt=F32):
            return ctx.enter_context(nc.sbuf_tensor(f"{tag}_{name}", shape, dt))

        def pb(name, shape, dt=F32):
            return ctx.enter_context(nc.psum_tensor(f"{tag}_{name}", shape, dt))

        sem = semaphores(nc, ctx, tag)

        S = ln_scratch(sb)
        w1, w2 = C["l1_w1"], C["l1_w2"]
        b1 = sb("b1", [P, HT])
        b2 = sb("b2", [P, E])
        b2s = sb("b2s", [P, 1])
        gw = sb("gw", [P, E])
        gb = sb("gb", [P, E])
        rw = sb("rw", [P, E])
        xn = sb("xn", [P, 2, GROUP_BLOCKS, DIM])
        xt = sb("xt", [P, 2, GROUP])
        hT = sb("hT", [P, 4, GROUP])
        yT = sb("yT", [P, 2, GROUP])
        lgT = sb("lgT", [E, GROUP])
        lg = sb("lg", [P, GROUP_BLOCKS, E])
        lq = sb("lq", [P, GROUP_BLOCKS, E])
        ms = sb("ms", [P, GROUP_BLOCKS])
        rr = sb("rr", [P, GROUP_BLOCKS])
        tt = sb("tt", [P, GROUP_BLOCKS])
        ng = sb("ng", [P, 3, GROUP_BLOCKS])
        upd = sb("upd", [P, GROUP_BLOCKS, DIM])
        pH = [pb(f"pH{i}", [P, GROUP]) for i in range(4)]
        pY, pB, pT, pG = (pb(n, [P, GROUP]) for n in ("pY", "pB", "pT", "pG"))

        w_in, setup = sem("weights_in"), sem("setup")
        ln_step, ln_ve, ln_rough = sem("ln_step"), sem("ln_ve"), sem("ln_rough")
        xn_ready, xT_done, xt_ready = sem("xn_ready"), sem("xT_done"), sem("xt_ready")
        lg_done, lgT_ready, lgB_done = sem("lg_done"), sem("lgT_ready"), sem("lgB_done")
        g_step, g_ms, g_rough, g_exp = sem("g_step"), sem("g_ms"), sem("g_rough"), sem("g_exp")
        g_scores = sem("g_scores")
        h_done, hT_ready, hT_used = sem("h_done"), sem("hT_ready"), sem("hT_used")
        yT_ready, yB_done, x_step, x_done = (sem(n) for n in ("yT_ready", "yB_done", "x_step", "x_done"))
        stored = sem("stored")

        block = ctx.enter_context(nc.Block())
        NW = 5

        @block.sync
        def _(sp):
            sp.dma_start(gw[:], D["L1_ffn_gate_wT"]).then_inc(w_in, 16)
            sp.dma_start(gb[:], D["L1_ffn_gate_b"].broadcast_to([P, E])).then_inc(w_in, 16)
            sp.dma_start(rw[:], D["L1_ffn_rms_w"].broadcast_to([P, E])).then_inc(w_in, 16)
            sp.dma_start(b1[:], D["L1_ffn_b1"].rearrange("t p -> p t"), allow_slow_non_contiguous=True).then_inc(w_in, 16)
            sp.dma_start(b2[:], D["L1_ffn_b2"].rearrange("e d -> d e"), allow_slow_non_contiguous=True).then_inc(w_in, 16)
            if out is not None:
                store_x(sp, out, x, x_done, stored)

        @block.gpsimd
        def _(pool):
            nc.gpsimd.memset(yT[:, 1, :], 0.0)
            nc.gpsimd.memset(ng[:], 0.0).then_inc(setup, 1)

            def powers(turn):
                pool.wait_ge(ln_ve, turn + 1)
                nc.gpsimd.tensor_tensor(S["y"][:], S["ve"][:], C["mhalf"][:, 0:GROUP_BLOCKS], ALU.pow).then_inc(ln_rough, 1)
                pool.wait_ge(g_ms, turn + 1)
                nc.gpsimd.tensor_tensor(rr[:], ms[:], C["mhalf"][:, 0:GROUP_BLOCKS], ALU.pow).then_inc(g_rough, 1)

            powers(0)
            with pool.Fori(0, GROUPS) as g:
                powers(g + 1)

        def layernorm(dve, gn, par):
            steps = Steps(dve, ln_step, LN_STEPS, gn)
            dve.wait_ge(xT_done, gn)
            ln_group_vector(nc, dve, lambda k: x[:, bass.ds((gn + 1) * GROUP_BLOCKS + k, 1), :], xn[:, par], S, steps,
                            ln_rough, gn + 1, ln_ve).then_inc(xn_ready, 1)
            steps.close()

        def gate(dve, gn, par):
            steps = Steps(dve, g_step, 16, gn)
            dve.wait_ge(lgB_done, gn + 1)
            steps.done(nc.vector.tensor_tensor(lg[:], pT[:, 0:GROUP_BLOCKS * E].rearrange("p (k e) -> p k e", e=E),
                                               gb[:].unsqueeze(1).broadcast_to([P, GROUP_BLOCKS, E]), ALU.add))
            steps.done(nc.vector.tensor_tensor(lq[:], lg[:], lg[:], ALU.mult))
            steps.done(nc.vector.tensor_reduce(tt[:], lq[:], AX.X, ALU.add))
            nc.vector.tensor_scalar(ms[:], tt[:], 1.0 / E, RMS_EPS, ALU.mult, ALU.add).then_inc(g_ms, 1)
            dve.wait_ge(g_rough, gn + 1)
            steps.done(nc.vector.tensor_tensor(tt[:], rr[:], rr[:], ALU.mult))
            steps.done(nc.vector.tensor_tensor(tt[:], tt[:], ms[:], ALU.mult))
            steps.done(nc.vector.tensor_scalar(tt[:], tt[:], -0.5, 1.5, ALU.mult, ALU.add))
            steps.done(nc.vector.tensor_tensor(rr[:], rr[:], tt[:], ALU.mult))
            steps.done(nc.vector.tensor_tensor(lg[:], lg[:], bcast(rr[:], E), ALU.mult))
            steps.done(nc.vector.tensor_tensor(lg[:], lg[:], rw[:].unsqueeze(1).broadcast_to([P, GROUP_BLOCKS, E]), ALU.mult))
            steps.done(nc.vector.tensor_reduce(tt[:], lg[:], AX.X, ALU.max))
            nc.vector.tensor_tensor(lg[:], lg[:], bcast(tt[:], E), ALU.subtract).then_inc(g_scores, 1)
            dve.wait_ge(g_exp, gn + 1)
            steps.done(nc.vector.tensor_reduce(tt[:], lq[:], AX.X, ALU.add))
            steps.done(nc.vector.reciprocal(ms[:], tt[:]))
            steps.done(nc.vector.tensor_scalar(tt[:], ms[:], 1e-6, None, ALU.add))
            steps.done(nc.vector.reciprocal(rr[:], tt[:]))
            steps.done(nc.vector.tensor_tensor(ng[:, par, :], ms[:], rr[:], ALU.mult))
            steps.done(nc.vector.tensor_copy(tt[:], ms[:]))
            steps.close()

        def finish(dve, gp, par, turn):
            dve.wait_ge(yB_done, turn + 1)
            xs = x[:, bass.ds((gp + 1) * GROUP_BLOCKS, GROUP_BLOCKS), :]
            nc.vector.tensor_tensor(upd[:], pB[:].rearrange("p (k d) -> p k d", d=DIM), bcast(ng[:, par, :], DIM),
                                    ALU.mult).then_inc(x_step, 1)
            dve.wait_ge(x_step, turn + 2)
            nc.vector.tensor_tensor(xs, xs, upd[:], ALU.add).then_inc(x_done, 1)

        @block.vector
        def _(dve):
            dve.wait_ge(w_in, 16 * NW)
            nc.vector.tensor_reduce(b2s[:], b2[:], AX.X, ALU.add).then_inc(setup, 1)
            layernorm(dve, 0, 0)
            dve.wait_ge(setup, 2)
            gate(dve, 0, 0)
            with dve.Fori(0, GROUPS // 2) as it:
                for par in (0, 1):
                    g = it * 2 + par
                    layernorm(dve, g + 1, 1 - par)
                    finish(dve, g - 1, 1 - par, g)
                    gate(dve, g + 1, 1 - par)
            finish(dve, GROUPS - 1, 1, GROUPS)

        @block.scalar
        def _(act):
            def to_xt(gn, par):
                act.wait_ge(xT_done, gn + 1)
                nc.scalar.activation(xt[:, par, :], pT[:], ACT.Copy).then_inc(xt_ready, 1)

            def to_lgT(gn):
                act.wait_ge(lg_done, gn + 1)
                nc.scalar.activation(lgT[:], pG[0:E, :], ACT.Copy).then_inc(lgT_ready, 1)

            def gate_exp(gn):
                act.wait_ge(g_scores, gn + 1)
                nc.scalar.activation(lq[:], lg[:], ACT.Exp, scale=2.0).then_inc(g_exp, 1)

            act.wait_ge(w_in, 16 * NW)
            act.wait_ge(setup, 2)
            to_xt(0, 0)
            to_lgT(0)
            gate_exp(0)
            with act.Fori(0, GROUPS // 2) as it:
                for par in (0, 1):
                    g = it * 2 + par
                    for f in range(HT):
                        act.wait_ge(h_done, g * HT + f + 1)
                        act.wait_ge(hT_used, g * HT + f + 1)
                        nc.scalar.activation(hT[:, f % 4, :], pH[f % 4][:], ACT.Gelu, bias=b1[:, f:f + 1]).then_inc(hT_ready, 1)
                        if f == 9:
                            to_xt(g + 1, 1 - par)
                        if f == 11:
                            to_lgT(g + 1)
                        if f == 15:
                            gate_exp(g + 1)
                    act.wait_ge(hT_used, (g + 1) * HT + 4)
                    nc.scalar.activation(yT[:, par, :], pY[:], ACT.Identity, bias=b2s[:, 0:1]).then_inc(yT_ready, 1)

        @block.tensor
        def _(pe):
            def transposes(gn, par):
                pe.wait_ge(xn_ready, gn + 1)
                for k in range(GROUP_BLOCKS):
                    ins = nc.tensor.transpose(pT[:, k * P:(k + 1) * P], xn[:, par, k, :], C["ident"][:])
                ins.then_inc(xT_done, 1)

            def logits(gn, par):
                pe.wait_ge(xt_ready, gn + 1)
                nc.tensor.matmul(pG[0:E, :], gw[:], xt[:, par, :], start=True, stop=True).then_inc(lg_done, 1)

            def logits_back(gn):
                pe.wait_ge(lgT_ready, gn + 1)
                for k in range(GROUP_BLOCKS):
                    ins = nc.tensor.matmul(pT[:, k * E:(k + 1) * E], lgT[:, k * P:(k + 1) * P], C["ident"][0:E, 0:E],
                                           start=True, stop=True)
                ins.then_inc(lgB_done, 1)

            def y_back(turn, par):
                pe.wait_ge(yT_ready, turn + 1)
                pe.wait_ge(x_step, turn + 1)
                for k in range(GROUP_BLOCKS):
                    ins = nc.tensor.transpose(pB[:, k * P:(k + 1) * P], yT[:, par, k * P:(k + 1) * P], C["ident"][:])
                ins.then_inc(yB_done, 1)

            pe.wait_ge(w_in, 16 * NW)
            pe.wait_ge(C["ffn_in"], FFN_LOADS * 16)
            pe.wait_ge(setup, 2)
            pe.sem_inc(hT_used, 4)
            pe.sem_inc(yT_ready, 1)
            pe.sem_inc(x_step, 1)
            pe.sem_inc(x_done, 1)
            transposes(0, 0)
            logits(0, 0)
            logits_back(0)
            with pe.Fori(0, GROUPS // 2) as it:
                for par in (0, 1):
                    g = it * 2 + par

                    def down(f):
                        pe.wait_ge(hT_ready, g * HT + f + 1)
                        nc.tensor.matmul(pY[:], w2[:, f, :], hT[:, f % 4, :], start=(f == 0),
                                         stop=(f == HT - 1)).then_inc(hT_used, 1)

                    for f in range(HT):
                        if f >= 4:
                            pe.wait_ge(hT_ready, g * HT + f - 3)
                        else:
                            pe.wait_ge(yT_ready, g + 1)
                        nc.tensor.matmul(pH[f % 4][:], w1[:, f, :], xt[:, par, :], start=True, stop=True).then_inc(h_done, 1)
                        if f >= 2:
                            down(f - 2)
                        if f == 4:
                            y_back(g, 1 - par)
                        if f == 7:
                            pe.wait_ge(g_step, (g + 1) * 16)
                            transposes(g + 1, 1 - par)
                        if f == 9:
                            logits(g + 1, 1 - par)
                        if f == 11:
                            logits_back(g + 1)
                    down(HT - 2)
                    down(HT - 1)
            y_back(GROUPS, 1)


def l0_ffn(nc, D, x, C, tag, out=None):
    E = 8
    HT = E + 1
    NSLOT = 3
    with ExitStack() as ctx:
        def sb(name, shape, dt=F32):
            return ctx.enter_context(nc.sbuf_tensor(f"{tag}_{name}", shape, dt))

        def pb(name, shape, dt=F32):
            return ctx.enter_context(nc.psum_tensor(f"{tag}_{name}", shape, dt))

        sem = semaphores(nc, ctx, tag)

        S = ln_scratch(sb)
        w1, w2 = C["l0_w1"], C["l0_w2"]
        gw = sb("gw", [P, E])
        lb = sb("lb", [P, E])
        rank = sb("rank", [P, E])
        sel24 = sb("sel24", [3 * E, E, P], BF16)
        xn = sb("xn", [P, 2, GROUP_BLOCKS, DIM])
        xt = sb("xt", [P, 2, GROUP])
        rT = sb("rT", [P, NSLOT, GROUP])
        hT = sb("hT", [P, NSLOT, GROUP])
        yT = sb("yT", [P, 2, GROUP])
        lgT = sb("lgT", [E, GROUP])
        G8 = [P, GROUP_BLOCKS, E]
        lg, sc, eq, sel1, sel2, sg, we, rest = (sb(n, G8) for n in ("lg", "sc", "eq", "sel1", "sel2", "sg", "we", "rest"))
        mx, den = sb("mx", [P, GROUP_BLOCKS]), sb("den", [P, GROUP_BLOCKS])
        we3 = sb("we3", [P, GROUP_BLOCKS, 3 * E], BF16)
        weT = sb("weT", [3 * E, 2, GROUP], BF16)
        pH = [pb(f"pH{i}", [P, GROUP]) for i in range(2)]
        pW = [pb(f"pW{i}", [P, GROUP]) for i in range(2)]
        pY, pB, pT, pG = (pb(n, [P, GROUP]) for n in ("pY", "pB", "pT", "pG"))
        pGb = pG[:].bitcast(BF16)

        w_in, setup = sem("weights_in"), sem("setup")
        ln_step, ln_ve, ln_rough = sem("ln_step"), sem("ln_ve"), sem("ln_rough")
        xn_ready, xT_done, xt_ready = sem("xn_ready"), sem("xT_done"), sem("xt_ready")
        lg_done, lgT_ready, lgB_done = sem("lg_done"), sem("lgT_ready"), sem("lgB_done")
        g_step, lg_ready, sg_ready = sem("g_step"), sem("lg_ready"), sem("sg_ready")
        we_done, weT_ready, wb_done, wb_used = sem("we_done"), sem("weT_ready"), sem("wb_done"), sem("wb_used")
        h_done, r_ready, s_ready, hT_used = (sem(n) for n in ("h_done", "r_ready", "s_ready", "hT_used"))
        yT_ready, yB_done, x_done = (sem(n) for n in ("yT_ready", "yB_done", "x_done"))
        stored = sem("stored")
        NW = 4
        G_STEPS = 23

        block = ctx.enter_context(nc.Block())

        @block.sync
        def _(sp):
            sp.dma_start(gw[:], D["L0_ffn_gate_wT"]).then_inc(w_in, 16)
            sp.dma_start(lb[:], D["L0_ffn_lb_bias"].broadcast_to([P, E])).then_inc(w_in, 16)
            sp.dma_start(rank[:], D["rank"].broadcast_to([P, E])).then_inc(w_in, 16)
            sp.dma_start(sel24[:], D["sel24"]).then_inc(w_in, 16)
            if out is not None:
                store_x(sp, out, x, x_done, stored)

        @block.gpsimd
        def _(pool):
            nc.gpsimd.memset(yT[:, 1, :], 0.0).then_inc(setup, 1)

            def powers(turn):
                pool.wait_ge(ln_ve, turn + 1)
                nc.gpsimd.tensor_tensor(S["y"][:], S["ve"][:], C["mhalf"][:, 0:GROUP_BLOCKS], ALU.pow).then_inc(ln_rough, 1)

            powers(0)
            with pool.Fori(0, GROUPS) as g:
                powers(g + 1)

        def src(gn):
            return lambda k: x[:, bass.ds((gn + 1) * GROUP_BLOCKS + k, 1), :]

        def ln_first(dve, steps, gn):
            for k in range(GROUP_BLOCKS):
                ins = nc.vector.bn_stats(S["st"][:, k, :], src(gn)(k))
            steps.done(ins)
            ln_variance(nc, S, steps, ln_ve)

        def ln_second(dve, steps, gn, par):
            ln_newton(nc, dve, S, steps, ln_rough, gn + 1)
            dve.wait_ge(xT_done, gn)
            ln_apply(nc, src(gn), xn[:, par], S).then_inc(xn_ready, 1)
            steps.close()

        def spread(t):
            return t[:].unsqueeze(1).broadcast_to(G8)

        def best(steps, sel):
            steps.done(nc.vector.tensor_reduce(mx[:], sc[:], AX.X, ALU.max))
            steps.done(nc.vector.tensor_tensor(eq[:], sc[:], bcast(mx[:], E), ALU.is_ge))
            steps.done(nc.vector.tensor_tensor(eq[:], eq[:], spread(rank), ALU.mult))
            steps.done(nc.vector.tensor_reduce(mx[:], eq[:], AX.X, ALU.max))
            steps.done(nc.vector.tensor_tensor(sel[:], eq[:], bcast(mx[:], E), ALU.is_equal))

        def gate_first(dve, steps, gn):
            dve.wait_ge(lgB_done, gn + 1)
            nc.vector.tensor_copy(lg[:], pT[:, 0:GROUP_BLOCKS * E].rearrange("p (k e) -> p k e", e=E)).then_inc(lg_ready, 1)
            dve.wait_ge(lg_ready, gn + 1)
            steps.done(nc.vector.tensor_tensor(sc[:], lg[:], spread(lb), ALU.add))
            best(steps, sel1)

        def gate_second(steps):
            steps.done(nc.vector.scalar_tensor_tensor(sc[:], sel1[:], -3e38, sc[:], ALU.mult, ALU.add))
            best(steps, sel2)

        def gate_weights(dve, steps, gn):
            steps.done(nc.vector.tensor_tensor(sel1[:], sel1[:], sel2[:], ALU.add))
            dve.wait_ge(sg_ready, gn + 1)
            steps.done(nc.vector.tensor_tensor(sg[:], sg[:], sel1[:], ALU.mult))
            steps.done(nc.vector.tensor_reduce(den[:], sg[:], AX.X, ALU.add))
            steps.done(nc.vector.tensor_scalar(den[:], den[:], 1e-6, None, ALU.add))
            steps.done(nc.vector.reciprocal(mx[:], den[:]))
            steps.done(nc.vector.tensor_tensor(we[:], sg[:], bcast(mx[:], E), ALU.mult))

        def gate_parts(steps):
            steps.done(nc.vector.tensor_copy(we3[:, :, 0:E], we[:]))
            steps.done(nc.vector.tensor_tensor(rest[:], we[:], we3[:, :, 0:E], ALU.subtract))
            steps.done(nc.vector.tensor_copy(we3[:, :, E:2 * E], rest[:]))
            steps.done(nc.vector.tensor_tensor(rest[:], rest[:], we3[:, :, E:2 * E], ALU.subtract))
            steps.done(nc.vector.tensor_copy(we3[:, :, 2 * E:3 * E], rest[:]))
            steps.close()

        def finish(dve, gp, turn):
            dve.wait_ge(yB_done, turn + 1)
            xs = x[:, bass.ds((gp + 1) * GROUP_BLOCKS, GROUP_BLOCKS), :]
            nc.vector.tensor_tensor(xs, xs, pB[:].rearrange("p (k d) -> p k d", d=DIM), ALU.add).then_inc(x_done, 1)

        @block.vector
        def _(dve):
            dve.wait_ge(w_in, 16 * NW)
            lns = Steps(dve, ln_step, LN_STEPS, 0)
            ln_first(dve, lns, 0)
            ln_second(dve, lns, 0, 0)
            gs = Steps(dve, g_step, G_STEPS, 0)
            gate_first(dve, gs, 0)
            gate_second(gs)
            gate_weights(dve, gs, 0)
            gate_parts(gs)
            with dve.Fori(0, GROUPS // 2) as it:
                for par in (0, 1):
                    g = it * 2 + par

                    def weigh(e):
                        n = g * E + e + 1
                        dve.wait_ge(wb_done, n)
                        dve.wait_ge(s_ready, g * HT + e + 1)
                        dve.wait_ge(hT_used, g * HT + e + 1)
                        nc.vector.tensor_tensor(hT[:, e % NSLOT, :], rT[:, e % NSLOT, :], pW[e % 2][:], ALU.mult).then_inc(wb_used, 1)

                    lns = Steps(dve, ln_step, LN_STEPS, g + 1)
                    gs = Steps(dve, g_step, G_STEPS, g + 1)
                    ln_first(dve, lns, g + 1)
                    weigh(0)
                    ln_second(dve, lns, g + 1, 1 - par)
                    weigh(1)
                    weigh(2)
                    finish(dve, g - 1, g)
                    weigh(3)
                    weigh(4)
                    weigh(5)
                    gate_first(dve, gs, g + 1)
                    weigh(6)
                    gate_second(gs)
                    weigh(7)
                    gate_weights(dve, gs, g + 1)
                    gate_parts(gs)
            finish(dve, GROUPS - 1, GROUPS)

        @block.scalar
        def _(act):
            def to_xt(gn, par):
                act.wait_ge(xT_done, gn + 1)
                nc.scalar.activation(xt[:, par, :], pT[:], ACT.Copy).then_inc(xt_ready, 1)

            def to_lgT(gn):
                act.wait_ge(lg_done, gn + 1)
                nc.scalar.activation(lgT[:], pG[0:E, :], ACT.Copy).then_inc(lgT_ready, 1)

            def gate_sigmoid(gn):
                act.wait_ge(lg_ready, gn + 1)
                nc.scalar.activation(sg[:], lg[:], ACT.Sigmoid).then_inc(sg_ready, 1)

            def to_weT(gn, par):
                act.wait_ge(we_done, gn + 1)
                nc.scalar.activation(weT[:, par, :], pGb[0:3 * E, 0:GROUP], ACT.Copy).then_inc(weT_ready, 1)

            act.wait_ge(w_in, 16 * NW)
            to_xt(0, 0)
            to_lgT(0)
            gate_sigmoid(0)
            with act.Fori(0, GROUPS // 2) as it:
                for par in (0, 1):
                    g = it * 2 + par

                    def relu(f):
                        act.wait_ge(h_done, g * HT + f + 1)
                        if f >= NSLOT:
                            act.wait_ge(wb_used, g * E + f - NSLOT + 1)
                        nc.scalar.activation(rT[:, f % NSLOT, :], pH[f % 2][:], ACT.Relu).then_inc(r_ready, 1)

                    def square(f):
                        act.wait_ge(r_ready, g * HT + f + 2)
                        to = rT
                        if f == E:
                            act.wait_ge(hT_used, g * HT + f + 1)
                            to = hT
                        nc.scalar.activation(to[:, f % NSLOT, :], rT[:, f % NSLOT, :], ACT.Square).then_inc(s_ready, 1)

                    relu(0)
                    for f in range(1, HT):
                        relu(f)
                        if f == 1:
                            to_weT(g, par)
                        square(f - 1)
                        if f == 4:
                            to_xt(g + 1, 1 - par)
                        if f == 6:
                            to_lgT(g + 1)
                        if f == 8:
                            gate_sigmoid(g + 1)
                    square(E)
                    act.wait_ge(hT_used, (g + 1) * HT + NSLOT)
                    nc.scalar.activation(yT[:, par, :], pY[:], ACT.Copy).then_inc(yT_ready, 1)

        @block.tensor
        def _(pe):
            def transposes(gn, par):
                pe.wait_ge(xn_ready, gn + 1)
                for k in range(GROUP_BLOCKS):
                    ins = nc.tensor.transpose(pT[:, k * P:(k + 1) * P], xn[:, par, k, :], C["ident"][:])
                ins.then_inc(xT_done, 1)

            def logits(gn, par):
                pe.wait_ge(xt_ready, gn + 1)
                nc.tensor.matmul(pG[0:E, :], gw[:], xt[:, par, :], start=True, stop=True).then_inc(lg_done, 1)

            def logits_back(gn):
                pe.wait_ge(lgT_ready, gn + 1)
                for k in range(GROUP_BLOCKS):
                    ins = nc.tensor.matmul(pT[:, k * E:(k + 1) * E], lgT[:, k * P:(k + 1) * P], C["ident"][0:E, 0:E],
                                           start=True, stop=True)
                ins.then_inc(lgB_done, 1)

            def weights_T(gn):
                pe.wait_ge(g_step, (gn + 1) * G_STEPS)
                for k in range(GROUP_BLOCKS):
                    ins = nc.tensor.transpose(pGb[0:3 * E, k * P:(k + 1) * P], we3[:, k, :], C["ident16"][:])
                ins.then_inc(we_done, 1)

            def y_back(turn, par):
                pe.wait_ge(yT_ready, turn + 1)
                pe.wait_ge(x_done, turn + 1)
                for k in range(GROUP_BLOCKS):
                    ins = nc.tensor.transpose(pB[:, k * P:(k + 1) * P], yT[:, par, k * P:(k + 1) * P], C["ident"][:])
                ins.then_inc(yB_done, 1)

            pe.wait_ge(w_in, 16 * NW)
            pe.wait_ge(C["ffn_in"], FFN_LOADS * 16)
            pe.wait_ge(setup, 1)
            pe.sem_inc(hT_used, NSLOT)
            pe.sem_inc(yT_ready, 1)
            pe.sem_inc(x_done, 1)
            transposes(0, 0)
            logits(0, 0)
            logits_back(0)
            pe.sem_inc(r_ready, 1)
            with pe.Fori(0, GROUPS // 2) as it:
                for par in (0, 1):
                    g = it * 2 + par

                    def down(f):
                        if f < E:
                            pe.wait_ge(wb_used, g * E + f + 1)
                        else:
                            pe.wait_ge(s_ready, (g + 1) * HT)
                        nc.tensor.matmul(pY[:], w2[:, f, :], hT[:, f % NSLOT, :], start=(f == 0),
                                         stop=(f == HT - 1)).then_inc(hT_used, 1)

                    def up(f):
                        pe.wait_ge(r_ready, g * HT + max(f, 1))
                        nc.tensor.matmul(pH[f % 2][:], w1[:, f, :], xt[:, par, :], start=True, stop=True).then_inc(h_done, 1)

                    def weights(f):
                        if f >= 2:
                            pe.wait_ge(wb_used, g * E + f - 1)
                        nc.tensor.matmul(pW[f % 2][:], sel24[:, f, :], weT[:, par, :], start=True, stop=True).then_inc(wb_done, 1)

                    up(0)
                    up(1)
                    weights_T(g)
                    pe.wait_ge(weT_ready, g + 1)
                    weights(0)
                    weights(1)
                    y_back(g, 1 - par)
                    for f in range(2, HT):
                        up(f)
                        if f < E:
                            weights(f)
                        if f == 3:
                            pe.wait_ge(lg_ready, g + 1)
                            transposes(g + 1, 1 - par)
                        if f == 5:
                            logits(g + 1, 1 - par)
                        if f == 6:
                            logits_back(g + 1)
                        down(f - 2)
                    down(HT - 2)
                    down(HT - 1)
            y_back(GROUPS, 1)


def l0_attn_b(nc, D, x, C, tag, out=None):
    HEADS, HD = 16, 64
    INNER = HEADS * HD
    PAIRS = HEADS // 2
    BANK_PAIRS = 3
    VC = 2 * HD + 1
    HALVES = SEQ // GROUP
    with ExitStack() as ctx:
        def sb(name, shape, dt=F32):
            return ctx.enter_context(nc.sbuf_tensor(f"{tag}_{name}", shape, dt))

        def pb(name, shape, dt=F32):
            return ctx.enter_context(nc.psum_tensor(f"{tag}_{name}", shape, dt))

        sem = semaphores(nc, ctx, tag)

        S = ln_scratch(sb)
        wqkT = sb("wqkT", [HD, 2 * HEADS, DIM])
        wf = sb("wf", [HD, HD])
        wq = sb("wq", [P, INNER])
        wk = sb("wk", [P, INNER])
        wv = sb("wv", [P, INNER])
        wo = sb("wo", [P, PAIRS, DIM])
        bo = sb("bo", [P, 1])
        bf = sb("bf", [P, 1])
        bfr = sb("bfr", [P, GROUP // HD, HD])
        eps = sb("eps", [P, 1])
        xn = sb("xn", [P, 2, GROUP_BLOCKS, DIM])
        xt = sb("xt", [P, 2, GROUP])
        qT = sb("qT", [P, PAIRS, SEQ])
        kr = sb("kr", [P, 2, INNER])
        vb = sb("vb", [P, 2, PAIRS, VC])
        kvd = sb("kvd", [P, PAIRS, P])
        ksd = sb("ksd", [P, PAIRS, P])
        dn = sb("dn", [P, 2, GROUP])
        cT = sb("cT", [P, 2, GROUP])
        yT = sb("yT", [P, 2, GROUP])
        pA = [pb(f"pA{i}", [P, GROUP]) for i in range(3)]
        pK = [pb(f"pK{i}", [P, GROUP]) for i in range(3)]
        pY, pT = pb("pY", [P, GROUP]), pb("pT", [P, GROUP])

        w_in, setup, folded, fold_used = sem("weights_in"), sem("setup"), sem("folded"), sem("fold_used")
        ln_step, ln_ve, ln_rough = sem("ln_step"), sem("ln_ve"), sem("ln_rough")
        xn_ready, xT_done, xt_ready = sem("xn_ready"), sem("xT_done"), sem("xt_ready")
        q_done, q_used, k_done, k_raw, k_ready = sem("q_done"), sem("q_used"), sem("k_done"), sem("k_raw"), sem("k_ready")
        v_done, v_ready, kv_done, kvd_ready = sem("v_done"), sem("v_ready"), sem("kv_done"), sem("kvd_ready")
        nd_done, dn_ready, dn_step, c_ready, c_used = (sem(n) for n in
                                                      ("nd_done", "dn_ready", "dn_step", "c_ready", "c_used"))
        yT_ready, yB_done, x_done = (sem(n) for n in ("yT_ready", "yB_done", "x_done"))
        stored = sem("stored")
        NW = 7

        jobs = []
        for half in range(HALVES):
            jobs += [("q", half, i) for i in range(PAIRS)]
            for tb in range(GROUP_BLOCKS):
                jobs += [("k", half * GROUP_BLOCKS + tb, i) for i in (0, 1)]
                jobs += [("v", half * GROUP_BLOCKS + tb, i) for i in (0, 1)]
        PER = {"q": HALVES * PAIRS, "k": 2 * HALVES * GROUP_BLOCKS, "v": 2 * HALVES * GROUP_BLOCKS}
        used = {"q": q_used, "k": k_raw, "v": v_ready}

        def number(job):
            kind, a, i = job
            return a * PAIRS + i if kind == "q" else 2 * a + i

        block = ctx.enter_context(nc.Block())

        @block.sync
        def _(sp):
            sp.dma_start(wf[:], D["L0_attn_b_W_f"]).then_inc(w_in, 16)
            sp.dma_start(wqkT[:], D["L0_attn_b_WqkT"].rearrange("(h d) n -> d h n", d=HD)).then_inc(w_in, 16)
            sp.dma_start(wv[:], D["L0_attn_b_Wv"]).then_inc(w_in, 16)
            sp.dma_start(wo[:], D["L0_attn_b_W_out"].rearrange("(t p) n -> p t n", p=P)).then_inc(w_in, 16)
            sp.dma_start(bo[:], D["L0_attn_b_b_out"]).then_inc(w_in, 16)
            sp.dma_start(bf[:], D["L0_attn_b_b_f2"]).then_inc(w_in, 16)
            sp.dma_start(bfr[:], D["L0_attn_b_b_f"].unsqueeze(1).broadcast_to([P, GROUP // HD, HD])).then_inc(w_in, 16)
            if out is not None:
                store_x(sp, out, x, x_done, stored)

        @block.gpsimd
        def _(pool):
            nc.gpsimd.memset(yT[:, 1, :], 0.0).then_inc(setup, 1)
            nc.gpsimd.memset(eps[:], 1e-6).then_inc(setup, 1)
            nc.gpsimd.memset(kvd[:], 0.0).then_inc(setup, 1)
            nc.gpsimd.memset(ksd[:], 0.0).then_inc(setup, 1)
            nc.gpsimd.memset(vb[:, :, :, VC - 1:VC], 1.0).then_inc(setup, 1)

            def powers(turn):
                pool.wait_ge(ln_ve, turn + 1)
                nc.gpsimd.tensor_tensor(S["y"][:], S["ve"][:], C["mhalf"][:, 0:GROUP_BLOCKS], ALU.pow).then_inc(ln_rough, 1)

            powers(0)
            with pool.Fori(0, GROUPS) as g:
                powers(g + 1)

        def layernorm(dve, gn, par):
            steps = Steps(dve, ln_step, LN_STEPS, gn)
            dve.wait_ge(xT_done, gn)
            ln_group_vector(nc, dve, lambda k: x[:, bass.ds((gn + 1) * GROUP_BLOCKS + k, 1), :], xn[:, par], S, steps,
                            ln_rough, gn + 1, ln_ve).then_inc(xn_ready, 1)
            steps.close()

        def finish(dve, gp, turn):
            dve.wait_ge(yB_done, turn + 1)
            xs = x[:, bass.ds((gp + 1) * GROUP_BLOCKS, GROUP_BLOCKS), :]
            nc.vector.tensor_tensor(xs, xs, pT[:].rearrange("p (k d) -> p k d", d=DIM), ALU.add).then_inc(x_done, 1)

        @block.vector
        def _(dve):
            dve.wait_ge(w_in, 16 * NW)
            for i, w in enumerate((wq, wk)):
                dve.wait_ge(folded, i + 1)
                for j in (0, 1):
                    nc.vector.tensor_copy(w[:, j * GROUP:(j + 1) * GROUP], pA[j][:]).then_inc(fold_used, 1)
            dve.wait_ge(setup, 5)
            layernorm(dve, 0, 0)
            with dve.Fori(0, BATCH) as b:
                layernorm(dve, b * 2 + 1, 1)
                finish(dve, b * 2 - 1, b * 2)
                for job in jobs:
                    if job[0] != "k":
                        continue
                    n, tb = number(job), job[1]
                    i = job[2]
                    dve.wait_ge(k_done, b * PER["k"] + n + 1)
                    dve.wait_ge(kv_done, b * 8 + tb + 1)
                    bank = jobs.index(job) % 3
                    nc.vector.tensor_tensor(kr[:, tb % 2, i * GROUP:(i + 1) * GROUP], pA[bank][:],
                                            bfr[:].rearrange("p a d -> p (a d)"), ALU.add).then_inc(k_raw, 1)
                layernorm(dve, b * 2 + 2, 0)
                dve.wait_ge(kv_done, b * 8 + 10)
                for t in range(PAIRS):
                    src = pK[t // BANK_PAIRS][:, (t % BANK_PAIRS) * VC:(t % BANK_PAIRS + 1) * VC]
                    for lo in (0, HD):
                        nc.vector.tensor_copy(kvd[lo:lo + HD, t, lo:lo + HD], src[lo:lo + HD, lo:lo + HD])
                        ins = nc.vector.tensor_copy(ksd[lo:lo + HD, t, lo:lo + HD],
                                                    src[lo:lo + HD, VC - 1:VC].broadcast_to([HD, HD]))
                ins.then_inc(kvd_ready, 1)
                for half in range(HALVES):
                    for t in range(PAIRS):
                        n = b * HALVES * PAIRS + half * PAIRS + t
                        dve.wait_ge(dn_ready, n + 1)
                        nc.vector.reciprocal(dn[:, t % 2, :], dn[:, t % 2, :]).then_inc(dn_step, 1)
                        dve.wait_ge(dn_step, n + 1)
                        dve.wait_ge(c_used, n + 1)
                        nc.vector.tensor_tensor(cT[:, t % 2, :], pA[t % 2][:], dn[:, t % 2, :], ALU.mult).then_inc(c_ready, 1)
                        if half == 1 and t == 2:
                            finish(dve, b * 2, b * 2 + 1)
            finish(dve, GROUPS - 1, GROUPS)

        @block.scalar
        def _(act):
            def to_xt(gn, par):
                act.wait_ge(xT_done, gn + 1)
                nc.scalar.activation(xt[:, par, :], pT[:], ACT.Copy).then_inc(xt_ready, 1)

            act.wait_ge(w_in, 16 * NW)
            act.wait_ge(setup, 5)
            to_xt(0, 0)
            with act.Fori(0, BATCH) as b:
                for j, job in enumerate(jobs):
                    kind, a, i = job
                    n = b * PER[kind] + number(job)
                    if kind == "q":
                        act.wait_ge(q_done, n + 1)
                        nc.scalar.activation(qT[:, i, a * GROUP:(a + 1) * GROUP], pA[j % 3][:], ACT.Relu,
                                             bias=bf[:, 0:1]).then_inc(q_used, 1)
                        if a == 0 and i == 6:
                            to_xt(b * 2 + 1, 1)
                    elif kind == "k":
                        act.wait_ge(k_raw, n + 1)
                        ks = kr[:, a % 2, i * GROUP:(i + 1) * GROUP]
                        nc.scalar.activation(ks, ks, ACT.Relu).then_inc(k_ready, 1)
                    else:
                        act.wait_ge(v_done, n + 1)
                        act.wait_ge(kv_done, b * 8 + a + 1)
                        nc.scalar.activation(vb[:, a % 2, i * 4:i * 4 + 4, 0:2 * HD],
                                             pA[j % 3][:].rearrange("p (t c) -> p t c", c=2 * HD), ACT.Copy).then_inc(v_ready, 1)
                for half in range(HALVES):
                    for t in range(PAIRS):
                        n = b * HALVES * PAIRS + half * PAIRS + t
                        act.wait_ge(nd_done, n + 1)
                        act.wait_ge(c_used, n + 1)
                        nc.scalar.activation(dn[:, t % 2, :], pK[t % 2][:], ACT.Identity, bias=eps[:, 0:1]).then_inc(dn_ready, 1)
                        if half == 0 and t == 2:
                            to_xt(b * 2 + 2, 0)
                    act.wait_ge(c_used, (b * 2 + half + 1) * PAIRS + 2)
                    nc.scalar.activation(yT[:, half, :], pY[:], ACT.Identity, bias=bo[:, 0:1]).then_inc(yT_ready, 1)

        @block.tensor
        def _(pe):
            def transposes(gn, par):
                pe.wait_ge(xn_ready, gn + 1)
                for k in range(GROUP_BLOCKS):
                    ins = nc.tensor.transpose(pT[:, k * P:(k + 1) * P], xn[:, par, k, :], C["ident"][:])
                ins.then_inc(xT_done, 1)

            def y_back(turn, par):
                pe.wait_ge(yT_ready, turn + 1)
                for k in range(GROUP_BLOCKS):
                    ins = nc.tensor.transpose(pT[:, k * P:(k + 1) * P], yT[:, par, k * P:(k + 1) * P], C["ident"][:])
                ins.then_inc(yB_done, 1)

            pe.wait_ge(w_in, 16 * NW)
            for i in (0, 1):
                if i:
                    pe.wait_ge(fold_used, 2)
                for h in range(HEADS):
                    ins = nc.tensor.matmul(pA[h // 8][:, (h % 8) * HD:(h % 8 + 1) * HD], wqkT[:, i * HEADS + h, :], wf[:],
                                           start=True, stop=True)
                ins.then_inc(folded, 1)
            pe.wait_ge(fold_used, 4)
            pe.wait_ge(setup, 5)
            pe.sem_inc(kv_done, 2)
            pe.sem_inc(c_used, 2)
            pe.sem_inc(yT_ready, 1)
            pe.sem_inc(x_done, 1)
            transposes(0, 0)
            with pe.Fori(0, BATCH) as b:
                def kv(tb):
                    pe.wait_ge(k_ready, b * PER["k"] + 2 * tb + 2)
                    pe.wait_ge(v_ready, b * PER["v"] + 2 * tb + 2)
                    for t in range(PAIRS):
                        ins = nc.tensor.matmul(pK[t // BANK_PAIRS][:, (t % BANK_PAIRS) * VC:(t % BANK_PAIRS + 1) * VC],
                                               kr[:, tb % 2, t * P:(t + 1) * P], vb[:, tb % 2, t, :],
                                               start=(tb == 0 and t % BANK_PAIRS == 0), stop=(tb == 7),
                                               skip_group_check=True)
                    ins.then_inc(kv_done, 1)

                pe.wait_ge(yT_ready, b * 2 + 1)
                for j, job in enumerate(jobs):
                    kind, a, i = job
                    if j % (len(jobs) // 2) == 0:
                        pe.wait_ge(xt_ready, b * 2 + j // (len(jobs) // 2) + 1)
                    if j >= 3:
                        before = jobs[j - 3]
                        pe.wait_ge(used[before[0]], b * PER[before[0]] + number(before) + 1)
                    half = a if kind == "q" else a // GROUP_BLOCKS
                    if kind == "q":
                        nc.tensor.matmul(pA[j % 3][:], wq[:, i * P:(i + 1) * P], xt[:, half, :], start=True, stop=True).then_inc(q_done, 1)
                        if a == 0 and i == 2:
                            y_back(b * 2, 1)
                        if a == 0 and i == 6:
                            pe.wait_ge(x_done, b * 2 + 2)
                            transposes(b * 2 + 1, 1)
                    else:
                        w, done = (wk, k_done) if kind == "k" else (wv, v_done)
                        tb = a % GROUP_BLOCKS
                        nc.tensor.matmul(pA[j % 3][:], xt[:, half, tb * P:(tb + 1) * P], w[:, i * GROUP:(i + 1) * GROUP],
                                         start=True, stop=True).then_inc(done, 1)
                        if kind == "v" and i == 1 and a >= 1:
                            kv(a - 1)
                kv(7)
                pe.wait_ge(kvd_ready, b + 1)
                for half in range(HALVES):
                    def down(t):
                        pe.wait_ge(c_ready, b * HALVES * PAIRS + half * PAIRS + t + 1)
                        nc.tensor.matmul(pY[:], wo[:, t, :], cT[:, t % 2, :], start=(t == 0), stop=(t == PAIRS - 1)).then_inc(c_used, 1)

                    if half:
                        pe.wait_ge(yT_ready, b * 2 + 2)
                    for t in range(PAIRS):
                        n = b * HALVES * PAIRS + half * PAIRS + t
                        if half or t >= 2:
                            pe.wait_ge(c_ready, n - 1)
                        q = qT[:, t, half * GROUP:(half + 1) * GROUP]
                        nc.tensor.matmul(pA[t % 2][:], kvd[:, t, :], q, start=True, stop=True)
                        nc.tensor.matmul(pK[t % 2][:], ksd[:, t, :], q, start=True, stop=True).then_inc(nd_done, 1)
                        if t >= 1:
                            down(t - 1)
                        if half == 0 and t == 2:
                            transposes(b * 2 + 2, 0)
                        if half == 1 and t == 2:
                            pe.wait_ge(xt_ready, b * 2 + 3)
                            y_back(b * 2 + 1, 0)
                    down(PAIRS - 1)
            y_back(GROUPS, 1)


RUNS = ((0, 3), (3, 2), (5, 1))


def send_parts(sp, dram, b, rows, part, par, cols, repeat, sent):
    for p, (pos, n) in enumerate(RUNS):
        src = part[rows, par, p:p + 1, :].broadcast_to([rows.stop - rows.start, n, GROUP]) if repeat else part[rows, par, 0:n, :]
        sp.dma_start(dram[bass.ds(b, 1), pos:pos + n, :, cols].rearrange("o s p t -> p (o s) t"), src).then_inc(sent, 16)


def attention_rows(nc, C, tag, hd, q_stacks, k_stacks, products, table, v_at, out_dram=None, columns=None):
    HEADS = 64
    U = SEQ // P
    BLOCK = [(U // 2 + u) % U for u in range(U)]
    with ExitStack() as ctx:
        def sb(name, shape, dt=F32):
            return ctx.enter_context(nc.sbuf_tensor(f"{tag}_{name}", shape, dt))

        def pb(name, shape, dt=F32):
            return ctx.enter_context(nc.psum_tensor(f"{tag}_{name}", shape, dt))

        sem = semaphores(nc, ctx, tag)

        qs = [sb(f"qs{i}", [s["rows"], 2, SEQ], BF16) for i, s in enumerate(q_stacks)]
        ks = [s["resident"] if "resident" in s else sb(f"ks{i}", [s["rows"], 2, SEQ], BF16) for i, s in enumerate(k_stacks)]
        tab = sb("tab", [P, 2, SEQ])
        vw = hd + 1 if columns else hd
        vh = sb("vh", [P, 2, U, vw])
        sg = sb("sg", [P, 4, SEQ])
        mn = sb("mn", [P, 4])
        den = sb("den", [P, 2, U])
        rd = sb("rd", [P, U])
        pT = sb("pT", [P, 2, SEQ])
        co = sb("co", [P, U, 2, hd]) if out_dram else sb("co", [vw, 2, SEQ])
        pS = [pb(f"pS{i}", [P, SEQ]) for i in range(2)]
        pX = [pb(f"pX{i}", [P, GROUP]) for i in range(2)]
        pO = [pb(f"pO{i}", [P, GROUP]) for i in range(2)]

        waited = sem("waited")
        ones_set, o_out, col_sent = sem("ones_set"), sem("o_out"), [sem("col_sent0"), sem("col_sent1")]
        const_in, loaded, v_ready = sem("const_in"), [sem("loaded0"), sem("loaded1")], sem("v_ready")
        s_done, m_done, e_done, t_done = sem("s_done"), sem("m_done"), sem("e_done"), sem("t_done")
        x_act, x_dve, pv_done, rd_ready, norm_done, sent = (sem(n) for n in
                                                    ("x_act", "x_dve", "pv_done", "rd_ready", "norm_done", "sent"))

        width = [(b + 1) * P for b in BLOCK]
        chunks, first_chunk = [], []
        for u in range(U):
            first_chunk.append(len(chunks))
            for lo in range(0, width[u], GROUP):
                chunks.append((u, lo, min(GROUP, width[u] - lo)))
        by_act = {(0, 0), (1, 0), (2, 0), (3, 0), (7, 0)}
        NC = len(chunks)
        owner = ["act" if (u, lo) in by_act else "dve" for u, lo, _ in chunks]
        per = {e: owner.count(e) for e in ("act", "dve")}

        def copied(eng, head, c):
            if c < 0:
                head, c = head - 1, c + NC
            e = owner[c]
            eng.wait_ge(x_act if e == "act" else x_dve, head * per[e] + owner[:c + 1].count(e))

        def place(s):
            return s // U, s % U

        block = ctx.enter_context(nc.Block())
        NL = sum(len(s["loads"](0)) for s in q_stacks + k_stacks if "loads" in s) + 1
        consts = []
        for t, s in list(zip(qs, q_stacks)) + list(zip(ks, k_stacks)):
            for lo, n, src in s.get("consts", []):
                consts += [(t[lo:lo + n, i, :], src) for i in (0, 1)]

        @block.sync
        def _(sp):
            for dst, src in consts:
                sp.dma_start(dst, src).then_inc(const_in, 16)

            def load(bh, par):
                for t, s in list(zip(qs, q_stacks)) + list(zip(ks, k_stacks)):
                    for lo, n, src in s["loads"](bh) if "loads" in s else []:
                        sp.dma_start(t[lo:lo + n, par, :], src).then_inc(loaded[par], 16)
                sp.dma_start(tab[:, par, :], table(bh)).then_inc(loaded[par], 16)

            def store(pair):
                sp.wait_ge(norm_done, pair * 2 + 4)
                sp.dma_start(out_dram(pair), co[:].rearrange("p u i d -> p (u i d)")).then_inc(sent, 16)

            def store_columns(bh, par):
                sp.wait_ge(o_out, bh * 2 + 4)
                for dst, lo, hi in ((columns[0][bass.ds(bh * hd, hd), :], 0, hd), (columns[1][bass.ds(bh, 1), :], hd, vw)):
                    sp.dma_start(dst, co[lo:hi, par, :]).then_inc(col_sent[par], 16)

            load(0, 0)
            load(1, 1)
            with sp.Fori(1, HEADS // 2) as it:
                for par in (0, 1):
                    bh = it * 2 + par
                    sp.wait_ge(m_done, (bh - 1) * U)
                    load(bh, par)
                    if columns:
                        store_columns(bh - 2, par)
                if out_dram is not None:
                    store(it - 1)
            sp.wait_ge(m_done, (HEADS - 1) * U)
            load(HEADS, 0)
            if out_dram is not None:
                store(HEADS // 2 - 1)
                sp.wait_ge(sent, (HEADS // 2 + 1) * 16)
            for par in (0, 1) if columns else ():
                store_columns(HEADS - 2 + par, par)
                sp.wait_ge(col_sent[par], (HEADS // 2 + 1) * 32)

        @block.gpsimd
        def _(pool):
            def v_copy(bh, par):
                nc.gpsimd.tensor_copy(vh[:, par, :, 0:hd], v_at(bh)).then_inc(v_ready, 1)

            if columns:
                nc.gpsimd.memset(vh[:], 1.0).then_inc(ones_set, 1)
                pool.wait_ge(ones_set, 1)
            v_copy(0, 0)
            v_copy(1, 1)
            with pool.Fori(1, HEADS // 2) as it:
                for par in (0, 1):
                    bh = it * 2 + par
                    pool.wait_ge(pv_done, bh * U - U)
                    v_copy(bh, par)

        @block.tensor
        def _(pe):
            if consts:
                pe.wait_ge(const_in, 16 * len(consts))
            pe.sem_inc(norm_done, 2)
            pe.sem_inc(o_out, 2)
            for par in (0, 1):
                pe.sem_inc(col_sent[par], 32)

            def scores(bh, par, u, slot, free=None):
                if u == 0:
                    pe.wait_ge(loaded[par], ((bh - par) // 2 + 1) * 16 * NL if isinstance(bh, int)
                               else (bh + (2 - par)) * (8 * NL))
                if free is not None:
                    pe.wait_ge(m_done, free)
                lo = BLOCK[u] * P
                for c in range(0, width[u], GROUP):
                    w = min(GROUP, width[u] - c)
                    for i, (q, k) in enumerate(products):
                        rhs = (ks[k][:, bass.ds(bh // 16 * SEQ + c, w)] if "resident" in k_stacks[k]
                               else ks[k][:, par, c:c + w])
                        ins = nc.tensor.matmul(pS[slot][:, c:c + w], qs[q][:, par, lo:lo + P], rhs,
                                               start=(i == 0), stop=(i == len(products) - 1))
                ins.then_inc(s_done, 1)

            def turn(bh, u, n, first=False):
                pe.wait_ge(e_done, n + 1)
                for c, (cu, lo, w) in enumerate(chunks):
                    if cu != u:
                        continue
                    if not (first and c < 2):
                        copied(pe, bh, c - 2)
                    for a in range(lo, lo + w, P):
                        ins = nc.tensor.transpose(pX[c % 2][:, a - lo:a - lo + P], sg[:, u % 4, a:a + P], C["ident"][:])
                    ins.then_inc(t_done, 1)

            def weigh_columns(bh, par, u):
                block = BLOCK[u]
                o = pO[block // 4][0:vw, block % 4 * P:(block % 4 + 1) * P]
                if u == 0:
                    pe.wait_ge(v_ready, bh + 1)
                if u % 4 == 0:
                    pe.wait_ge(o_out, bh * 2 + 1 + u // 4)
                for c, (cu, lo, w) in enumerate(chunks):
                    if cu != u:
                        continue
                    copied(pe, bh, c)
                    for a in range(lo, lo + w, P):
                        ins = nc.tensor.matmul(o, vh[:, par, a // P, :], pT[:, u % 2, a:a + P], start=(a == 0),
                                               stop=(a + P == width[u]))
                ins.then_inc(pv_done, 1)

            def weigh(bh, par, u):
                if columns:
                    weigh_columns(bh, par, u)
                    return
                if u == 0:
                    pe.wait_ge(v_ready, bh + 1)
                    pe.wait_ge(norm_done, bh + 1)
                for c, (cu, lo, w) in enumerate(chunks):
                    if cu != u:
                        continue
                    copied(pe, bh, c)
                    for a in range(lo, lo + w, P):
                        ins = nc.tensor.matmul(pO[par][:, BLOCK[u] * hd:(BLOCK[u] + 1) * hd], pT[:, u % 2, a:a + P],
                                               vh[:, par, a // P, :], start=(u == 0 and a == 0),
                                               stop=(a + P == width[u]), skip_group_check=True)
                ins.then_inc(pv_done, 1)

            scores(0, 0, 0, 0)
            scores(0, 0, 1, 1)
            scores(0, 0, 2, 0, free=1)
            turn(0, 0, 0, first=True)
            with pe.Fori(0, HEADS // 2) as it:
                for s in range(2 * U):
                    n = it * (2 * U) + s
                    h3, u3 = place(s + 3)
                    scores(it * 2 + h3, h3 % 2, u3, (s + 3) % 2, free=n + 2)
                    h1, u1 = place(s + 1)
                    turn(it * 2 + h1, u1, n + 1)
                    h0, u0 = place(s)
                    weigh(it * 2 + h0, h0, u0)

        def copies(eng, name, bh, u, out_sem, copy):
            for c, (cu, lo, w) in enumerate(chunks):
                if cu == u and owner[c] == name:
                    eng.wait_ge(t_done, bh * NC + c + 1)
                    copy(pT[:, u % 2, lo:lo + w], pX[c % 2][:, 0:w]).then_inc(out_sem, 1)

        @block.vector
        def _(dve):
            def add_min(par, u, n):
                dve.wait_ge(s_done, n + 1)
                dve.sem_inc(waited, 1)
                w = width[u]
                nc.vector.tensor_tensor_reduce(sg[:, u % 4, 0:w], pS[u % 2][:, 0:w], tab[:, par, SEQ - w:SEQ], 1.0, 3e38,
                                               ALU.add, ALU.min, mn[:, u % 4:u % 4 + 1]).then_inc(m_done, 1)

            def norm(bh, par):
                dve.wait_ge(pv_done, (bh + 1) * U)
                nc.vector.reciprocal(rd[:], den[:, par, :]).then_inc(rd_ready, 1)
                dve.wait_ge(rd_ready, bh + 1)
                if out_dram is not None and par == 0:
                    dve.wait_ge(sent, (bh // 2 + 1) * 16)
                nc.vector.tensor_tensor(co[:, :, par, :],
                                        pO[par][:, 0:U * hd].rearrange("p (u d) -> p u d", d=hd),
                                        bcast(rd[:], hd), ALU.mult).then_inc(norm_done, 1)

            if out_dram is not None:
                dve.sem_inc(sent, 16)
            dve.wait_ge(loaded[0], 16 * NL)
            add_min(0, 0, 0)
            add_min(0, 1, 1)
            copies(dve, "dve", 0, 0, x_dve, nc.vector.tensor_copy)
            with dve.Fori(0, HEADS // 2) as it:
                for s in range(2 * U):
                    n = it * (2 * U) + s
                    h2, u2 = place(s + 2)
                    if u2 == 0:
                        dve.wait_ge(loaded[h2 % 2], (it * 2 + h2 + (2 - h2 % 2)) * (8 * NL))
                    add_min(h2 % 2, u2, n + 2)
                    h1, u1 = place(s + 1)
                    copies(dve, "dve", it * 2 + h1, u1, x_dve, nc.vector.tensor_copy)
                    if s % U == U - 1 and not columns:
                        norm(it * 2 + s // U, s // U)

        @block.scalar
        def _(act):
            def exps(bh, par, u, n):
                act.wait_ge(m_done, n + 1)
                if u == 0 and not isinstance(bh, int) and not columns:
                    act.wait_ge(norm_done, bh + 1)
                w = width[u]
                sums = {} if columns else dict(accum_out=den[:, par, BLOCK[u]:BLOCK[u] + 1])
                nc.scalar.activation(sg[:, u % 4, 0:w], sg[:, u % 4, 0:w], ACT.Exp, bias=mn[:, u % 4:u % 4 + 1],
                                     scale=-1.0, **sums).then_inc(e_done, 1)

            def copy(dst, src):
                return nc.scalar.activation(dst, src, ACT.Copy)

            def out_columns(bh, par, bank, turn):
                act.wait_ge(pv_done, bh * U + (4 if bank else 8))
                if bank:
                    act.wait_ge(col_sent[par], (turn + 1) * 32)
                nc.scalar.activation(co[:, par, bank * GROUP:(bank + 1) * GROUP], pO[bank][0:vw, :], ACT.Copy).then_inc(o_out, 1)

            exps(0, 0, 0, 0)
            exps(0, 0, 1, 1)
            copies(act, "act", 0, 0, x_act, copy)
            with act.Fori(0, HEADS // 2) as it:
                for s in range(2 * U):
                    if columns and s in (5, 9, 13):
                        out_columns(it * 2 + (s - 2) // U, (s - 2) // U, s % U // 4, it)
                    h2, u2 = place(s + 2)
                    if columns:
                        exps(it * 2 + h2, h2 % 2, u2, it * (2 * U) + s + 2)
                    h1, u1 = place(s + 1)
                    copies(act, "act", it * 2 + h1, u1, x_act, copy)
                    if not columns:
                        exps(it * 2 + h2, h2 % 2, u2, it * (2 * U) + s + 2)
                if columns:
                    out_columns(it * 2 + 1, 1, 0, it)


def l0_attn_a(nc, D, x, C, tag, out=None):
    with ExitStack() as ctx:
        h0 = ctx.enter_context(nc.sbuf_tensor(f"{tag}_h0", [P, BLOCKS, DIM], F32))
        cx = nc.dram_tensor(f"{tag}_ctx", (BATCH * DIM, SEQ), F32, kind="Internal").ap()
        den = nc.dram_tensor(f"{tag}_den", (BATCH * 16, SEQ), F32, kind="Internal").ap()
        with ExitStack() as inner:
            v_all = inner.enter_context(nc.sbuf_tensor(f"{tag}_v", [P, SEQ // P, BATCH * DIM], F32))
            pooled = inner.enter_context(nc.sbuf_tensor(f"{tag}_pooled", [P, BATCH], F32))
            NPOS = 6
            qd, kd = (nc.dram_tensor(f"{tag}_{n}", (BATCH + 1, NPOS, P, SEQ), BF16, kind="Internal").ap() for n in ("qd", "kd"))
            qm, km = (nc.dram_tensor(f"{tag}_{n}", (BATCH + 1, 3, 16, SEQ), BF16, kind="Internal").ap() for n in ("qm", "km"))
            table = nc.dram_tensor(f"{tag}_table", (65, SEQ + P), F32, kind="Internal").ap()
            mods = [nc.dram_tensor(f"{tag}_mods{n}", (BATCH, n), F32, kind="Internal").ap() for n in (256, 128)]
            l0a_project(nc, D, x, C, f"{tag}p", h0, v_all, pooled, qd, kd, qm, km)
            l0a_table(nc, D, C, f"{tag}t", pooled, mods, table)

            def dots(dram):
                return lambda bh: [(0, NPOS * 8, dram[bass.ds(bh // 16, 1), :, bass.ds(bh % 16 * 8, 8), :]
                                    .rearrange("o s c t -> (o s) c t"))]

            def singles(dram, lo):
                return lambda bh: [(lo, 3, dram[bass.ds(bh // 16, 1), :, bass.ds(bh % 16, 1), :]
                                    .rearrange("o s c t -> (o s c) t"))]

            qd_at, kd_at = dots(qd), dots(kd)
            qm_at, km_at = singles(qm, 48), singles(km, 51)
            attention_rows(
                nc, C, f"{tag}a", 8,
                q_stacks=[dict(rows=54, loads=lambda bh: qd_at(bh) + qm_at(bh), consts=[(51, 3, D["minus_ones"])])],
                k_stacks=[dict(rows=54, loads=lambda bh: kd_at(bh) + km_at(bh), consts=[(48, 3, D["ones"])])],
                products=[(0, 0)],
                table=lambda bh: bass.AP(table.tensor, bh * (SEQ + P), [[1, P], [1, SEQ]]),
                v_at=lambda bh: v_all[:, :, bass.ds(bh * 8, 8)],
                columns=(cx, den))
        l0a_output(nc, D, x, C, f"{tag}o", h0, cx, den, out)


def l0a_project(nc, D, x, C, tag, h0, v_all, pooled, qd, kd, qm, km):
    SCALE = -0.15 / 8 ** 0.5
    with ExitStack() as ctx:
        def sb(name, shape, dt=F32):
            return ctx.enter_context(nc.sbuf_tensor(f"{tag}_{name}", shape, dt))

        def pb(name, shape, dt=F32):
            return ctx.enter_context(nc.psum_tensor(f"{tag}_{name}", shape, dt))

        sem = semaphores(nc, ctx, tag)

        S = ln_scratch(sb)
        cq, ck, vw = sb("cq", [P, P]), sb("ck", [P, P]), sb("vw", [P, DIM])
        qmw, kmw = sb("qmw", [P, 32]), sb("kmw", [P, 32])
        mb, msign = sb("mb", [32, 1]), sb("msign", [32, 1])
        vb = sb("vb", [P, DIM])
        xn = sb("xn", [P, 2, GROUP_BLOCKS, DIM])
        xt, xr = sb("xt", [P, 2, GROUP]), sb("xr", [P, 2, GROUP])
        total = sb("total", [P, 2])
        f = {n: sb(f"f{n}", [rows, GROUP]) for n, rows in (("q", P), ("k", P), ("m", 32))}
        part = {n: sb(f"part{n}", [rows, 2, 3, GROUP], BF16) for n, rows in (("q", P), ("k", P), ("m", 32))}
        pT, pR, pQ, pK, pM, pV = (pb(n, [P, GROUP]) for n in ("pT", "pR", "pQ", "pK", "pM", "pV"))
        src = {"q": pQ, "k": pK, "m": f["m"]}

        w_in, zeroed = sem("weights_in"), sem("zeroed")
        ln_step, ln_ve, ln_rough = sem("ln_step"), sem("ln_ve"), sem("ln_rough")
        xn_ready, xT_done, xt_ready, h0_ready = sem("xn_ready"), sem("xT_done"), sem("xt_ready"), sem("h0_ready")
        done = {n: sem(f"{n}_done") for n in "qkmv"}
        hi, rest, mid, low = ({n: sem(f"{n}_{w}") for n in "qkm"} for w in ("hi", "rest", "mid", "low"))
        pooled_ready = sem("pooled_ready")
        m_ready, v_ready, total_ready, sent = sem("m_ready"), sem("v_ready"), sem("total_ready"), [sem("sent0"), sem("sent1")]
        NW = 8

        block = ctx.enter_context(nc.Block())
        SENDS = 2 * len(RUNS) + 2

        @block.sync
        def _(sp):
            for dst, name in ((cq, "cq_w"), (ck, "ck_w"), (vw, "v_w"), (qmw, "qmw32"), (kmw, "kmw32"), (mb, "mb32")):
                sp.dma_start(dst[:], D[f"L0_attn_a_{name}"]).then_inc(w_in, 16)
            sp.dma_start(msign[:], D["msign"]).then_inc(w_in, 16)
            sp.dma_start(vb[:], D["L0_attn_a_v_b"].broadcast_to([P, DIM])).then_inc(w_in, 16)
            for d in (qd, kd):
                sp.dma_start(d[BATCH, :, 0:8, :], D["zeros"][0:48, :].rearrange("(s c) t -> s c t", c=8)).then_inc(zeroed, 16)
            for d in (qm, km):
                sp.dma_start(d[BATCH, :, 0, :], D["zeros"][0:3, :]).then_inc(zeroed, 16)
            load_ffn_weights(sp, D, C)
            with sp.Fori(0, BATCH) as b:
                for par in (0, 1):
                    g = b * 2 + par
                    t = slice(par * GROUP, (par + 1) * GROUP)
                    sp.wait_ge(low["q"], g + 1)
                    send_parts(sp, qd, b, slice(0, P), part["q"], par, t, True, sent[par])
                    sp.wait_ge(low["k"], g + 1)
                    send_parts(sp, kd, b, slice(0, P), part["k"], par, t, False, sent[par])
                    sp.wait_ge(low["m"], g + 2)
                    for d, lo in ((qm, 0), (km, 16)):
                        sp.dma_start(d[bass.ds(b, 1), :, :, t].rearrange("o s p t -> p (o s) t"),
                                     part["m"][lo:lo + 16, par, :, :]).then_inc(sent[par], 16)
            for par in (0, 1):
                sp.wait_ge(sent[par], 16 * SENDS * (BATCH + 1))
            sp.wait_ge(zeroed, 64)

        @block.gpsimd
        def _(pool):
            def powers(turn):
                pool.wait_ge(ln_ve, turn + 1)
                nc.gpsimd.tensor_tensor(S["y"][:], S["ve"][:], C["mhalf"][:, 0:GROUP_BLOCKS], ALU.pow).then_inc(ln_rough, 1)

            powers(0)
            with pool.Fori(0, BATCH) as b:
                for par in (0, 1):
                    pool.wait_ge(xn_ready, b * 2 + par + 1)
                    nc.gpsimd.tensor_copy(h0[:, bass.ds((b * 2 + par) * GROUP_BLOCKS, GROUP_BLOCKS), :],
                                          xn[:, par, :, :]).then_inc(h0_ready, 1)
                    pool.wait_ge(h0_ready, b * 2 + par + 3)
                    powers(b * 2 + par + 1)

        @block.vector
        def _(dve):
            def split(n, g, par):
                dve.wait_ge(hi[n], g + 1)
                if n == "q":
                    nc.vector.scalar_tensor_tensor(f[n][:], src[n][:], SCALE, part[n][:, par, 0, :], ALU.mult,
                                                   ALU.subtract).then_inc(rest[n], 1)
                else:
                    nc.vector.tensor_tensor(f[n][:], src[n][:], part[n][:, par, 0, :], ALU.subtract).then_inc(rest[n], 1)

            def layernorm(gn, par):
                steps = Steps(dve, ln_step, LN_STEPS, gn)
                dve.wait_ge(h0_ready, gn + 1)
                dve.wait_ge(xT_done, gn + 1)
                ln_group_vector(nc, dve, lambda k: x[:, bass.ds((gn + 1) * GROUP_BLOCKS + k, 1), :], xn[:, par], S, steps,
                                ln_rough, gn + 1, ln_ve).then_inc(xn_ready, 1)
                steps.close()

            def split_low(n, g, par):
                dve.wait_ge(mid[n], g + 1)
                nc.vector.tensor_tensor(part[n][:, par, 2, :], f[n][:], part[n][:, par, 1, :], ALU.subtract).then_inc(low[n], 1)

            for par in (0, 1):
                dve.sem_inc(sent[par], 16 * SENDS)
            dve.wait_ge(w_in, 16 * NW)
            layernorm(0, 0)
            with dve.Fori(0, BATCH) as b:
                for par in (0, 1):
                    g = b * 2 + par
                    layernorm(g + 1, 1 - par)
                    dve.wait_ge(done["m"], g + 1)
                    dve.wait_ge(low["m"], g + 1)
                    nc.vector.tensor_scalar(f["m"][:], pM[0:32, :], mb[:, 0:1], msign[:, 0:1], ALU.add, ALU.mult).then_inc(m_ready, 1)
                    split("q", g, par)
                    split("k", g, par)
                    dve.wait_ge(done["v"], g + 1)
                    nc.vector.tensor_tensor(v_all[:, par * GROUP_BLOCKS:(par + 1) * GROUP_BLOCKS, bass.ds(b * DIM, DIM)],
                                            pV[:].rearrange("p (k d) -> p k d", d=DIM),
                                            vb[:].unsqueeze(1).broadcast_to([P, GROUP_BLOCKS, DIM]), ALU.add).then_inc(v_ready, 1)
                    split("m", g, par)
                    for n in "qkm":
                        split_low(n, g, par)
                dve.wait_ge(total_ready, b * 2 + 2)
                nc.vector.tensor_tensor(pooled[:, bass.ds(b, 1)], total[:, 0:1], total[:, 1:2], ALU.add).then_inc(pooled_ready, 1)

        @block.scalar
        def _(act):
            act.wait_ge(w_in, 16 * NW)
            def to_xt(gn, par):
                act.wait_ge(xT_done, gn + 3)
                nc.scalar.activation(xt[:, par, :], pT[:], ACT.Copy, accum_out=total[:, par:par + 1]).then_inc(total_ready, 1)
                nc.scalar.activation(xr[:, par, :], pR[:], ACT.Copy).then_inc(xt_ready, 1)

            to_xt(0, 0)
            with act.Fori(0, BATCH) as b:
                for par in (0, 1):
                    g = b * 2 + par
                    act.wait_ge(sent[par], (b + 1) * (16 * SENDS))
                    for n, scale in (("q", SCALE), ("k", 1.0)):
                        act.wait_ge(done[n], g + 1)
                        nc.scalar.activation(part[n][:, par, 0, :], src[n][:], ACT.Copy, scale=scale).then_inc(hi[n], 1)
                    act.wait_ge(m_ready, g + 2)
                    nc.scalar.activation(part["m"][:, par, 0, :], f["m"][:], ACT.Copy).then_inc(hi["m"], 1)
                    for n in "qkm":
                        act.wait_ge(rest[n], g + 2)
                        nc.scalar.activation(part[n][:, par, 1, :], f[n][:], ACT.Copy).then_inc(mid[n], 1)
                    if par == 1:
                        act.wait_ge(pooled_ready, b + 1)
                    to_xt(g + 1, 1 - par)

        @block.tensor
        def _(pe):
            def transposes(gn, par):
                pe.wait_ge(xn_ready, gn + 1)
                for k in range(GROUP_BLOCKS):
                    nc.tensor.transpose(pT[:, k * P:(k + 1) * P], xn[:, par, k, :], C["ident"][:])
                for k in range(GROUP_BLOCKS):
                    ins = nc.tensor.matmul(pR[:, k * P:(k + 1) * P], xn[:, par, k, :], C["flip"][:], start=True, stop=True)
                ins.then_inc(xT_done, 1)

            pe.wait_ge(w_in, 16 * NW)
            pe.sem_inc(h0_ready, 2)
            pe.sem_inc(xT_done, 2)
            for s in (low["m"], m_ready, v_ready, rest["q"], rest["k"], rest["m"]):
                pe.sem_inc(s, 1)
            transposes(0, 0)
            with pe.Fori(0, BATCH) as b:
                for par in (0, 1):
                    g = b * 2 + par
                    pe.wait_ge(xt_ready, g + 1)
                    pe.wait_ge(m_ready, g + 1)
                    nc.tensor.matmul(pM[0:32, :], qmw[:], xr[:, par, :], start=True, stop=False)
                    nc.tensor.matmul(pM[0:32, :], kmw[:], xt[:, par, :], start=False, stop=True).then_inc(done["m"], 1)
                    pe.wait_ge(rest["q"], g + 1)
                    nc.tensor.matmul(pQ[:], cq[:], xr[:, par, :], start=True, stop=True).then_inc(done["q"], 1)
                    pe.wait_ge(rest["k"], g + 1)
                    nc.tensor.matmul(pK[:], ck[:], xt[:, par, :], start=True, stop=True).then_inc(done["k"], 1)
                    pe.wait_ge(v_ready, g + 1)
                    for k in range(GROUP_BLOCKS):
                        ins = nc.tensor.matmul(pV[:, k * P:(k + 1) * P], xt[:, par, k * P:(k + 1) * P], vw[:], start=True, stop=True)
                    ins.then_inc(done["v"], 1)
                    transposes(g + 1, 1 - par)


def l0a_table(nc, D, C, tag, pooled, mods, table):
    H, M, R = 16, 16, 8
    BH = BATCH * H
    ROUND = 1.5 * 2 ** 23
    TWO_PI = 6.283185
    with ExitStack() as ctx:
        def sb(name, shape, dt=F32):
            return ctx.enter_context(nc.sbuf_tensor(f"{tag}_{name}", shape, dt))

        def pb(name, shape, dt=F32):
            return ctx.enter_context(nc.psum_tensor(f"{tag}_{name}", shape, dt))

        sem = semaphores(nc, ctx, tag)

        fp = sb("fp", [3, H * P])
        pos = sb("pos", [3, SEQ])
        win = sb("win", [BH, SEQ])
        amps = sb("amps", [P, H])
        gmw = sb("gmw", [P, 384])
        gmb = sb("gmb", [BH, M + R])
        basis = sb("basis", [BH, R, M])
        spread = sb("spread", [M, P])
        pl = sb("pl", [P, BATCH])
        g4 = sb("g4", [BATCH, 384])
        gl = sb("gl", [BH, M + R])
        soft, hard, t16 = sb("soft", [BH, M]), sb("hard", [BH, M]), sb("t16", [BH, M])
        top, one, two = sb("top", [BH, 8]), sb("one", [BH, 1]), sb("two", [BH, 1])
        wT = sb("wT", [M, BH])
        L = sb("L", [P, H, BH])
        rn, fr = sb("rn", [P, 2, SEQ]), sb("fr", [P, 3, SEQ])
        sf, hd = sb("sf", [BH, SEQ]), sb("hd", [BH, SEQ])
        tb = sb("tb", [BH, SEQ + P])
        pU = [pb(f"pU{i}", [P, SEQ]) for i in range(2)]
        pN = pb("pN", [P, SEQ])
        pG, pW = pb("pG", [P, GROUP]), pb("pW", [P, GROUP])

        w_in, zero, pooled_in, g_done, g_out, g_back, g_in = (sem(n) for n in
            ("weights_in", "zero", "pooled_in", "g_done", "g_out", "g_back", "g_in"))
        st, e_in, e_out, wt_done, wt_in, wx_done, L_ready = (sem(n) for n in
            ("step", "e_in", "e_out", "wt_done", "wt_in", "wx_done", "L_ready"))
        u_done, f_step, f_ready, s_ready, n_done, sg_ready, t_ready, stored = (sem(n) for n in
            ("u_done", "f_step", "f_ready", "s_ready", "n_done", "sg_ready", "t_ready", "stored"))
        NW = 8

        block = ctx.enter_context(nc.Block())

        @block.sync
        def _(sp):
            for dst, name in ((fp, "L0_attn_a_fp"), (pos, "positions"), (win, "window"), (amps, "L0_attn_a_ampsT"),
                              (gmw, "L0_attn_a_gmw"), (gmb, "L0_attn_a_gmb"), (basis, "L0_attn_a_basis"), (spread, "spread")):
                sp.dma_start(dst[:], D[name]).then_inc(w_in, 16)
            sp.wait_ge(g_out, 1)
            sp.dma_start(mods[0], g4[:, 0:256]).then_inc(g_back, 16)
            sp.dma_start(mods[1], g4[:, 256:384]).then_inc(g_back, 16)
            sp.wait_ge(g_back, 32)
            sp.dma_start(gl[:, 0:M], mods[0].rearrange("b (h m) -> (b h) m", m=M)).then_inc(g_in, 16)
            sp.dma_start(gl[:, M:M + R], mods[1].rearrange("b (h r) -> (b h) r", r=R)).then_inc(g_in, 16)
            sp.wait_ge(t_ready, 2)
            sp.dma_start(table[0:BH, :], tb[:]).then_inc(stored, 16)
            sp.dma_start(table[BH:BH + 1, :], tb[0:1, :]).then_inc(stored, 16)
            sp.wait_ge(stored, 32)

        @block.gpsimd
        def _(pool):
            nc.gpsimd.memset(L[:], 0.0).then_inc(zero, 1)
            nc.gpsimd.memset(tb[:, SEQ:], 1e30).then_inc(t_ready, 1)

        @block.scalar
        def _(act):
            act.wait_ge(w_in, 16 * NW)
            nc.scalar.activation(pl[:], pooled[:], ACT.Copy, scale=1.0 / SEQ).then_inc(pooled_in, 1)
            act.wait_ge(g_done, 1)
            nc.scalar.activation(g4[:], pG[0:BATCH, 0:384], ACT.Copy).then_inc(g_out, 1)
            act.wait_ge(e_in, 1)
            nc.scalar.activation(soft[:], t16[:], ACT.Exp).then_inc(e_out, 1)
            act.wait_ge(wt_done, 1)
            nc.scalar.activation(wT[:], pG[0:M, 0:BH], ACT.Copy).then_inc(wt_in, 1)
            for h in range(H):
                act.wait_ge(f_ready, h + 1)
                nc.scalar.activation(fr[:, h % 3, :], fr[:, h % 3, :], ACT.Sin, scale=TWO_PI).then_inc(s_ready, 1)
            act.wait_ge(n_done, H)
            nc.scalar.activation(sf[:], pN[0:BH, :], ACT.Sigmoid, scale=6.0).then_inc(sg_ready, 1)

        @block.vector
        def _(dve):
            def reduce_range(h):
                dve.wait_ge(u_done, h + 1)
                nc.vector.tensor_scalar(rn[:, h % 2, :], pU[h % 2][:], ROUND, -ROUND, ALU.add, ALU.add).then_inc(f_step, 1)
                dve.wait_ge(f_step, h + 1)
                if h >= 3:
                    dve.wait_ge(n_done, h - 2)
                nc.vector.tensor_tensor(fr[:, h % 3, :], pU[h % 2][:], rn[:, h % 2, :], ALU.subtract).then_inc(f_ready, 1)

            steps = Steps(dve, st, 0, 0)
            dve.wait_ge(w_in, 16 * NW)
            reduce_range(0)
            reduce_range(1)
            dve.wait_ge(g_in, 32)
            steps.done(nc.vector.tensor_tensor(gl[:], gl[:], gmb[:], ALU.add))
            for r in range(R):
                steps.done(nc.vector.scalar_tensor_tensor(gl[:, 0:M], basis[:, r, :], gl[:, M + r:M + r + 1], gl[:, 0:M],
                                                          ALU.mult, ALU.add))
            steps.done(nc.vector.tensor_reduce(one[:], gl[:, 0:M], AX.X, ALU.max))
            nc.vector.tensor_scalar(t16[:], gl[:, 0:M], one[:, 0:1], None, ALU.subtract).then_inc(e_in, 1)
            dve.wait_ge(e_out, 1)
            steps.done(nc.vector.tensor_reduce(one[:], soft[:], AX.X, ALU.add))
            steps.done(nc.vector.reciprocal(two[:], one[:]))
            steps.done(nc.vector.tensor_scalar(soft[:], soft[:], two[:, 0:1], None, ALU.mult))
            steps.done(nc.vector.max(top[:], soft[:]))
            steps.done(nc.vector.tensor_scalar(hard[:], soft[:], top[:, 7:8], None, ALU.is_ge))
            steps.done(nc.vector.tensor_reduce(one[:], hard[:], AX.X, ALU.add))
            steps.done(nc.vector.tensor_scalar(one[:], one[:], 1e-8, None, ALU.add))
            steps.done(nc.vector.reciprocal(two[:], one[:]))
            steps.done(nc.vector.tensor_scalar(hard[:], hard[:], two[:, 0:1], None, ALU.mult))
            steps.done(nc.vector.tensor_tensor(soft[:], soft[:], hard[:], ALU.subtract))
            steps.done(nc.vector.tensor_tensor(soft[:], hard[:], soft[:], ALU.add))
            assert steps.k == 21
            dve.wait_ge(wx_done, 1)
            dve.wait_ge(zero, 1)
            diag = bass.AP(L[:].tensor, L[:].offset, [list(L[:].ap[0]), [BH + 1, H], [H, BATCH]])
            nc.vector.tensor_tensor(diag, pW[:, 0:BH].rearrange("p (b h) -> p h b", h=H), bcast(amps[:], BATCH),
                                    ALU.mult).then_inc(L_ready, 1)
            for h in range(2, H):
                reduce_range(h)
            dve.wait_ge(n_done, H)
            dve.wait_ge(sg_ready, 1)
            nc.vector.tensor_scalar(hd[:], pN[0:BH, :], 0.0, None, ALU.is_gt).then_inc(f_step, 1)
            dve.wait_ge(f_step, H + 1)
            nc.vector.tensor_tensor(sf[:], sf[:], hd[:], ALU.subtract).then_inc(f_step, 1)
            dve.wait_ge(f_step, H + 2)
            nc.vector.tensor_tensor(sf[:], hd[:], sf[:], ALU.add).then_inc(f_step, 1)
            dve.wait_ge(f_step, H + 3)
            nc.vector.tensor_tensor(tb[:, 0:SEQ], sf[:], win[:], ALU.mult).then_inc(t_ready, 1)

        @block.tensor
        def _(pe):
            def phases(h):
                if h >= 2:
                    pe.wait_ge(f_ready, h - 1)
                for c in (0, GROUP):
                    ins = nc.tensor.matmul(pU[h % 2][:, c:c + GROUP], fp[:, h * P:(h + 1) * P], pos[:, c:c + GROUP],
                                           start=True, stop=True)
                ins.then_inc(u_done, 1)

            pe.wait_ge(w_in, 16 * NW)
            phases(0)
            phases(1)
            pe.wait_ge(pooled_in, 1)
            nc.tensor.matmul(pG[0:BATCH, 0:384], pl[:], gmw[:], start=True, stop=True).then_inc(g_done, 1)
            pe.wait_ge(st, 21)
            nc.tensor.transpose(pG[0:M, 0:BH], soft[:], C["ident"][0:BH, 0:BH]).then_inc(wt_done, 1)
            pe.wait_ge(wt_in, 1)
            nc.tensor.matmul(pW[:, 0:BH], spread[:], wT[:], start=True, stop=True).then_inc(wx_done, 1)
            pe.wait_ge(L_ready, 1)
            for h in range(H):
                if h + 2 < H:
                    phases(h + 2)
                pe.wait_ge(s_ready, h + 1)
                for c in (0, GROUP):
                    ins = nc.tensor.matmul(pN[0:BH, c:c + GROUP], L[:, h, :], fr[:, h % 3, c:c + GROUP],
                                           start=(h == 0), stop=(h == H - 1))
                ins.then_inc(n_done, 1)


def divided_columns(sp, cx, den, dall, cg, dn, D_in, cg_in, c_in, rd_done):
    flat = den.rearrange("r (c t) -> (r c) t", t=GROUP)
    sp.dma_start(dall[:], flat).then_inc(D_in, 16)
    sp.wait_ge(rd_done, 1)
    sp.dma_start(flat, dall[:]).then_inc(D_in, 16)
    sp.wait_ge(D_in, 32)
    with sp.Fori(0, BATCH) as b:
        for par in (0, 1):
            sp.wait_ge(c_in, b * 2 + par + 1)
            t = slice(par * GROUP, (par + 1) * GROUP)
            sp.dma_start(cg[:, par, :], cx[bass.ds(b * DIM, DIM), t]).then_inc(cg_in[par], 16)
            sp.dma_start(dn[:, par, :], den[bass.ds(b * 16, 16), t]).then_inc(cg_in[par], 16)


def l0a_output(nc, D, x, C, tag, h0, cx, den, out=None):
    FT = 4
    with ExitStack() as ctx:
        def sb(name, shape, dt=F32):
            return ctx.enter_context(nc.sbuf_tensor(f"{tag}_{name}", shape, dt))

        def pb(name, shape, dt=F32):
            return ctx.enter_context(nc.psum_tensor(f"{tag}_{name}", shape, dt))

        sem = semaphores(nc, ctx, tag)

        SA = ln_scratch(lambda n, *a: sb(f"A_{n}", *a))
        SB = ln_scratch(lambda n, *a: sb(f"B_{n}", *a))
        ow, w1, w2 = sb("ow", [P, DIM]), sb("w1", [P, FT * P]), sb("w2", [P, FT, DIM])
        ob, b1, b2 = sb("ob", [P, DIM]), sb("b1", [P, FT]), sb("b2", [P, 1])
        g1, c1, g2, c2 = (sb(n, [P, DIM]) for n in ("g1", "c1", "g2", "c2"))
        B4 = [P, GROUP_BLOCKS, DIM]
        rA, uA, rB, uB = (sb(n, B4) for n in ("rA", "uA", "rB", "uB"))
        h = sb("h", [P, 2] + B4[1:])
        sel = sb("sel", [16, P])
        dall = sb("dall", [P, GROUP])
        cg, dn = sb("cg", [P, 2, GROUP]), sb("dn", [16, 2, GROUP])
        cT, aT, hT, fT = (sb(n, [P, GROUP]) for n in ("cT", "aT", "hT", "fT"))
        hid = sb("hid", [P, FT, GROUP])
        pC, pA, pR, pT, pH0, pH1, pF, pB = (pb(n, [P, GROUP]) for n in ("pC", "pA", "pR", "pT", "pH0", "pH1", "pF", "pB"))
        pH = [pH0, pH1]
        w_in, stored, x_done = sem("weights_in"), sem("stored"), sem("x_done")
        stA, stB, veA, veB, roughA, roughB = (sem(n) for n in ("stA", "stB", "veA", "veB", "roughA", "roughB"))
        D_in, rd_done, cg_in = sem("D_in"), sem("rd_done"), [sem("cg_in0"), sem("cg_in1")]
        c_done, c_in, a_done, a_in, aB_done = (sem(n) for n in ("c_done", "c_in", "a_done", "a_in", "aB_done"))
        h_ready, hT_done, hT_in, u_done, u_in, f_done, f_in, fB_done = (sem(n) for n in
            ("h_ready", "hT_done", "hT_in", "u_done", "u_in", "f_done", "f_in", "fB_done"))
        NW = 11
        A_STEPS, B_STEPS = LN_STEPS + 3, LN_STEPS + 4
        block = ctx.enter_context(nc.Block())

        def groups(eng, step):
            with eng.Fori(0, BATCH - 1) as b:
                for par in (0, 1):
                    step(b * 2 + par, par, True)
            step(GROUPS - 2, 0, True)
            step(GROUPS - 1, 1, False)

        @block.sync
        def _(sp):
            for dst, name in ((ow, "out_w"), (w1, "ffn_w1"), (b1, "ffn_b1"), (b2, "ffn_b2")):
                sp.dma_start(dst[:], D[f"L0_attn_a_{name}"]).then_inc(w_in, 16)
            sp.dma_start(w2[:], D["L0_attn_a_ffn_w2"].rearrange("(t p) n -> p t n", p=P)).then_inc(w_in, 16)
            sp.dma_start(sel[:], D["spread"]).then_inc(w_in, 16)
            for dst, name in ((ob, "out_b"), (g1, "ln1_g"), (c1, "ln1_b"), (g2, "ln2_g"), (c2, "ln2_b")):
                sp.dma_start(dst[:], D[f"L0_attn_a_{name}"].broadcast_to([P, DIM])).then_inc(w_in, 16)
            divided_columns(sp, cx, den, dall, cg, dn, D_in, cg_in, c_in, rd_done)
            if out is not None:
                store_x(sp, out, x, x_done, stored)

        @block.gpsimd
        def _(pool):
            def power(S, ve, rough, g):
                pool.wait_ge(ve, g + 1)
                nc.gpsimd.tensor_tensor(S["y"][:], S["ve"][:], C["mhalf"][:, 0:GROUP_BLOCKS], ALU.pow).then_inc(rough, 1)

            def step(g, par, more):
                if more:
                    power(SA, veA, roughA, g + 1)
                power(SB, veB, roughB, g)

            power(SA, veA, roughA, 0)
            groups(pool, step)

        @block.vector
        def _(dve):
            def spread(t):
                return t[:].unsqueeze(1).broadcast_to(B4)

            def blocks(bank):
                return bank[:].rearrange("p (k d) -> p k d", d=DIM)

            def make_h(g, par):
                steps = Steps(dve, stA, A_STEPS, g)
                dve.wait_ge(cg_in[par], (g // 2 + 1) * 32)
                dve.wait_ge(c_done, g + 1)
                nc.vector.tensor_tensor(cT[:], cg[:, par, :], pC[:], ALU.mult).then_inc(c_in, 1)
                dve.wait_ge(a_done, g + 1)
                nc.vector.tensor_tensor(blocks(aT), blocks(pA), spread(ob), ALU.add).then_inc(a_in, 1)
                dve.wait_ge(aB_done, g + 1)
                steps.done(nc.vector.tensor_tensor(rA[:], blocks(pR), h0[:, bass.ds(g * GROUP_BLOCKS, GROUP_BLOCKS), :], ALU.add))
                steps.done(ln_group_vector(nc, dve, lambda k: rA[:, k, :], uA, SA, steps, roughA, g + 1, veA))
                steps.done(nc.vector.tensor_tensor(uA[:], uA[:], spread(g1), ALU.mult))
                nc.vector.tensor_tensor(h[:, par], uA[:], spread(c1), ALU.add).then_inc(h_ready, 1)
                steps.close()

            def step(g, par, more):
                if more:
                    make_h(g + 1, 1 - par)
                steps = Steps(dve, stB, B_STEPS, g)
                xs = x[:, bass.ds((g + 1) * GROUP_BLOCKS, GROUP_BLOCKS), :]
                dve.wait_ge(fB_done, g + 1)
                dve.wait_ge(h_ready, g + 1)
                steps.done(nc.vector.tensor_tensor(rB[:], blocks(pB), h[:, par], ALU.add))
                steps.done(ln_group_vector(nc, dve, lambda k: rB[:, k, :], uB, SB, steps, roughB, g + 1, veB))
                steps.done(nc.vector.tensor_tensor(uB[:], uB[:], spread(g2), ALU.mult))
                steps.done(nc.vector.tensor_tensor(uB[:], uB[:], spread(c2), ALU.add))
                nc.vector.tensor_tensor(xs, xs, uB[:], ALU.add).then_inc(x_done, 1)
                steps.close()

            dve.wait_ge(D_in, 16)
            nc.vector.reciprocal(dall[:], dall[:]).then_inc(rd_done, 1)
            dve.wait_ge(w_in, 16 * NW)
            make_h(0, 0)
            groups(dve, step)

        @block.scalar
        def _(act):
            def step(g, par, more):
                act.wait_ge(hT_done, g + 1)
                nc.scalar.activation(hT[:], pT[:], ACT.Copy).then_inc(hT_in, 1)
                for t in range(FT):
                    act.wait_ge(u_done, g * FT + t + 1)
                    nc.scalar.activation(hid[:, t, :], pH[t % 2][:], ACT.Gelu, bias=b1[:, t:t + 1]).then_inc(u_in, 1)
                act.wait_ge(f_done, g + 1)
                nc.scalar.activation(fT[:], pF[:], ACT.Identity, bias=b2[:, 0:1]).then_inc(f_in, 1)

            act.wait_ge(w_in, 16 * NW)
            groups(act, step)

        @block.tensor
        def _(pe):
            def divisors(g, par):
                pe.wait_ge(cg_in[par], (g // 2 + 1) * 32)
                nc.tensor.matmul(pC[:], sel[:], dn[:, par, :], start=True, stop=True).then_inc(c_done, 1)

            def project(g):
                pe.wait_ge(c_in, g + 3)
                for k in range(GROUP_BLOCKS):
                    ins = nc.tensor.matmul(pA[:, k * P:(k + 1) * P], cT[:, k * P:(k + 1) * P], ow[:], start=True, stop=True)
                ins.then_inc(a_done, 1)

            def turn_back(g):
                pe.wait_ge(a_in, g + 1)
                nc.tensor.matmul(pR[:], C["flip"][:], aT[:], start=True, stop=True).then_inc(aB_done, 1)

            def step(g, par, more):
                pe.wait_ge(h_ready, g + 1)
                for k in range(GROUP_BLOCKS):
                    ins = nc.tensor.transpose(pT[:, k * P:(k + 1) * P], h[:, par, k, :], C["ident"][:])
                ins.then_inc(hT_done, 1)
                if more:
                    divisors(g + 1, 1 - par)
                pe.wait_ge(hT_in, g + 1)
                for t in range(FT):
                    if t >= 2:
                        pe.wait_ge(u_in, g * FT + t - 1)
                    nc.tensor.matmul(pH[t % 2][:], w1[:, t * P:(t + 1) * P], hT[:], start=True, stop=True).then_inc(u_done, 1)
                if more:
                    project(g + 1)
                for t in range(FT):
                    pe.wait_ge(u_in, g * FT + t + 1)
                    ins = nc.tensor.matmul(pF[:], w2[:, t, :], hid[:, t, :], start=(t == 0), stop=(t == FT - 1))
                    if t == 0 and more:
                        turn_back(g + 1)
                ins.then_inc(f_done, 1)
                pe.wait_ge(f_in, g + 1)
                pe.wait_ge(x_done, g + 2)
                for k in range(GROUP_BLOCKS):
                    ins = nc.tensor.transpose(pB[:, k * P:(k + 1) * P], fT[:, k * P:(k + 1) * P], C["ident"][:])
                ins.then_inc(fB_done, 1)

            pe.wait_ge(w_in, 16 * NW)
            pe.sem_inc(c_in, 2)
            pe.sem_inc(x_done, 2)
            divisors(0, 0)
            project(0)
            turn_back(0)
            groups(pe, step)


def l1_attn_b(nc, D, x, C, tag, out=None):
    HD = 64
    with ExitStack() as ctx:
        ks = [ctx.enter_context(nc.sbuf_tensor(f"{tag}_k{i}", [P, (BATCH + 1) * SEQ], BF16)) for i in range(3)]
        qd = nc.dram_tensor(f"{tag}_qd", (BATCH + 1, 3, 16 * HD, SEQ), BF16, kind="Internal").ap()
        cx = nc.dram_tensor(f"{tag}_ctx", (BATCH * 8, P, SEQ // P * 2 * HD), F32, kind="Internal").ap()
        table = nc.dram_tensor(f"{tag}_table", (16, SEQ + P), F32, kind="Internal").ap()
        with ExitStack() as inner:
            v_all = inner.enter_context(nc.sbuf_tensor(f"{tag}_v", [P, SEQ // P, BATCH * HD], F32))
            l1b_project(nc, D, x, C, f"{tag}p", v_all, ks, qd, table)

            def q_part(p):
                return lambda bh: (qd[bass.ds(bh // 16, 1), p, bass.ds(bh % 16 * HD, HD), :].rearrange("o c t -> (o c) t"))

            hi, mid, low = q_part(0), q_part(1), q_part(2)
            attention_rows(
                nc, C, f"{tag}a", HD,
                q_stacks=[dict(rows=P, loads=lambda bh: [(0, HD, hi(bh)), (HD, HD, mid(bh))]),
                          dict(rows=P, loads=lambda bh: [(0, HD, hi(bh)), (HD, HD, low(bh))])],
                k_stacks=[dict(rows=P, resident=k) for k in ks],
                products=[(0, 0), (0, 1), (1, 2)],
                table=lambda bh: bass.AP(table.tensor, bh % 16 * (SEQ + P), [[1, P], [1, SEQ]]),
                v_at=lambda bh: v_all[:, :, bass.ds(bh // 16 * HD, HD)],
                out_dram=lambda pair: cx[bass.ds(pair, 1), :, :].rearrange("o p e -> (o p) e"))
        l1b_output(nc, D, x, C, f"{tag}o", cx, out)


def l1b_project(nc, D, x, C, tag, v_all, ks, qd, table):
    HD, QT = 64, 8
    NB = 4
    SCALE = -0.125
    with ExitStack() as ctx:
        def sb(name, shape, dt=F32):
            return ctx.enter_context(nc.sbuf_tensor(f"{tag}_{name}", shape, dt))

        def pb(name, shape, dt=F32):
            return ctx.enter_context(nc.psum_tensor(f"{tag}_{name}", shape, dt))

        sem = semaphores(nc, ctx, tag)

        S = ln_scratch(sb)
        wq, wk, wv = sb("wq", [P, QT * P]), sb("wk", [P, P]), sb("wv", [P, HD])
        rel, tb = sb("rel", [16, SEQ]), sb("tb", [16, SEQ + P])
        xn = sb("xn", [P, 2, GROUP_BLOCKS, DIM])
        xt, xr = sb("xt", [P, GROUP]), sb("xr", [P, GROUP])
        fk, fq = sb("fk", [P, GROUP]), sb("fq", [P, 2, GROUP])
        part = sb("part", [P, NB, 3, GROUP], BF16)
        pT, pR, pK, pV = (pb(n, [P, GROUP]) for n in ("pT", "pR", "pK", "pV"))
        pQ = [pb(f"pQ{i}", [P, GROUP]) for i in range(2)]

        w_in, zeroed, t_ready = sem("weights_in"), sem("zeroed"), sem("t_ready")
        ln_step, ln_ve, ln_rough = sem("ln_step"), sem("ln_ve"), sem("ln_rough")
        xn_ready, xT_done, xt_ready = sem("xn_ready"), sem("xT_done"), sem("xt_ready")
        k_copied = sem("k_copied")
        k_done, k_hi, k_rest, k_mid, k_low, v_done, v_ready = (sem(n) for n in
            ("k_done", "k_hi", "k_rest", "k_mid", "k_low", "v_done", "v_ready"))
        q_done, q_hi, q_rest, q_mid, q_low = (sem(n) for n in ("q_done", "q_hi", "q_rest", "q_mid", "q_low"))
        sent = [sem(f"sent{i}") for i in range(NB)]
        NW = 4

        block = ctx.enter_context(nc.Block())

        @block.sync
        def _(sp):
            for dst, name in ((wk, "Wkk"), (wv, "Wv"), (rel, "rel_by_distance"), (wq, "Wq")):
                sp.dma_start(dst[:], D[f"L1_attn_b_{name}"]).then_inc(w_in, 16)
            for p in range(3):
                sp.dma_start(qd[BATCH, p, 0:HD, :], D["zeros"]).then_inc(zeroed, 16)
            sp.wait_ge(t_ready, 2)
            sp.dma_start(table, tb[:]).then_inc(zeroed, 16)
            with sp.Fori(0, BATCH) as b:
                for par in (0, 1):
                    for t in range(QT):
                        sp.wait_ge(q_low, (b * 2 + par) * QT + t + 3)
                        sp.dma_start(qd[bass.ds(b, 1), :, t * P:(t + 1) * P, par * GROUP:(par + 1) * GROUP]
                                     .rearrange("o s p t -> p (o s) t"), part[:, t % NB, :, :]).then_inc(sent[t % NB], 16)
            for i in range(NB):
                sp.wait_ge(sent[i], 16 * (1 + GROUPS * QT // NB))
            sp.wait_ge(zeroed, 64)

        @block.gpsimd
        def _(pool):
            def powers(turn):
                pool.wait_ge(ln_ve, turn + 1)
                nc.gpsimd.tensor_tensor(S["y"][:], S["ve"][:], C["mhalf"][:, 0:GROUP_BLOCKS], ALU.pow).then_inc(ln_rough, 1)

            nc.gpsimd.memset(tb[:, SEQ:], 1e30).then_inc(t_ready, 1)
            for k in ks:
                nc.gpsimd.memset(k[:, BATCH * SEQ:], 0.0)
            powers(0)
            with pool.Fori(0, GROUPS) as g:
                pool.wait_ge(k_hi, g + 1)
                at = g * GROUP
                nc.gpsimd.tensor_copy(ks[2][HD:P, bass.ds(at, GROUP)], ks[0][HD:P, bass.ds(at, GROUP)]).then_inc(k_copied, 1)
                pool.wait_ge(k_copied, g + 1)
                powers(g + 1)

        @block.vector
        def _(dve):
            def src(gn):
                return lambda k: x[:, bass.ds((gn + 1) * GROUP_BLOCKS + k, 1), :]

            def ln_first(steps, gn):
                for k in range(GROUP_BLOCKS):
                    ins = nc.vector.bn_stats(S["st"][:, k, :], src(gn)(k))
                steps.done(ins)
                ln_variance(nc, S, steps, ln_ve)

            def ln_second(steps, gn, par):
                ln_newton(nc, dve, S, steps, ln_rough, gn + 1)
                dve.wait_ge(xT_done, gn + 1)
                ln_apply(nc, src(gn), xn[:, par], S).then_inc(xn_ready, 1)
                steps.close()

            dve.wait_ge(w_in, 16 * NW)
            lns = Steps(dve, ln_step, LN_STEPS, 0)
            ln_first(lns, 0)
            ln_second(lns, 0, 0)
            nc.vector.tensor_scalar(tb[:, 0:SEQ], rel[:], -8.0, None, ALU.mult).then_inc(t_ready, 1)
            with dve.Fori(0, BATCH) as b:
                for par in (0, 1):
                    g = b * 2 + par
                    at = g * GROUP
                    lns = Steps(dve, ln_step, LN_STEPS, g + 1)
                    ln_first(lns, g + 1)
                    dve.wait_ge(k_hi, g + 1)
                    nc.vector.tensor_tensor(fk[:], pK[:], ks[0][:, bass.ds(at, GROUP)], ALU.subtract).then_inc(k_rest, 1)
                    dve.wait_ge(v_done, g + 1)
                    nc.vector.tensor_copy(v_all[:, par * GROUP_BLOCKS:(par + 1) * GROUP_BLOCKS, bass.ds(b * HD, HD)],
                                          pV[:, 0:GROUP_BLOCKS * HD].rearrange("p (k d) -> p k d", d=HD)).then_inc(v_ready, 1)
                    dve.wait_ge(k_mid, g + 1)
                    nc.vector.tensor_tensor(ks[2][0:HD, bass.ds(at, GROUP)], fk[0:HD, :], ks[1][0:HD, bass.ds(at, GROUP)],
                                            ALU.subtract).then_inc(k_low, 1)
                    for t in range(QT + 1):
                        n = g * QT + t
                        if t < QT:
                            dve.wait_ge(q_hi, n + 1)
                            dve.wait_ge(q_low, n + 1)
                            nc.vector.scalar_tensor_tensor(fq[:, t % 2, :], pQ[t % 2][:], SCALE, part[:, t % NB, 0, :],
                                                           ALU.mult, ALU.subtract).then_inc(q_rest, 1)
                        if t == 1:
                            ln_second(lns, g + 1, 1 - par)
                        if t >= 1:
                            dve.wait_ge(q_mid, n)
                            u = (t - 1) % NB
                            nc.vector.tensor_tensor(part[:, u, 2, :], fq[:, u % 2, :], part[:, u, 1, :],
                                                    ALU.subtract).then_inc(q_low, 1)

        @block.scalar
        def _(act):
            def to_xt(gn):
                act.wait_ge(xT_done, gn + 3)
                nc.scalar.activation(xt[:], pT[:], ACT.Copy)
                nc.scalar.activation(xr[:], pR[:], ACT.Copy).then_inc(xt_ready, 1)

            act.wait_ge(w_in, 16 * NW)
            to_xt(0)
            with act.Fori(0, BATCH) as b:
                for par in (0, 1):
                    g = b * 2 + par
                    at = g * GROUP
                    act.wait_ge(k_done, g + 1)
                    nc.scalar.activation(ks[0][:, bass.ds(at, GROUP)], pK[:], ACT.Copy).then_inc(k_hi, 1)
                    act.wait_ge(k_rest, g + 1)
                    nc.scalar.activation(ks[1][:, bass.ds(at, GROUP)], fk[:], ACT.Copy).then_inc(k_mid, 1)
                    for t in range(QT + 1):
                        n = g * QT + t
                        if t < QT:
                            act.wait_ge(q_done, n + 1)
                            act.wait_ge(sent[t % NB], (g * (QT // NB) + t // NB + 1) * 16)
                            nc.scalar.activation(part[:, t % NB, 0, :], pQ[t % 2][:], ACT.Copy, scale=SCALE).then_inc(q_hi, 1)
                        if t >= 1:
                            act.wait_ge(q_rest, n + 2)
                            u = (t - 1) % NB
                            nc.scalar.activation(part[:, u, 1, :], fq[:, u % 2, :], ACT.Copy).then_inc(q_mid, 1)
                    to_xt(g + 1)

        @block.tensor
        def _(pe):
            def transposes(gn, par):
                pe.wait_ge(xn_ready, gn + 1)
                for k in range(GROUP_BLOCKS):
                    nc.tensor.transpose(pT[:, k * P:(k + 1) * P], xn[:, par, k, :], C["ident"][:])
                for k in range(GROUP_BLOCKS):
                    ins = nc.tensor.matmul(pR[:, k * P:(k + 1) * P], xn[:, par, k, :], C["flip"][:], start=True, stop=True)
                ins.then_inc(xT_done, 1)

            pe.wait_ge(w_in, 16 * NW)
            pe.sem_inc(xT_done, 2)
            pe.sem_inc(q_rest, 2)
            pe.sem_inc(q_low, 2)
            for i in range(NB):
                pe.sem_inc(sent[i], 16)
            transposes(0, 0)
            with pe.Fori(0, BATCH) as b:
                for par in (0, 1):
                    g = b * 2 + par
                    pe.wait_ge(xt_ready, g + 1)
                    nc.tensor.matmul(pK[:], wk[:], xt[:], start=True, stop=True).then_inc(k_done, 1)
                    for k in range(GROUP_BLOCKS):
                        ins = nc.tensor.matmul(pV[:, k * HD:(k + 1) * HD], xt[:, k * P:(k + 1) * P], wv[:], start=True, stop=True)
                    ins.then_inc(v_done, 1)
                    for t in range(QT):
                        pe.wait_ge(q_rest, g * QT + t + 1)
                        nc.tensor.matmul(pQ[t % 2][:], wq[:, t * P:(t + 1) * P], xr[:], start=True, stop=True).then_inc(q_done, 1)
                    transposes(g + 1, 1 - par)


def l1b_output(nc, D, x, C, tag, cx, out=None):
    T = 8
    with ExitStack() as ctx:
        def sb(name, shape, dt=F32):
            return ctx.enter_context(nc.sbuf_tensor(f"{tag}_{name}", shape, dt))

        def pb(name, shape, dt=F32):
            return ctx.enter_context(nc.psum_tensor(f"{tag}_{name}", shape, dt))

        sem = semaphores(nc, ctx, tag)

        wo, bo = sb("wo", [P, T, DIM]), sb("bo", [P, DIM])
        cg = sb("cg", [P, 2, T, GROUP_BLOCKS, P])
        cT = sb("cT", [P, T, GROUP])
        yr = sb("yr", [P, GROUP])
        pC = [pb(f"pC{i}", [P, GROUP]) for i in range(4)]
        pY, pB = pb("pY", [P, GROUP]), pb("pB", [P, GROUP])
        w_in, stored, x_done = sem("weights_in"), sem("stored"), sem("x_done")
        cg_in, c_act, c_dve, c_done = [sem("cg_in0"), sem("cg_in1")], sem("c_act"), sem("c_dve"), sem("c_done")
        y_done, y_in, b_done = sem("y_done"), sem("y_in"), sem("b_done")
        block = ctx.enter_context(nc.Block())

        @block.sync
        def _(sp):
            sp.dma_start(wo[:], D["L1_attn_b_Wout"].rearrange("(t p) d -> p t d", p=P)).then_inc(w_in, 16)
            sp.dma_start(bo[:], D["L1_attn_b_bout"].broadcast_to([P, DIM])).then_inc(w_in, 16)
            with sp.Fori(0, BATCH) as b:
                for par in (0, 1):
                    sp.wait_ge(c_done, (b * 2 + par + 1) * T)
                    sp.dma_start(cg[:, par].rearrange("p t k e -> p t (k e)"),
                                 cx[bass.ds(b * T, T), :, par * GROUP_BLOCKS * P:(par + 1) * GROUP_BLOCKS * P]
                                 .rearrange("t p e -> p t e")).then_inc(cg_in[par], 16)
            if out is not None:
                store_x(sp, out, x, x_done, stored)

        @block.vector
        def _(dve):
            dve.wait_ge(w_in, 32)
            with dve.Fori(0, GROUPS) as g:
                for t in range(1, T, 2):
                    dve.wait_ge(c_done, (g + 2) * T + t + 1)
                    nc.vector.tensor_copy(cT[:, t, :], pC[t % 4][:]).then_inc(c_dve, 1)
                dve.wait_ge(y_done, g + 1)
                nc.vector.tensor_tensor(yr[:].rearrange("p (k d) -> p k d", d=DIM), pY[:].rearrange("p (k d) -> p k d", d=DIM),
                                        bo[:].unsqueeze(1).broadcast_to([P, GROUP_BLOCKS, DIM]), ALU.add).then_inc(y_in, 1)
                dve.wait_ge(b_done, g + 1)
                xs = x[:, bass.ds((g + 1) * GROUP_BLOCKS, GROUP_BLOCKS), :]
                nc.vector.tensor_tensor(xs, xs, pB[:].rearrange("p (k d) -> p k d", d=DIM), ALU.add).then_inc(x_done, 1)

        @block.scalar
        def _(act):
            with act.Fori(0, GROUPS) as g:
                for t in range(0, T, 2):
                    act.wait_ge(c_done, (g + 2) * T + t + 1)
                    nc.scalar.activation(cT[:, t, :], pC[t % 4][:], ACT.Copy).then_inc(c_act, 1)

        @block.tensor
        def _(pe):
            pe.wait_ge(w_in, 32)
            pe.sem_inc(c_done, 2 * T)
            pe.sem_inc(x_done, 2)
            pe.sem_inc(c_act, 2)
            pe.sem_inc(c_dve, 2)
            with pe.Fori(0, BATCH) as b:
                for par in (0, 1):
                    g = b * 2 + par
                    pe.wait_ge(cg_in[par], 16 * (b + 1))
                    for t in range(T):
                        pe.wait_ge((c_act, c_dve)[t % 2], g * (T // 2) + t // 2 + 1)
                        for k in range(GROUP_BLOCKS):
                            ins = nc.tensor.transpose(pC[t % 4][:, k * P:(k + 1) * P],
                                                      cg[:, par, t, k, :], C["ident"][:])
                        ins.then_inc(c_done, 1)
                    pe.wait_ge(c_act, (g + 1) * (T // 2) + 2)
                    pe.wait_ge(c_dve, (g + 1) * (T // 2) + 2)
                    for k in range(GROUP_BLOCKS):
                        for t in range(T):
                            ins = nc.tensor.matmul(pY[:, k * P:(k + 1) * P], cT[:, t, k * P:(k + 1) * P], wo[:, t, :],
                                                   start=(t == 0), stop=(t == T - 1))
                    ins.then_inc(y_done, 1)
                    pe.wait_ge(y_in, g + 1)
                    pe.wait_ge(x_done, g + 2)
                    nc.tensor.matmul(pB[:], C["flip"][:], yr[:], start=True, stop=True).then_inc(b_done, 1)


def l1_attn_a(nc, D, x, C, tag, out=None):
    with ExitStack() as ctx:
        cx = nc.dram_tensor(f"{tag}_ctx", (BATCH * DIM, SEQ), F32, kind="Internal").ap()
        den = nc.dram_tensor(f"{tag}_den", (BATCH * 16, SEQ), F32, kind="Internal").ap()
        with ExitStack() as inner:
            v_all = inner.enter_context(nc.sbuf_tensor(f"{tag}_v", [P, SEQ // P, BATCH * DIM], F32))
            NPOS = 6
            dram = {n: nc.dram_tensor(f"{tag}_{n}", (BATCH + 1, NPOS, rows, SEQ), BF16, kind="Internal").ap()
                    for n, rows in (("qc", P), ("kc", P), ("qr", 64), ("kr", 4))}
            l1a_project(nc, D, x, C, f"{tag}p", v_all, dram)
            attention_columns(nc, D, C, f"{tag}a", dram, v_all, cx, den)
        l1a_output(nc, D, x, C, f"{tag}o", cx, den, out)


def l1a_project(nc, D, x, C, tag, v_all, dram):
    L = 100
    R = 68
    with ExitStack() as ctx:
        def sb(name, shape, dt=F32):
            return ctx.enter_context(nc.sbuf_tensor(f"{tag}_{name}", shape, dt))

        def pb(name, shape, dt=F32):
            return ctx.enter_context(nc.psum_tensor(f"{tag}_{name}", shape, dt))

        sem = semaphores(nc, ctx, tag)

        S = ln_scratch(sb)
        wl = sb("wl", [P, L])
        wuq, wuk, wuv = (sb(n, [64, P]) for n in ("wuq", "wuk", "wuv"))
        wr = sb("wr", [L, 2, R])
        cos, sin = sb("cos", [R, SEQ]), sb("sin", [R, SEQ])
        xn = sb("xn", [P, 2, GROUP_BLOCKS, DIM])
        xt = sb("xt", [P, GROUP])
        lat = sb("lat", [L, GROUP])
        t1, t2 = sb("t1", [R, GROUP]), sb("t2", [R, GROUP])
        f = {n: sb(f"f{n}", [rows, GROUP]) for n, rows in (("q", P), ("k", P), ("r", R))}
        part = {n: sb(f"part{n}", [rows, 2, 3, GROUP], BF16) for n, rows in (("q", P), ("k", P), ("r", R))}
        pT, pL, pQ, pK, pR, pS, pV = (pb(n, [P, GROUP]) for n in ("pT", "pL", "pQ", "pK", "pR", "pS", "pV"))
        src = {"q": pQ, "k": pK, "r": f["r"]}

        w_in, zeroed = sem("weights_in"), sem("zeroed")
        ln_step, ln_ve, ln_rough = sem("ln_step"), sem("ln_ve"), sem("ln_rough")
        xn_ready, xT_done, xt_ready = sem("xn_ready"), sem("xT_done"), sem("xt_ready")
        lat_done, lat_in, rope = sem("lat_done"), sem("lat_in"), sem("rope")
        done = {n: sem(f"{n}_done") for n in "qkrv"}
        hi, rest, mid, low = ({n: sem(f"{n}_{w}") for n in "qkr"} for w in ("hi", "rest", "mid", "low"))
        r_ready, v_ready, sent = sem("r_ready"), sem("v_ready"), [sem("sent0"), sem("sent1")]
        NW = 7

        block = ctx.enter_context(nc.Block())
        SENDS = 4 * len(RUNS)

        @block.sync
        def _(sp):
            for dst, name in ((wl, "L1_attn_a_latents"), (wuq, "L1_attn_a_W_UQ"), (wuk, "L1_attn_a_W_UK"),
                              (wuv, "L1_attn_a_W_UV"), (wr, "L1_attn_a_rotary"), (cos, "rope_cos"), (sin, "rope_sin")):
                sp.dma_start(dst[:], D[name]).then_inc(w_in, 16)
            for n, rows in (("qc", 8), ("kc", 8), ("qr", 4), ("kr", 4)):
                sp.dma_start(dram[n][BATCH, :, 0:rows, :], D["zeros"][0:6 * rows, :].rearrange("(s c) t -> s c t", c=rows)).then_inc(zeroed, 16)
            with sp.Fori(0, BATCH) as b:
                for par in (0, 1):
                    g = b * 2 + par
                    t = slice(par * GROUP, (par + 1) * GROUP)

                    sp.wait_ge(low["q"], g + 1)
                    send_parts(sp, dram["qc"], b, slice(0, P), part["q"], par, t, True, sent[par])
                    sp.wait_ge(low["k"], g + 1)
                    send_parts(sp, dram["kc"], b, slice(0, P), part["k"], par, t, False, sent[par])
                    sp.wait_ge(low["r"], g + 1)
                    send_parts(sp, dram["qr"], b, slice(0, 64), part["r"], par, t, True, sent[par])
                    send_parts(sp, dram["kr"], b, slice(64, R), part["r"], par, t, False, sent[par])
            for par in (0, 1):
                sp.wait_ge(sent[par], 16 * SENDS * (BATCH + 1))
            sp.wait_ge(zeroed, 64)

        @block.gpsimd
        def _(pool):
            def powers(turn):
                pool.wait_ge(ln_ve, turn + 1)
                nc.gpsimd.tensor_tensor(S["y"][:], S["ve"][:], C["mhalf"][:, 0:GROUP_BLOCKS], ALU.pow).then_inc(ln_rough, 1)

            powers(0)
            with pool.Fori(0, GROUPS) as g:
                powers(g + 1)

        @block.vector
        def _(dve):
            for par in (0, 1):
                dve.sem_inc(sent[par], 16 * SENDS)
            dve.wait_ge(w_in, 16 * NW)
            def layernorm(gn, par):
                steps = Steps(dve, ln_step, LN_STEPS, gn)
                dve.wait_ge(xT_done, gn + 1)
                ln_group_vector(nc, dve, lambda k: x[:, bass.ds((gn + 1) * GROUP_BLOCKS + k, 1), :], xn[:, par], S, steps,
                                ln_rough, gn + 1, ln_ve).then_inc(xn_ready, 1)
                steps.close()

            layernorm(0, 0)
            with dve.Fori(0, BATCH) as b:
                for par in (0, 1):
                    g = b * 2 + par
                    t = slice(par * GROUP, (par + 1) * GROUP)
                    layernorm(g + 1, 1 - par)
                    dve.wait_ge(done["r"], g + 1)
                    nc.vector.tensor_tensor(t1[:], pR[0:R, :], cos[:, t], ALU.mult)
                    nc.vector.tensor_tensor(t2[:], pS[0:R, :], sin[:, t], ALU.mult).then_inc(rope, 1)
                    dve.wait_ge(rope, g + 2)
                    nc.vector.tensor_tensor(f["r"][:], t1[:], t2[:], ALU.add).then_inc(r_ready, 1)
                    for n in "qk":
                        dve.wait_ge(hi[n], g + 1)
                        nc.vector.tensor_tensor(f[n][:], src[n][:], part[n][:, par, 0, :], ALU.subtract).then_inc(rest[n], 1)
                    dve.wait_ge(done["v"], g + 1)
                    nc.vector.tensor_copy(v_all[:, par * GROUP_BLOCKS:(par + 1) * GROUP_BLOCKS, bass.ds(b * DIM, DIM)],
                                          pV[:].rearrange("p (k d) -> p k d", d=DIM)).then_inc(v_ready, 1)
                    dve.wait_ge(hi["r"], g + 1)
                    nc.vector.tensor_tensor(f["r"][:], f["r"][:], part["r"][:, par, 0, :], ALU.subtract).then_inc(rest["r"], 1)
                    for n in "qkr":
                        dve.wait_ge(mid[n], g + 1)
                        nc.vector.tensor_tensor(part[n][:, par, 2, :], f[n][:], part[n][:, par, 1, :], ALU.subtract).then_inc(low[n], 1)

        @block.scalar
        def _(act):
            act.wait_ge(w_in, 16 * NW)
            def to_xt(gn):
                act.wait_ge(xT_done, gn + 3)
                nc.scalar.activation(xt[:], pT[:], ACT.Copy).then_inc(xt_ready, 1)

            to_xt(0)
            with act.Fori(0, BATCH) as b:
                for par in (0, 1):
                    g = b * 2 + par
                    act.wait_ge(lat_done, g + 1)
                    nc.scalar.activation(lat[:], pL[0:L, :], ACT.Copy).then_inc(lat_in, 1)
                    act.wait_ge(sent[par], (b + 1) * (16 * SENDS))
                    for n in "qk":
                        act.wait_ge(done[n], g + 1)
                        nc.scalar.activation(part[n][:, par, 0, :], src[n][:], ACT.Copy).then_inc(hi[n], 1)
                    act.wait_ge(r_ready, g + 1)
                    nc.scalar.activation(part["r"][:, par, 0, :], f["r"][:], ACT.Copy).then_inc(hi["r"], 1)
                    for n in "qkr":
                        act.wait_ge(rest[n], g + 2)
                        nc.scalar.activation(part[n][:, par, 1, :], f[n][:], ACT.Copy).then_inc(mid[n], 1)
                    to_xt(g + 1)

        @block.tensor
        def _(pe):
            def transposes(gn, par):
                pe.wait_ge(xn_ready, gn + 1)
                for k in range(GROUP_BLOCKS):
                    ins = nc.tensor.transpose(pT[:, k * P:(k + 1) * P], xn[:, par, k, :], C["ident"][:])
                ins.then_inc(xT_done, 1)

            pe.wait_ge(w_in, 16 * NW)
            pe.sem_inc(xT_done, 2)
            for s in (rope, v_ready, rest["q"], rest["k"], rest["r"]):
                pe.sem_inc(s, 1)
            transposes(0, 0)
            with pe.Fori(0, BATCH) as b:
                for par in (0, 1):
                    g = b * 2 + par
                    pe.wait_ge(xt_ready, g + 1)
                    nc.tensor.matmul(pL[0:L, :], wl[:], xt[:], start=True, stop=True).then_inc(lat_done, 1)
                    pe.wait_ge(rope, g + 1)
                    pe.wait_ge(lat_in, g + 1)
                    for i, p in enumerate((pR, pS)):
                        ins = nc.tensor.matmul(p[0:R, :], wr[:, i, :], lat[:], start=True, stop=True)
                    ins.then_inc(done["r"], 1)
                    pe.wait_ge(rest["q"], g + 1)
                    nc.tensor.matmul(pQ[:], wuq[:], lat[0:64, :], start=True, stop=True).then_inc(done["q"], 1)
                    pe.wait_ge(rest["k"], g + 1)
                    nc.tensor.matmul(pK[:], wuk[:], lat[0:64, :], start=True, stop=True).then_inc(done["k"], 1)
                    pe.wait_ge(v_ready, g + 1)
                    for k in range(GROUP_BLOCKS):
                        ins = nc.tensor.matmul(pV[:, k * P:(k + 1) * P], lat[0:64, k * P:(k + 1) * P], wuv[:], start=True, stop=True)
                    ins.then_inc(done["v"], 1)
                    transposes(g + 1, 1 - par)


def attention_columns(nc, D, C, tag, dram, v_all, cx, den):
    HEADS, HD, U, ROWS = 64, 8, SEQ // P, 72
    ROOT = 12 ** 0.5
    CLIP = 80.0
    with ExitStack() as ctx:
        def sb(name, shape, dt=F32):
            return ctx.enter_context(nc.sbuf_tensor(f"{tag}_{name}", shape, dt))

        def pb(name, shape, dt=F32):
            return ctx.enter_context(nc.psum_tensor(f"{tag}_{name}", shape, dt))

        sem = semaphores(nc, ctx, tag)

        qs, ks = sb("qs", [ROWS, 2, SEQ], BF16), sb("ks", [ROWS, 2, SEQ], BF16)
        ceiling = sb("ceiling", [P, P])
        vh = sb("vh", [P, 2, U, HD + 1])
        e = sb("e", [P, 4, SEQ])
        co = sb("co", [HD + 1, 2, SEQ])
        pS = [pb(f"pS{i}", [P, SEQ]) for i in range(2)]
        pO = [pb(f"pO{i}", [P, SEQ]) for i in range(2)]
        const_in, loaded, v_ready, ones_set = sem("const_in"), [sem("loaded0"), sem("loaded1")], sem("v_ready"), sem("ones_set")
        s_done, e_done, clipped, pv_done, o_out = (sem(n) for n in ("s_done", "e_done", "clipped", "pv_done", "o_out"))
        sent = [sem("sent0"), sem("sent1")]
        BLOCK = [b for i in range(U // 2) for b in (i, U - 1 - i)]
        width = [SEQ - b * P for b in BLOCK]
        NL = 4
        block = ctx.enter_context(nc.Block())

        def place(s):
            return s // U, s % U

        @block.sync
        def _(sp):
            sp.dma_start(ceiling[:], D["causal_ceiling"]).then_inc(const_in, 16)

            def load(bh, par):
                for dst, lo, name, rows, h in ((qs, 0, "qc", 8, bh % 16 * 8), (ks, 0, "kc", 8, bh % 16 * 8),
                                               (qs, 48, "qr", 4, bh % 16 * 4), (ks, 48, "kr", 4, 0)):
                    src = dram[name][bass.ds(bh // 16, 1), :, bass.ds(h, rows), :]
                    sp.dma_start(dst[lo:lo + 6 * rows, par, :], src.rearrange("o s c t -> (o s) c t")).then_inc(loaded[par], 16)

            def store(bh, par):
                sp.wait_ge(o_out, bh + 3)
                for dst, lo, hi in ((cx[bass.ds(bh * HD, HD), :], 0, HD), (den[bass.ds(bh, 1), :], HD, HD + 1)):
                    sp.dma_start(dst, co[lo:hi, par, :]).then_inc(sent[par], 16)

            load(0, 0)
            load(1, 1)
            with sp.Fori(1, HEADS // 2) as it:
                for par in (0, 1):
                    bh = it * 2 + par
                    sp.wait_ge(s_done, (bh - 1) * U)
                    load(bh, par)
                    store(bh - 2, par)
            sp.wait_ge(s_done, (HEADS - 1) * U)
            load(HEADS, 0)
            for par in (0, 1):
                store(HEADS - 2 + par, par)
                sp.wait_ge(sent[par], (HEADS // 2 + 1) * 32)

        @block.gpsimd
        def _(pool):
            def v_copy(bh, par):
                nc.gpsimd.tensor_copy(vh[:, par, :, 0:HD], v_all[:, :, bass.ds(bh * HD, HD)]).then_inc(v_ready, 1)

            nc.gpsimd.memset(vh[:], 1.0).then_inc(ones_set, 1)
            pool.wait_ge(ones_set, 1)
            v_copy(0, 0)
            v_copy(1, 1)
            with pool.Fori(1, HEADS // 2) as it:
                for par in (0, 1):
                    bh = it * 2 + par
                    pool.wait_ge(pv_done, (bh - 1) * U + 4)
                    v_copy(bh, par)

        @block.tensor
        def _(pe):
            pe.sem_inc(o_out, 2)
            for par in (0, 1):
                pe.sem_inc(sent[par], 32)
            pe.sem_inc(pv_done, 4)

            def scores(bh, par, u, slot, free=None):
                if u == 0:
                    pe.wait_ge(loaded[par], ((bh - par) // 2 + 1) * 16 * NL if isinstance(bh, int)
                               else (bh + (2 - par)) * (8 * NL))
                if free is not None:
                    pe.wait_ge(clipped, free)
                first = BLOCK[u] * P
                k = ks[:, par, first:first + P]
                for a in range(0, width[u], GROUP):
                    z = min(a + GROUP, width[u])
                    ins = nc.tensor.matmul(pS[slot][:, a:z], k, qs[:, par, first + a:first + z], start=True, stop=True)
                ins.then_inc(s_done, 1)

            def weigh(bh, par, u, n):
                if u == 0:
                    pe.wait_ge(v_ready, bh + 1)
                    pe.wait_ge(o_out, bh + 1)
                pe.wait_ge(e_done, n + 1)
                first = BLOCK[u] * P
                for bank in range(first // GROUP, SEQ // GROUP):
                    a, z = max(first, bank * GROUP), (bank + 1) * GROUP
                    ins = nc.tensor.matmul(pO[par][0:HD + 1, a:z], vh[:, par, BLOCK[u], :], e[:, u % 4, a - first:z - first],
                                           start=(u == 0), stop=(u == (6, 7)[bank]), skip_group_check=True)
                ins.then_inc(pv_done, 1)

            scores(0, 0, 0, 0)
            scores(0, 0, 1, 1)
            scores(0, 0, 2, 0, free=1)
            with pe.Fori(0, HEADS // 2) as it:
                for s in range(2 * U):
                    n = it * (2 * U) + s
                    h3, u3 = place(s + 3)
                    scores(it * 2 + h3, h3 % 2, u3, (s + 3) % 2, free=n + 2)
                    h0, u0 = place(s)
                    weigh(it * 2 + h0, h0, u0, n)

        @block.scalar
        def _(act):
            def exps(u, n):
                act.wait_ge(clipped, n + 1)
                w = width[u]
                nc.scalar.activation(e[:, u % 4, 0:w], e[:, u % 4, 0:w], ACT.Exp, scale=1 / ROOT).then_inc(e_done, 1)

            def out(bh, par, turn):
                act.wait_ge(pv_done, (bh + 1) * U + 4)
                act.wait_ge(sent[par], (turn + 1) * 32)
                nc.scalar.activation(co[:, par, :], pO[par][0:HD + 1, :], ACT.Copy).then_inc(o_out, 1)

            exps(0, 0)
            with act.Fori(0, HEADS // 2) as it:
                for s in range(2 * U):
                    exps((s + 1) % U, it * (2 * U) + s + 1)
                    if s == U + 1:
                        out(it * 2, 0, it)
                out(it * 2 + 1, 1, it)

        @block.vector
        def _(dve):
            def clip(u, n):
                dve.wait_ge(s_done, n + 1)
                dve.wait_ge(pv_done, n + 1)
                s, w = pS[u % 2], width[u]
                ins = nc.vector.scalar_tensor_tensor(e[:, u % 4, 0:P], s[:, 0:P], -CLIP, ceiling[:], ALU.max, ALU.min)
                if w > P:
                    ins = nc.vector.tensor_scalar(e[:, u % 4, P:w], s[:, P:w], -CLIP, CLIP, ALU.max, ALU.min)
                ins.then_inc(clipped, 1)

            dve.wait_ge(const_in, 16)
            clip(0, 0)
            with dve.Fori(0, HEADS // 2) as it:
                for s in range(2 * U):
                    clip((s + 1) % U, it * (2 * U) + s + 1)


def l1a_output(nc, D, x, C, tag, cx, den, out=None):
    with ExitStack() as ctx:
        def sb(name, shape, dt=F32):
            return ctx.enter_context(nc.sbuf_tensor(f"{tag}_{name}", shape, dt))

        def pb(name, shape, dt=F32):
            return ctx.enter_context(nc.psum_tensor(f"{tag}_{name}", shape, dt))

        sem = semaphores(nc, ctx, tag)

        wo, sel = sb("wo", [P, DIM]), sb("sel", [16, P])
        cg, dn = sb("cg", [P, 2, GROUP]), sb("dn", [16, 2, GROUP])
        dall = sb("dall", [P, GROUP])
        cT = sb("cT", [P, 2, GROUP])
        pC, pY = ([pb(f"{n}{i}", [P, GROUP]) for i in range(2)] for n in ("pC", "pY"))
        w_in, stored, x_done = sem("weights_in"), sem("stored"), sem("x_done")
        D_in, rd_done, cg_in = sem("D_in"), sem("rd_done"), [sem("cg_in0"), sem("cg_in1")]
        c_done, c_in, y_done = sem("c_done"), sem("c_in"), sem("y_done")
        block = ctx.enter_context(nc.Block())

        @block.sync
        def _(sp):
            sp.dma_start(wo[:], D["L1_attn_a_W_O"]).then_inc(w_in, 16)
            sp.dma_start(sel[:], D["spread"]).then_inc(w_in, 16)
            divided_columns(sp, cx, den, dall, cg, dn, D_in, cg_in, c_in, rd_done)
            if out is not None:
                store_x(sp, out, x, x_done, stored)

        @block.vector
        def _(dve):
            dve.wait_ge(D_in, 16)
            nc.vector.reciprocal(dall[:], dall[:]).then_inc(rd_done, 1)
            with dve.Fori(0, BATCH) as b:
                for par in (0, 1):
                    g = b * 2 + par
                    dve.wait_ge(cg_in[par], (b + 1) * 32)
                    dve.wait_ge(c_done, g + 1)
                    nc.vector.tensor_tensor(cT[:, par, :], cg[:, par, :], pC[par][:], ALU.mult).then_inc(c_in, 1)
                    xs = x[:, bass.ds((g + 1) * GROUP_BLOCKS, GROUP_BLOCKS), :]
                    dve.wait_ge(y_done, g + 1)
                    nc.vector.tensor_tensor(xs, xs, pY[par][:].rearrange("p (k d) -> p k d", d=DIM), ALU.add).then_inc(x_done, 1)

        @block.tensor
        def _(pe):
            pe.wait_ge(w_in, 32)
            pe.sem_inc(c_in, 2)
            pe.sem_inc(x_done, 2)
            with pe.Fori(0, BATCH) as b:
                for par in (0, 1):
                    g = b * 2 + par
                    pe.wait_ge(cg_in[par], (b + 1) * 32)
                    nc.tensor.matmul(pC[par][:], sel[:], dn[:, par, :], start=True, stop=True).then_inc(c_done, 1)
                    pe.wait_ge(c_in, g + 3)
                    pe.wait_ge(x_done, g + 1)
                    for k in range(GROUP_BLOCKS):
                        ins = nc.tensor.matmul(pY[par][:, k * P:(k + 1) * P], cT[:, par, k * P:(k + 1) * P], wo[:], start=True, stop=True)
                    ins.then_inc(y_done, 1)


def build(nc, D, out):
    with ExitStack() as ctx:
        x = ctx.enter_context(nc.sbuf_tensor("x", [P, (GROUPS + 2) * GROUP_BLOCKS, DIM], F32))
        ident = ctx.enter_context(nc.sbuf_tensor("ident", [P, P], F32))
        mhalf = ctx.enter_context(nc.sbuf_tensor("minus_half", [P, 32], F32))
        loaded = ctx.enter_context(nc.semaphore("x_loaded"))
        ident16 = ctx.enter_context(nc.sbuf_tensor("ident16", [P, P], BF16))
        flip = ctx.enter_context(nc.sbuf_tensor("flip", [P, P], F32))
        C = {name: ctx.enter_context(nc.sbuf_tensor(name, [P, tiles, P], F32))
             for name, tiles in (("l0_w1", 9), ("l0_w2", 9), ("l1_w1", 16), ("l1_w2", 16))}
        C["ffn_in"] = ctx.enter_context(nc.semaphore("ffn_in"))
        C.update(ident=ident, mhalf=mhalf, ident16=ident16, flip=flip)
        with nc.Block() as block:
            @block.sync
            def _(sp):
                sp.dma_start(ident[:], D["identity"]).then_inc(loaded, 16)
                sp.dma_start(ident16[:], D["identity16"]).then_inc(loaded, 16)
                sp.dma_start(flip[:], D["flip"]).then_inc(loaded, 16)
                sp.dma_start(x[:, GROUP_BLOCKS:GROUP_BLOCKS + BLOCKS, :],
                             D["x"].rearrange("(b p) d -> p b d", p=P)).then_inc(loaded, 16)
                sp.wait_ge(loaded, 66)

            @block.vector
            def _(dve):
                nc.vector.memset(x[:, 0:GROUP_BLOCKS, :], 0.0)
                nc.vector.memset(x[:, GROUP_BLOCKS + BLOCKS:, :], 0.0).then_inc(loaded, 1)
                nc.vector.memset(mhalf[:], -0.5).then_inc(loaded, 1)
        l0_attn_a(nc, D, x, C, "l0a")
        l0_ffn(nc, D, x, C, "f0")
        l0_attn_b(nc, D, x, C, "l0b")
        l0_ffn(nc, D, x, C, "f1")
        l1_attn_a(nc, D, x, C, "l1a")
        l1_ffn(nc, D, x, C, "f2")
        l1_attn_b(nc, D, x, C, "l1b")
        l1_ffn(nc, D, x, C, "f3", out)


def kernel(**inputs):
    import ml_dtypes
    import numpy as np
    import concourse.bacc as bacc
    from concourse.bass_utils import run_bass_kernel_spmd

    a = {k: np.asarray(v) for k, v in inputs.items()}
    bf16 = ml_dtypes.bfloat16
    distance = np.arange(SEQ - 1, -1, -1, dtype=np.float64)
    root = np.sign(distance) * np.sqrt(distance + 1e-6) / np.sqrt(SEQ)
    positions = (np.stack([distance / SEQ, root, np.ones(SEQ)]) / (2 * np.pi)).astype(np.float32)
    window = (-3.0 * np.exp(-distance ** 2 / (2.0 * (SEQ / 4.0) ** 2))).astype(np.float32)
    n = np.arange(SEQ - 1, -1, -1)
    bucket = np.where(n < 16, n, np.minimum(16 + (np.log(np.maximum(n, 1) / 16.0) / np.log(8.0) * 16).astype(np.int32), 31))
    pairs = np.arange(64) ^ 1
    wqr, wkr = a["L1_attn_a_W_QR"], a["L1_attn_a_W_KR"]
    angle = np.arange(SEQ, dtype=np.float32)[None, :] * (np.float32(10000) ** (-np.arange(0, 4, 2, dtype=np.float32) / 4))[:, None]
    cos = np.tile(np.repeat(np.cos(angle.astype(np.float64)), 2, 0), (17, 1)).astype(np.float32)
    sin = np.tile(np.repeat(np.sin(angle.astype(np.float64)), 2, 0) * np.array([[-1], [1], [-1], [1]]), (17, 1)).astype(np.float32)
    later = np.arange(P)[None, :] >= np.arange(P)[:, None]
    rotary, zero32 = np.zeros((100, 2, 68), np.float32), np.zeros((32, P), np.float32)
    rotary[0:32, 0, 0:64], rotary[0:32, 1, 0:64] = wqr, wqr[:, pairs]
    rotary[64:68, 0, 64:68] = rotary[96:100, 1, 64:68] = np.eye(4)
    zero16 = np.zeros((DIM, 16), np.float32)
    arrays = {
        "x": a["L0_attn_a_x"].reshape(TOKENS, DIM),
        "identity": np.eye(P, dtype=np.float32),
        "flip": np.eye(P, dtype=np.float32)[::-1],
        "zeros": np.zeros((64, SEQ), bf16), "ones": np.ones((3, SEQ), bf16), "minus_ones": -np.ones((3, SEQ), bf16),
        "positions": positions, "window": np.broadcast_to(window, (64, SEQ)),
        "msign": np.repeat(np.float32([-1, 1]), 16).reshape(32, 1),
        "spread": np.kron(np.eye(16), np.ones((1, 8))).astype(np.float32),
        "L0_attn_a_cq_w": a["L0_attn_a_cq_w"], "L0_attn_a_ck_w": a["L0_attn_a_ck_w"], "L0_attn_a_v_w": a["L0_attn_a_v_w"],
        "L0_attn_a_qmw32": np.concatenate([a["L0_attn_a_qmod_w"], zero16], 1),
        "L0_attn_a_kmw32": np.concatenate([zero16, a["L0_attn_a_kmod_w"]], 1),
        "L0_attn_a_mb32": np.concatenate([a["L0_attn_a_qmod_b"], a["L0_attn_a_kmod_b"]]).reshape(32, 1),
        "L0_attn_a_v_b": a["L0_attn_a_v_b"].reshape(1, DIM),
        "L0_attn_a_fp": np.concatenate([a["L0_attn_a_freqs"].reshape(2048, 2).T, a["L0_attn_a_phases"].reshape(1, 2048)]),
        "L0_attn_a_ampsT": a["L0_attn_a_amps"].reshape(16, P).T,
        "L0_attn_a_gmw": np.concatenate([a["L0_attn_a_gate_w"], a["L0_attn_a_mod_w"]], 1),
        "L0_attn_a_gmb": np.tile(np.concatenate([a["L0_attn_a_gate_b"].reshape(16, 16),
                                                 a["L0_attn_a_mod_b"].reshape(16, 8)], 1), (BATCH, 1)),
        "L0_attn_a_basis": np.tile(a["L0_attn_a_mod_basis"].transpose(1, 0, 2), (BATCH, 1, 1)),
        "L0_attn_a_out_w": a["L0_attn_a_out_w"], "L0_attn_a_out_b": a["L0_attn_a_out_b"].reshape(1, DIM),
        "L0_attn_a_ffn_w1": a["L0_attn_a_ffn_w1"], "L0_attn_a_ffn_b1": a["L0_attn_a_ffn_b1"].reshape(4, P).T,
        "L0_attn_a_ffn_w2": a["L0_attn_a_ffn_w2"], "L0_attn_a_ffn_b2": a["L0_attn_a_ffn_b2"].reshape(DIM, 1),
        **{f"L0_attn_a_{n}": a[f"L0_attn_a_{n}"].reshape(1, DIM) for n in ("ln1_g", "ln1_b", "ln2_g", "ln2_b")},
        "identity16": np.eye(P, dtype=bf16),
        "rank": np.arange(8, 0, -1, dtype=np.float32).reshape(1, 8),
        "sel24": np.ascontiguousarray(np.broadcast_to(np.tile(np.eye(8), (3, 1))[:, :, None], (24, 8, P))).astype(bf16),
        "L0_attn_b_W_f": a["L0_attn_b_W_f"],
        "L0_attn_b_WqkT": a["L0_attn_b_W_qkv"][:, :2048].T,
        "L0_attn_b_Wv": a["L0_attn_b_W_qkv"][:, 2048:],
        "L0_attn_b_W_out": a["L0_attn_b_W_out"],
        "L0_attn_b_b_out": a["L0_attn_b_b_out"].reshape(DIM, 1),
        "L0_attn_b_b_f2": np.concatenate([a["L0_attn_b_b_f"]] * 2).reshape(P, 1),
        "L0_attn_b_b_f": a["L0_attn_b_b_f"].reshape(1, 64),
        "L0_ffn_gate_wT": a["L0_ffn_gate_w"].T,
        "L0_ffn_lb_bias": a["L0_ffn_lb_bias"].reshape(1, 8),
        "L0_ffn_w1T": a["L0_ffn_w1"].transpose(0, 2, 1),
        "L0_ffn_w2T": a["L0_ffn_w2"].transpose(0, 2, 1),
        "L0_ffn_cfcT": a["L0_ffn_cfc"].T,
        "L0_ffn_cprojT": a["L0_ffn_cproj"].T,
        "L1_attn_a_W_O": a["L1_attn_a_W_O"],
        "L1_attn_a_latents": np.concatenate([a["L1_attn_a_W_DQ"], a["L1_attn_a_W_DKV"], wkr, np.zeros((P, 28), np.float32),
                                             wkr[:, pairs[:4]]], 1),
        "L1_attn_a_W_UQ": np.concatenate([a["L1_attn_a_W_UQ"], zero32]),
        **{f"L1_attn_a_{n}": np.concatenate([zero32, a[f"L1_attn_a_{n}"]]) for n in ("W_UK", "W_UV")},
        "L1_attn_a_rotary": rotary,
        "rope_cos": cos, "rope_sin": sin,
        "causal_ceiling": np.where(later, 80.0, -1e30).astype(np.float32),
        "L1_attn_b_Wq": a["L1_attn_b_Wq"], "L1_attn_b_Wout": a["L1_attn_b_Wout"],
        "L1_attn_b_Wkk": np.concatenate([a["L1_attn_b_Wkv"][:, :64]] * 2, 1), "L1_attn_b_Wv": a["L1_attn_b_Wkv"][:, 64:],
        "L1_attn_b_bout": a["L1_attn_b_bout"].reshape(1, DIM),
        "L1_attn_b_rel_by_distance": a["L1_attn_b_rel_emb"][bucket].T,
        "L1_ffn_gate_wT": a["L1_ffn_gate_w"].T,
        "L1_ffn_gate_b": a["L1_ffn_gate_b"].reshape(1, 8),
        "L1_ffn_rms_w": a["L1_ffn_rms_w"].reshape(1, 8),
        "L1_ffn_w1": a["L1_ffn_w1"],
        "L1_ffn_b1": a["L1_ffn_b1"].reshape(16, P),
        "L1_ffn_w2": a["L1_ffn_w2"].reshape(16, P, DIM),
        "L1_ffn_b2": a["L1_ffn_b2"],
    }
    nc = bacc.Bacc("TRN2", target_bir_lowering=False, num_devices=1)
    D, feeds = {}, {}
    for name, v in arrays.items():
        v = np.ascontiguousarray(v)
        feeds[f"in_{name}"] = v
        D[name] = nc.dram_tensor(f"in_{name}", v.shape, mybir.dt.from_np(v.dtype), kind="ExternalInput").ap()
    out = nc.dram_tensor("out", (TOKENS, DIM), F32, kind="ExternalOutput").ap()
    build(nc, D, out)
    r = run_bass_kernel_spmd(nc, [feeds], core_ids=[0])
    return r.results[0]["out"].reshape(BATCH, SEQ, DIM)
```
